# Optimizing a Trainium2 kernel written in Bass

```python
import numpy as np
import jax
import jax.numpy as jnp

def _softmax(x, axis=-1):
    return jax.nn.softmax(x, axis=axis)

def _gelu(x):
    return jax.nn.gelu(x, approximate=True)

def _silu(x):
    return jax.nn.silu(x)

def _sigmoid(x):
    return jax.nn.sigmoid(x)

def _layernorm(x, axis=-1, eps=1e-05):
    m = jnp.mean(x, axis=axis, keepdims=True)
    v = jnp.var(x, axis=axis, keepdims=True)
    return (x - m) / jnp.sqrt(v + eps)

def _scatter_add(tgt, idx, src, axis=0):
    return tgt.at[idx].add(src)

def _segment_sum(src, seg, n):
    return jax.ops.segment_sum(src, seg, n)
kernel_name = 'mk_decoder_postln_d2_seqx_r8_53abc7'

def setup_inputs(seed: int=0):
    np.random.seed(seed)
    _w = jnp.asarray

    def _rec_inputs():
        import jax
        import jax.numpy as jnp
        _rk = jax.random.key(seed)
        x = -0.000125 + 0.9999 * jax.random.normal(jax.random.fold_in(_rk, 1), (32, 64, 256), jnp.float32)
        _lenS = 64 - jax.random.randint(jax.random.fold_in(_rk, 7), (32,), 0, max(1, 64 // 4) + 1, jnp.int32)
        _lenS2 = 64 - jax.random.randint(jax.random.fold_in(_rk, 8), (32,), 0, max(1, 64 // 4) + 1, jnp.int32)
        _ctx_2048P = jax.random.normal(jax.random.fold_in(_rk, 11), (32, 16, 256), jnp.float32)
        _ctx_2048c = jax.random.dirichlet(jax.random.fold_in(_rk, 511), 0.3 * jnp.ones((16,), jnp.float32), (32, 64))
        _ctx_2048t = jnp.einsum('bsk,bkd->bsd', _ctx_2048c, _ctx_2048P)
        _ctx_2048t = _ctx_2048t * jax.lax.rsqrt(jnp.mean(jnp.square(_ctx_2048t)) + 1e-12) * 0.953939
        ctx_2048 = 1.72703e-05 + 1.00003 * (_ctx_2048t + 0.3 * jax.random.normal(jax.random.fold_in(_rk, 611), (32, 64, 256), jnp.float32))
        return (x, ctx_2048)
    x, ctx_2048 = _rec_inputs()

    def _L0_attn_setup():
        import jax, jax.numpy as jnp
        import numpy as np
        B, T, HID = (1, 256, 256)
        H = 16
        D = HID // H
        EPS = 1e-05

        def _layer_norm(x, eps=1e-05):
            mu = jnp.mean(x, axis=-1, keepdims=True)
            var = jnp.mean((x - mu) ** 2, axis=-1, keepdims=True)
            return (x - mu) * jax.lax.rsqrt(var + eps)

        def _feature_map(x, gamma, beta):
            return _layer_norm(x * gamma + beta)
        key = jax.random.key(seed)
        ks = jax.random.split(key, 8)
        s = HID ** (-0.5)
        return {'hidden_states': jax.random.normal(ks[0], (B, T, HID), jnp.float32), 'Wq': jax.random.normal(ks[1], (HID, HID), jnp.float32) * s, 'Wk': jax.random.normal(ks[2], (HID, HID), jnp.float32) * s, 'Wv': jax.random.normal(ks[3], (HID, HID), jnp.float32) * s, 'Wo': jax.random.normal(ks[4], (HID, HID), jnp.float32) * s, 'gamma': 1.0 + 0.1 * jax.random.normal(ks[5], (D,), jnp.float32), 'beta': 0.1 * jax.random.normal(ks[6], (D,), jnp.float32)}
    _L0_attn_all = _L0_attn_setup()
    _L0_attn_in = {k: v for k, v in _L0_attn_all.items() if k in ('Wq', 'Wk', 'Wv', 'Wo', 'gamma', 'beta')}
    del _L0_attn_all

    def _L0_xattn_setup():
        import jax, jax.numpy as jnp
        import numpy as np
        DIM = 256
        NH = 16
        HD = DIM // NH
        EPS = 1e-06
        IMG_LEN = 257

        def rms_norm(x, w, eps=EPS):
            xf = x.astype(jnp.float32)
            y = xf * jax.lax.rsqrt(jnp.mean(xf * xf, axis=-1, keepdims=True) + eps)
            return y.astype(x.dtype) * w

        def linear(x, w, b):
            return jnp.einsum('blc,oc->blo', x, w) + b

        def attention(q, k, v):
            scale = 1.0 / jnp.sqrt(jnp.asarray(HD, q.dtype))
            scores = jnp.einsum('bqhd,bkhd->bhqk', q, k) * scale
            probs = jax.nn.softmax(scores, axis=-1)
            return jnp.einsum('bhqk,bkhd->bqhd', probs, v)
        key = jax.random.key(seed)
        ks = jax.random.split(key, 12)
        B, L = (2, 1024)
        s = 0.02
        inp = {'x': jax.random.normal(ks[0], (B, L, DIM), jnp.float32), 'context': jax.random.normal(ks[1], (B, 769, DIM), jnp.float32), 'q_w': jax.random.normal(ks[2], (DIM, DIM), jnp.float32) * s, 'q_b': jnp.zeros((DIM,), jnp.float32), 'k_w': jax.random.normal(ks[3], (DIM, DIM), jnp.float32) * s, 'k_b': jnp.zeros((DIM,), jnp.float32), 'v_w': jax.random.normal(ks[4], (DIM, DIM), jnp.float32) * s, 'v_b': jnp.zeros((DIM,), jnp.float32), 'k_img_w': jax.random.normal(ks[5], (DIM, DIM), jnp.float32) * s, 'k_img_b': jnp.zeros((DIM,), jnp.float32), 'v_img_w': jax.random.normal(ks[6], (DIM, DIM), jnp.float32) * s, 'v_img_b': jnp.zeros((DIM,), jnp.float32), 'o_w': jax.random.normal(ks[7], (DIM, DIM), jnp.float32) * s, 'o_b': jnp.zeros((DIM,), jnp.float32), 'norm_q_w': jnp.ones((DIM,), jnp.float32), 'norm_k_w': jnp.ones((DIM,), jnp.float32), 'norm_k_img_w': jnp.ones((DIM,), jnp.float32)}
        return inp
    _L0_xattn_all = _L0_xattn_setup()
    _L0_xattn_in = {k: v for k, v in _L0_xattn_all.items() if k in ('q_w', 'q_b', 'k_w', 'k_b', 'v_w', 'v_b', 'k_img_w', 'k_img_b', 'v_img_w', 'v_img_b', 'o_w', 'o_b', 'norm_q_w', 'norm_k_w', 'norm_k_img_w')}
    del _L0_xattn_all

    def _L0_ffn_setup():
        import jax, jax.numpy as jnp
        import numpy as np
        DIM = 256
        INTER = 176
        E = 16
        TOPK = 4
        G = 4
        TOPK_G = 2
        N_SHARED = 2
        SHARED_INTER = N_SHARED * INTER
        ROUTE_SCALE = 1.0

        def _moe_forward(x, Wg, W1, W3, W2, Ws1, Ws3, Ws2):
            B, S, D = x.shape
            xt = x.reshape(-1, D)
            T = xt.shape[0]
            scores = jax.nn.softmax(xt @ Wg.T, axis=-1)
            sg = scores.reshape(T, G, E // G)
            group_scores = sg.max(axis=-1)
            gidx = jax.lax.top_k(group_scores, TOPK_G)[1]
            gmask = jax.nn.one_hot(gidx, G, dtype=jnp.float32).sum(axis=1) > 0
            masked = jnp.where(gmask[:, :, None], sg, -jnp.inf).reshape(T, E)
            topi = jax.lax.top_k(masked, TOPK)[1]
            weights = jnp.take_along_axis(scores, topi, axis=1) * ROUTE_SCALE
            combine = jnp.zeros((T, E), xt.dtype).at[jnp.arange(T)[:, None], topi].add(weights)
            h = jax.nn.silu(jnp.einsum('td,eid->eti', xt, W1)) * jnp.einsum('td,eid->eti', xt, W3)
            expert_out = jnp.einsum('eti,edi->etd', h, W2)
            y = jnp.einsum('etd,te->td', expert_out, combine)
            z = jax.nn.silu(xt @ Ws1.T) * (xt @ Ws3.T) @ Ws2.T
            return (y + z).reshape(B, S, D)
        key = jax.random.key(seed)
        ks = jax.random.split(key, 8)
        s = 0.02
        x = jax.random.normal(ks[0], (1, 256, DIM), dtype=jnp.float32)
        Wg = jax.random.normal(ks[1], (E, DIM), dtype=jnp.float32) * s
        W1 = jax.random.normal(ks[2], (E, INTER, DIM), dtype=jnp.float32) * s
        W3 = jax.random.normal(ks[3], (E, INTER, DIM), dtype=jnp.float32) * s
        W2 = jax.random.normal(ks[4], (E, DIM, INTER), dtype=jnp.float32) * s
        Ws1 = jax.random.normal(ks[5], (SHARED_INTER, DIM), dtype=jnp.float32) * s
        Ws3 = jax.random.normal(ks[6], (SHARED_INTER, DIM), dtype=jnp.float32) * s
        Ws2 = jax.random.normal(ks[7], (DIM, SHARED_INTER), dtype=jnp.float32) * s
        return {'x': x, 'Wg': Wg, 'W1': W1, 'W3': W3, 'W2': W2, 'Ws1': Ws1, 'Ws3': Ws3, 'Ws2': Ws2}
    _L0_ffn_all = _L0_ffn_setup()
    _L0_ffn_in = {k: v for k, v in _L0_ffn_all.items() if k in ('Wg', 'W1', 'W3', 'W2', 'Ws1', 'Ws3', 'Ws2')}
    del _L0_ffn_all

    def _L1_attn_setup():
        import jax, jax.numpy as jnp
        import numpy as np
        B, T, E = (4, 256, 256)
        H, KV = (16, 4)
        G = H // KV
        D = E // H
        key = jax.random.key(seed)
        kx, kq, kk, kv, ko = jax.random.split(key, 5)
        s = 1.0 / np.sqrt(E).astype(np.float32)
        x = jax.random.normal(kx, (B, T, E), jnp.float32)
        Wq = jax.random.normal(kq, (E, H * D), jnp.float32) * s
        Wk = jax.random.normal(kk, (E, KV * D), jnp.float32) * s
        Wv = jax.random.normal(kv, (E, KV * D), jnp.float32) * s
        Wo = jax.random.normal(ko, (H * D, E), jnp.float32) * s
        return {'x': x, 'Wq': Wq, 'Wk': Wk, 'Wv': Wv, 'Wo': Wo}
    _L1_attn_all = _L1_attn_setup()
    _L1_attn_in = {k: v for k, v in _L1_attn_all.items() if k in ('Wq', 'Wk', 'Wv', 'Wo')}
    del _L1_attn_all

    def _L1_xattn_setup():
        import jax, jax.numpy as jnp
        import numpy as np
        DIM = 256
        NHEADS = 32
        HEAD_DIM = DIM // NHEADS
        EPS = 1e-06

        def _rmsnorm(t):
            return t * jax.lax.rsqrt(jnp.mean(t * t, axis=-1, keepdims=True) + EPS)
        key = jax.random.key(seed)
        kx, kc, kq, kk, kv = jax.random.split(key, 5)
        x = jax.random.normal(kx, (2, 512, DIM), dtype=jnp.float32)
        context = jax.random.normal(kc, (2, 64, DIM), dtype=jnp.float32)
        std = 0.02
        Wq = jax.random.normal(kq, (DIM, DIM), dtype=jnp.float32) * std
        Wk = jax.random.normal(kk, (DIM, DIM), dtype=jnp.float32) * std
        Wv = jax.random.normal(kv, (DIM, DIM), dtype=jnp.float32) * std
        return {'x': x, 'context': context, 'Wq': Wq, 'Wk': Wk, 'Wv': Wv}
    _L1_xattn_all = _L1_xattn_setup()
    _L1_xattn_in = {k: v for k, v in _L1_xattn_all.items() if k in ('Wq', 'Wk', 'Wv')}
    del _L1_xattn_all

    def _L1_ffn_setup():
        import jax, jax.numpy as jnp
        import numpy as np
        TOP_K = 2

        def _gelu(v):
            return jax.nn.gelu(v, approximate=False)
        key = jax.random.key(seed)
        ks = jax.random.split(key, 7)
        B, T, D, I, E = (2, 256, 256, 1024, 8)
        s = 0.02
        return {'x': jax.random.normal(ks[0], (B, T, D), jnp.float32), 'rw1': jax.random.normal(ks[1], (D, D // 2), jnp.float32) * s, 'rw2': jax.random.normal(ks[2], (D // 2, E), jnp.float32) * s, 'w1': jax.random.normal(ks[3], (E, D, I), jnp.float32) * s, 'b1': jax.random.normal(ks[4], (E, I), jnp.float32) * s, 'w2': jax.random.normal(ks[5], (E, I, D), jnp.float32) * s, 'b2': jax.random.normal(ks[6], (E, D), jnp.float32) * s}
    _L1_ffn_all = _L1_ffn_setup()
    _L1_ffn_in = {k: v for k, v in _L1_ffn_all.items() if k in ('rw1', 'rw2', 'w1', 'b1', 'w2', 'b2')}
    del _L1_ffn_all
    return {'x': x, 'ctx_2048': ctx_2048, 'L0_attn_Wq': _L0_attn_in['Wq'], 'L0_attn_Wk': _L0_attn_in['Wk'], 'L0_attn_Wv': _L0_attn_in['Wv'], 'L0_attn_Wo': _L0_attn_in['Wo'], 'L0_attn_gamma': _L0_attn_in['gamma'], 'L0_attn_beta': _L0_attn_in['beta'], 'L0_xattn_q_w': _L0_xattn_in['q_w'], 'L0_xattn_q_b': _L0_xattn_in['q_b'], 'L0_xattn_k_w': _L0_xattn_in['k_w'], 'L0_xattn_k_b': _L0_xattn_in['k_b'], 'L0_xattn_v_w': _L0_xattn_in['v_w'], 'L0_xattn_v_b': _L0_xattn_in['v_b'], 'L0_xattn_k_img_w': _L0_xattn_in['k_img_w'], 'L0_xattn_k_img_b': _L0_xattn_in['k_img_b'], 'L0_xattn_v_img_w': _L0_xattn_in['v_img_w'], 'L0_xattn_v_img_b': _L0_xattn_in['v_img_b'], 'L0_xattn_o_w': _L0_xattn_in['o_w'], 'L0_xattn_o_b': _L0_xattn_in['o_b'], 'L0_xattn_norm_q_w': _L0_xattn_in['norm_q_w'], 'L0_xattn_norm_k_w': _L0_xattn_in['norm_k_w'], 'L0_xattn_norm_k_img_w': _L0_xattn_in['norm_k_img_w'], 'L0_ffn_Wg': _L0_ffn_in['Wg'], 'L0_ffn_W1': _L0_ffn_in['W1'], 'L0_ffn_W3': _L0_ffn_in['W3'], 'L0_ffn_W2': _L0_ffn_in['W2'], 'L0_ffn_Ws1': _L0_ffn_in['Ws1'], 'L0_ffn_Ws3': _L0_ffn_in['Ws3'], 'L0_ffn_Ws2': _L0_ffn_in['Ws2'], 'L1_attn_Wq': _L1_attn_in['Wq'], 'L1_attn_Wk': _L1_attn_in['Wk'], 'L1_attn_Wv': _L1_attn_in['Wv'], 'L1_attn_Wo': _L1_attn_in['Wo'], 'L1_xattn_Wq': _L1_xattn_in['Wq'], 'L1_xattn_Wk': _L1_xattn_in['Wk'], 'L1_xattn_Wv': _L1_xattn_in['Wv'], 'L1_ffn_rw1': _L1_ffn_in['rw1'], 'L1_ffn_rw2': _L1_ffn_in['rw2'], 'L1_ffn_w1': _L1_ffn_in['w1'], 'L1_ffn_b1': _L1_ffn_in['b1'], 'L1_ffn_w2': _L1_ffn_in['w2'], 'L1_ffn_b2': _L1_ffn_in['b2']}

def reference(x, ctx_2048, L0_attn_Wq, L0_attn_Wk, L0_attn_Wv, L0_attn_Wo, L0_attn_gamma, L0_attn_beta, L0_xattn_q_w, L0_xattn_q_b, L0_xattn_k_w, L0_xattn_k_b, L0_xattn_v_w, L0_xattn_v_b, L0_xattn_k_img_w, L0_xattn_k_img_b, L0_xattn_v_img_w, L0_xattn_v_img_b, L0_xattn_o_w, L0_xattn_o_b, L0_xattn_norm_q_w, L0_xattn_norm_k_w, L0_xattn_norm_k_img_w, L0_ffn_Wg, L0_ffn_W1, L0_ffn_W3, L0_ffn_W2, L0_ffn_Ws1, L0_ffn_Ws3, L0_ffn_Ws2, L1_attn_Wq, L1_attn_Wk, L1_attn_Wv, L1_attn_Wo, L1_xattn_Wq, L1_xattn_Wk, L1_xattn_Wv, L1_ffn_rw1, L1_ffn_rw2, L1_ffn_w1, L1_ffn_b1, L1_ffn_w2, L1_ffn_b2):
    import jax
    import jax.numpy as jnp

    def _L0_attn_ref(hidden_states, Wq, Wk, Wv, Wo, gamma, beta):
        import jax, jax.numpy as jnp
        import numpy as np
        B, T, HID = (1, 256, 256)
        H = 16
        D = HID // H
        EPS = 1e-05

        def _layer_norm(x, eps=1e-05):
            mu = jnp.mean(x, axis=-1, keepdims=True)
            var = jnp.mean((x - mu) ** 2, axis=-1, keepdims=True)
            return (x - mu) * jax.lax.rsqrt(var + eps)

        def _feature_map(x, gamma, beta):
            return _layer_norm(x * gamma + beta)
        b, t, _ = hidden_states.shape
        q = (hidden_states @ Wq.T).reshape(b, t, H, D)
        k = (hidden_states @ Wk.T).reshape(b, t, H, D)
        v = (hidden_states @ Wv.T).reshape(b, t, H, D)
        q = _feature_map(q, gamma, beta)
        k = _feature_map(k, gamma, beta)
        q = q * D ** (-0.5)
        attn = jnp.einsum('bqhd,bkhd->bhqk', q, k) ** 2
        mask = jnp.tril(jnp.ones((t, t), dtype=bool))
        attn = jnp.where(mask, attn, 0.0)
        o = jnp.einsum('bhqk,bkhd->bqhd', attn, v)
        z = jnp.sum(attn, axis=-1)
        o = o / (jnp.swapaxes(z, 1, 2)[..., None] + EPS)
        o = o.reshape(b, t, H * D)
        return o @ Wo.T

    def _L0_xattn_ref(x, context, q_w, q_b, k_w, k_b, v_w, v_b, k_img_w, k_img_b, v_img_w, v_img_b, o_w, o_b, norm_q_w, norm_k_w, norm_k_img_w):
        import jax, jax.numpy as jnp
        import numpy as np
        DIM = 256
        NH = 16
        HD = DIM // NH
        EPS = 1e-06
        IMG_LEN = 257

        def rms_norm(x, w, eps=EPS):
            xf = x.astype(jnp.float32)
            y = xf * jax.lax.rsqrt(jnp.mean(xf * xf, axis=-1, keepdims=True) + eps)
            return y.astype(x.dtype) * w

        def linear(x, w, b):
            return jnp.einsum('blc,oc->blo', x, w) + b

        def attention(q, k, v):
            scale = 1.0 / jnp.sqrt(jnp.asarray(HD, q.dtype))
            scores = jnp.einsum('bqhd,bkhd->bhqk', q, k) * scale
            probs = jax.nn.softmax(scores, axis=-1)
            return jnp.einsum('bhqk,bkhd->bqhd', probs, v)
        B, L, _ = x.shape
        ctx_img = context[:, :IMG_LEN]
        ctx_txt = context[:, IMG_LEN:]
        q = rms_norm(linear(x, q_w, q_b), norm_q_w).reshape(B, L, NH, HD)
        k = rms_norm(linear(ctx_txt, k_w, k_b), norm_k_w).reshape(B, -1, NH, HD)
        v = linear(ctx_txt, v_w, v_b).reshape(B, -1, NH, HD)
        k_img = rms_norm(linear(ctx_img, k_img_w, k_img_b), norm_k_img_w).reshape(B, -1, NH, HD)
        v_img = linear(ctx_img, v_img_w, v_img_b).reshape(B, -1, NH, HD)
        img_x = attention(q, k_img, v_img)
        txt_x = attention(q, k, v)
        out = (txt_x + img_x).reshape(B, L, DIM)
        return linear(out, o_w, o_b)

    def _L0_ffn_ref(x, Wg, W1, W3, W2, Ws1, Ws3, Ws2):
        import jax, jax.numpy as jnp
        import numpy as np
        DIM = 256
        INTER = 176
        E = 16
        TOPK = 4
        G = 4
        TOPK_G = 2
        N_SHARED = 2
        SHARED_INTER = N_SHARED * INTER
        ROUTE_SCALE = 1.0

        def _moe_forward(x, Wg, W1, W3, W2, Ws1, Ws3, Ws2):
            B, S, D = x.shape
            xt = x.reshape(-1, D)
            T = xt.shape[0]
            scores = jax.nn.softmax(xt @ Wg.T, axis=-1)
            sg = scores.reshape(T, G, E // G)
            group_scores = sg.max(axis=-1)
            gidx = jax.lax.top_k(group_scores, TOPK_G)[1]
            gmask = jax.nn.one_hot(gidx, G, dtype=jnp.float32).sum(axis=1) > 0
            masked = jnp.where(gmask[:, :, None], sg, -jnp.inf).reshape(T, E)
            topi = jax.lax.top_k(masked, TOPK)[1]
            weights = jnp.take_along_axis(scores, topi, axis=1) * ROUTE_SCALE
            combine = jnp.zeros((T, E), xt.dtype).at[jnp.arange(T)[:, None], topi].add(weights)
            h = jax.nn.silu(jnp.einsum('td,eid->eti', xt, W1)) * jnp.einsum('td,eid->eti', xt, W3)
            expert_out = jnp.einsum('eti,edi->etd', h, W2)
            y = jnp.einsum('etd,te->td', expert_out, combine)
            z = jax.nn.silu(xt @ Ws1.T) * (xt @ Ws3.T) @ Ws2.T
            return (y + z).reshape(B, S, D)
        return _moe_forward(x, Wg, W1, W3, W2, Ws1, Ws3, Ws2)

    def _L1_attn_ref(x, Wq, Wk, Wv, Wo):
        import jax, jax.numpy as jnp
        import numpy as np
        B, T, E = (4, 256, 256)
        H, KV = (16, 4)
        G = H // KV
        D = E // H
        b, t, _ = x.shape
        scale = 1.0 / np.sqrt(D).astype(np.float32)
        q = (x @ Wq).reshape(b, t, KV, G, D)
        k = (x @ Wk).reshape(b, t, KV, D)
        v = (x @ Wv).reshape(b, t, KV, D)
        scores = jnp.einsum('bqhgd,bkhd->bhgqk', q, k) * scale
        causal_mask = jnp.tril(jnp.ones((t, t), dtype=bool))
        scores = jnp.where(causal_mask, scores, -jnp.inf)
        w = jax.nn.softmax(scores, axis=-1)
        y = jnp.einsum('bhgqk,bkhd->bqhgd', w, v)
        y = y.reshape(b, t, H * D)
        return y @ Wo

    def _L1_xattn_ref(x, context, Wq, Wk, Wv):
        import jax, jax.numpy as jnp
        import numpy as np
        DIM = 256
        NHEADS = 32
        HEAD_DIM = DIM // NHEADS
        EPS = 1e-06

        def _rmsnorm(t):
            return t * jax.lax.rsqrt(jnp.mean(t * t, axis=-1, keepdims=True) + EPS)
        b, n, _ = x.shape
        m = context.shape[1]
        q = x @ Wq.T
        k_raw = context @ Wk.T
        v_raw = context @ Wv.T
        q = q.reshape(b, n, NHEADS, HEAD_DIM).transpose(0, 2, 1, 3)
        kv = jnp.concatenate([k_raw, v_raw], axis=-1)
        kv = kv.reshape(b, m, NHEADS, HEAD_DIM, 2)
        k = kv[..., 0].transpose(0, 2, 1, 3)
        v = kv[..., 1].transpose(0, 2, 1, 3)
        q = _rmsnorm(q)
        k = _rmsnorm(k)
        scale = HEAD_DIM ** (-0.5)
        scores = jnp.einsum('bhnd,bhmd->bhnm', q, k) * scale
        attn = jax.nn.softmax(scores, axis=-1)
        out = jnp.einsum('bhnm,bhmd->bhnd', attn, v)
        return out.transpose(0, 2, 1, 3).reshape(b, n, NHEADS * HEAD_DIM)

    def _L1_ffn_ref(x, rw1, rw2, w1, b1, w2, b2):
        import jax, jax.numpy as jnp
        import numpy as np
        TOP_K = 2

        def _gelu(v):
            return jax.nn.gelu(v, approximate=False)
        logits = _gelu(x @ rw1) @ rw2
        probs = jax.nn.softmax(logits, axis=-1)
        wgt, idx = jax.lax.top_k(probs, TOP_K)
        E = w1.shape[0]
        out = jnp.zeros_like(x)
        for e in range(E):
            Ye = _gelu(x @ w1[e] + b1[e]) @ w2[e] + b2[e]
            Ce = _gelu(b1[e]) @ w2[e] + b2[e]
            for k in range(TOP_K):
                mask = idx[..., k] == e
                active = jnp.any(mask).astype(x.dtype)
                term = jnp.where(mask[..., None], Ye, Ce)
                out = out + active * wgt[..., k:k + 1] * term
        return out
    x = _layernorm(x + _L0_attn_ref(x, L0_attn_Wq, L0_attn_Wk, L0_attn_Wv, L0_attn_Wo, L0_attn_gamma, L0_attn_beta), axis=-1)
    x = _layernorm(x + _L0_xattn_ref(x, ctx_2048, L0_xattn_q_w, L0_xattn_q_b, L0_xattn_k_w, L0_xattn_k_b, L0_xattn_v_w, L0_xattn_v_b, L0_xattn_k_img_w, L0_xattn_k_img_b, L0_xattn_v_img_w, L0_xattn_v_img_b, L0_xattn_o_w, L0_xattn_o_b, L0_xattn_norm_q_w, L0_xattn_norm_k_w, L0_xattn_norm_k_img_w), axis=-1)
    x = _layernorm(x + _L0_ffn_ref(x, L0_ffn_Wg, L0_ffn_W1, L0_ffn_W3, L0_ffn_W2, L0_ffn_Ws1, L0_ffn_Ws3, L0_ffn_Ws2), axis=-1)
    x = _layernorm(x + _L1_attn_ref(x, L1_attn_Wq, L1_attn_Wk, L1_attn_Wv, L1_attn_Wo), axis=-1)
    x = _layernorm(x + _L1_xattn_ref(x, ctx_2048, L1_xattn_Wq, L1_xattn_Wk, L1_xattn_Wv), axis=-1)
    x = _layernorm(x + _L1_ffn_ref(x, L1_ffn_rw1, L1_ffn_rw2, L1_ffn_w1, L1_ffn_b1, L1_ffn_w2, L1_ffn_b2), axis=-1)
    return x

_drawn_inputs = setup_inputs


def setup_inputs(seed=0):
    import zlib

    import numpy as np

    out = dict(_drawn_inputs(seed))
    spreads = {'L0_xattn_q_b': (0.0, 0.8),
     'L0_xattn_k_b': (0.0, 0.1),
     'L0_xattn_v_b': (0.0, 0.1),
     'L0_xattn_k_img_b': (0.0, 0.8),
     'L0_xattn_v_img_b': (0.0, 0.1),
     'L0_xattn_o_b': (0.0, 0.1),
     'L0_xattn_norm_q_w': (1.0, 0.6),
     'L0_xattn_norm_k_w': (1.0, 0.2),
     'L0_xattn_norm_k_img_w': (1.0, 0.6)}
    factors = {'L0_xattn_q_w': 2.809,
     'L0_ffn_Wg': 8.0,
     'L0_ffn_W1': 8.0,
     'L0_ffn_W3': 8.0,
     'L0_ffn_W2': 8.0,
     'L0_ffn_Ws1': 2.825,
     'L0_ffn_Ws3': 2.786,
     'L0_ffn_Ws2': 2.787,
     'L1_ffn_rw1': 3.255,
     'L1_ffn_rw2': 3.224,
     'L1_ffn_w1': 2.85,
     'L1_ffn_b1': 8.0,
     'L1_ffn_w2': 2.679,
     'L1_ffn_b2': 3.844}
    for name, (base, spread) in spreads.items():
        noise = np.random.default_rng([zlib.crc32(name.encode()), seed]).standard_normal(out[name].shape)
        drawn = base * np.exp(spread * noise) if base else spread * noise
        out[name] = jnp.asarray(drawn.astype(out[name].dtype))
    for name, factor in factors.items():
        out[name] = (out[name] * factor).astype(out[name].dtype)
    return out
```

```python
import concourse.bass as bass
from concourse import mybir
from contextlib import ExitStack
import numpy as np

F32 = mybir.dt.float32
U32 = mybir.dt.uint32
ACT = mybir.ActivationFunctionType
ALU = mybir.AluOpType
AX = mybir.AxisListType.X

BATCH, SEQ, DIM = 32, 64, 256
TOKENS = BATCH * SEQ
P = 128
TILES = TOKENS // P
TG = 4
GROUPS = TILES // TG
GTOK = TG * P
KC = DIM // P
PER = P // SEQ
GSEQ = TG * PER
E0, I0, SHARED = 16, 176, 2
EALL = E0 + SHARED
NGRP, TOPG, TOP0 = 4, 2, 4
E1, I1, TOP1 = 8, 1024, 2
H16, D16 = 16, 16
H32, D32 = 32, 8
EPS_LN, EPS_RMS = 1e-5, 1e-6
NEG = -1.0e30


class Event:

    def __init__(self, es, nc, name, per, primed=False, step=1, continues=None):
        self.per, self.step, self.primed = per, step, primed
        if continues is None:
            self.sem, self.base = es.enter_context(nc.semaphore(name)), 0
        else:
            assert not primed and not continues.primed and not continues.base
            self.sem, self.base = continues.sem, GROUPS * continues.per * continues.step

    def prime(self, engine):
        engine.sem_inc(self.sem, self.per * self.step)

    def at(self, g, k):
        return g * (self.per * self.step) + (k + 1 + (self.per if self.primed else 0)) * self.step + self.base


class Chain:

    def __init__(self, es, nc, name, per):
        self.sem, self.per, self.k = es.enter_context(nc.semaphore(name)), per, 0

    def link(self, engine, g, instruction):
        self.k += 1
        instruction.then_inc(self.sem, 1)
        engine.wait_ge(self.sem, g * self.per + self.k)

    def close(self):
        assert self.k == self.per, (self.k, self.per)


class Ring:

    def __init__(self, banks, full, emptied, uses):
        self.banks, self.full, self.emptied, self.uses = banks, full, emptied, uses
        self.at = {name: i for i, (name, _) in enumerate(uses)}
        self.next = 0
        assert len(uses) % 2 == 0 and len(self.at) == len(uses) == full.per

    def bank(self, name):
        return self.banks[self.at[name] % 2]

    def rank(self, i):
        return sum(e == self.uses[i][1] for _, e in self.uses[:i])

    def before_fill(self, pe, g, name):
        i = self.at[name]
        assert i == self.next, (name, i, self.next)
        self.next += 1
        e = self.emptied[self.uses[i - 2][1]]
        if i >= 2:
            pe.wait_ge(e.sem, e.at(g, self.rank(i - 2)))
        else:
            pe.wait_ge(e.sem, e.at(g, self.rank(len(self.uses) + i - 2) - e.per))

    def wait_filled_before(self, engine, g, name):
        engine.wait_ge(self.full.sem, self.full.at(g, self.at[name] - self.full.per))

    def wait_emptied_before(self, engine, g, name):
        i = self.at[name]
        e = self.emptied[self.uses[i][1]]
        engine.wait_ge(e.sem, e.at(g, self.rank(i) - e.per))

    def wait_full(self, engine, g, name):
        engine.wait_ge(self.full.sem, self.full.at(g, self.at[name]))

    def wait_emptied(self, engine, g, name):
        i = self.at[name]
        e = self.emptied[self.uses[i][1]]
        engine.wait_ge(e.sem, e.at(g, self.rank(i)))


def settle(engine, passed):
    engine.sem_inc(passed, 1)


def heads(ap, h):
    return ap.rearrange("p (h d) -> p h d", h=h)


def per_tile(name, engine):
    return [((name, t), engine) for t in range(TG)]


def staggered(*stages):
    last = max(lag for _, lag in stages)
    return [(name, step - lag) for step in range(TG + last) for name, lag in stages if 0 <= step - lag < TG]


class Core:

    def __init__(self, es, nc, x, h, d, keys_first, continues=None):
        self.x, self.h, self.d, self.keys_first = x, h, d, keys_first
        self.nb = h // 8
        self.lag = 1 if keys_first else 2
        self.w = PER * (d + 1)

        self.events = {}

        def ev(name, per):
            self.events[name] = Event(es, nc, x + name, per, continues=continues and continues.events[name])
            return self.events[name]

        self.masked = ev("masked", 1)
        self.s_full = ev("s_full", TG * self.nb)
        self.s_used = ev("s_used", TG * self.nb)
        self.p_ready = ev("p_ready", TG * self.nb)
        self.pt_full = ev("pt_full", TG * 2)
        self.pt_used = ev("pt_used", TG * 2)
        self.o_full = ev("o_full", TG)
        self.o_done = ev("o_done", TG)

    def uses(self):
        return [((self.x + n, t), {"otr": "A", "out": "D"}[n]) for n, t in self.tail()]

    def tail(self):
        return [(n, s - self.lag - k) for s in range(TG + self.lag + 2) for n, k in (("otr", 1), ("out", 2))
                if 0 <= s - self.lag - k < TG]


def core_pe(nc, pe, g, c, ring, still, masked, S, OB, weights, turned, values, O, OT, ident, out_product):
    hc = c.h // KC
    for step in range(TG + c.lag + 2):
        if step < TG:
            t = step
            if t == 0:
                pe.wait_ge(c.masked.sem, c.masked.at(g, 0))
            for b in range(c.nb):
                u = t * c.nb + b
                if u >= 4 and c.keys_first:
                    pe.wait_ge(c.s_used.sem, c.s_used.at(g, u - 4))
                if not c.keys_first and t >= 2 and b == 0:
                    pe.wait_ge(c.pt_used.sem, c.pt_used.at(g, 2 * (t - 2) + 1))
                m, lo = divmod(8 * b, hc)
                for s in range(PER):
                    last = nc.tensor.matmul(S[u % 4][s * SEQ:(s + 1) * SEQ, :],
                                            still[:, m, t * P + s * SEQ:t * P + (s + 1) * SEQ],
                                            masked[:, m, t * PER + s, lo:lo + 8, :], start=True, stop=True)
                last.then_inc(c.s_full.sem, 1)
        if not c.keys_first and 0 <= step - 1 < TG:
            t = step - 1
            for b in range(2):
                pe.wait_ge(c.p_ready.sem, c.p_ready.at(g, 2 * t + b))
                for j in range(4):
                    last = nc.tensor.transpose(S[(2 * t + b) % 4][:, j * P:(j + 1) * P],
                                               weights[:, t % 2, 8 * b + 2 * j:8 * b + 2 * j + 2, :], ident[:])
                last.then_inc(c.pt_full.sem, 1)
        if 0 <= step - c.lag < TG:
            t = step - c.lag
            o = OB[t % 2]
            if t >= 2:
                pe.wait_ge(c.o_done.sem, c.o_done.at(g, t - 2))
            if c.keys_first:
                pe.wait_ge(c.p_ready.sem, c.p_ready.at(g, c.nb * t + c.nb - 1))
                ring.wait_emptied(pe, g, (c.x + "v", t))
                for h in range(c.h):
                    j, a = divmod(h, 2)
                    last = nc.tensor.matmul(o[a * SEQ:(a + 1) * SEQ, j * c.w:(j + 1) * c.w],
                                            weights[:, t % 2, h, :], values[:, t, h, :], start=True, stop=True)
            else:
                pe.wait_ge(c.pt_used.sem, c.pt_used.at(g, 2 * t + 1))
                ring.wait_emptied(pe, g, (c.x + "v", t))
                for j in range(c.h // 2):
                    for s in range(PER):
                        last = nc.tensor.matmul(o[s * SEQ:(s + 1) * SEQ, j * c.w:(j + 1) * c.w],
                                                turned[:, t % 2, j, s * SEQ:(s + 1) * SEQ], values[:, t, s, j, :],
                                                start=True, stop=True)
            last.then_inc(c.o_full.sem, 1)
        if 0 <= step - c.lag - 1 < TG:
            t = step - c.lag - 1
            ring.before_fill(pe, g, (c.x + "otr", t))
            pe.wait_ge(c.o_done.sem, c.o_done.at(g, t))
            for m in range(KC):
                last = nc.tensor.transpose(ring.bank((c.x + "otr", t))[:, m * P:(m + 1) * P],
                                           O[:, t % 2, m * P:(m + 1) * P], ident[:])
            last.then_inc(ring.full.sem, 1)
        if 0 <= step - c.lag - 2 < TG:
            t = step - c.lag - 2
            ring.before_fill(pe, g, (c.x + "out", t))
            ring.wait_emptied(pe, g, (c.x + "otr", t))
            out_product(ring.bank((c.x + "out", t)), t).then_inc(ring.full.sem, 1)


def core_outputs(nc, dve, g, c, t, OB, O, den, chain, eps):
    dve.wait_ge(c.o_full.sem, c.o_full.at(g, t))
    n, w = c.h // 2, c.d + 1
    got = OB[t % 2][:, 0:n * 2 * w].rearrange("p (j s w) -> p j s w", j=n, s=2)
    sums = den[:, t, 0:2 * n].rearrange("p (j s) -> p j s", s=2)
    if eps:
        chain.link(dve, g, nc.vector.tensor_scalar(sums, got[:, :, :, c.d], eps, None, ALU.add))
        chain.link(dve, g, nc.vector.reciprocal(sums, sums))
    else:
        chain.link(dve, g, nc.vector.reciprocal(sums, got[:, :, :, c.d]))
    if c.keys_first:
        to = O[:, t % 2, :].rearrange("p (s j d) -> p j s d", s=2, d=c.d)
    else:
        to = O[:, t % 2, :].rearrange("p (j s d) -> p j s d", s=2, d=c.d)
    nc.vector.tensor_tensor(to, got[:, :, :, 0:c.d], sums.unsqueeze(3).broadcast_to([P, n, 2, c.d]),
                            ALU.mult).then_inc(c.o_done.sem, 1)


def core_turned_output(nc, act, g, c, t, ring, OT):
    name = (c.x + "otr", t)
    ring.wait_full(act, g, name)
    src = ring.bank(name)[:, 0:KC * P]
    if c.keys_first:
        src = src.rearrange("p (s a q) -> p a s q", s=PER, a=2)
        dst = OT[:, :, t * P:(t + 1) * P].rearrange("p a (s q) -> p a s q", s=PER)
    else:
        src = src.rearrange("p (m q) -> p m q", m=KC)
        dst = OT[:, :, t * P:(t + 1) * P]
    nc.scalar.activation(dst, src, ACT.Copy).then_inc(ring.emptied["A"].sem, 1)


def mask_heads(nc, dve, dst, src, hm, n, chain_event, part=None):
    for h in (range(n) if part is None else part):
        for m in range(KC):
            last = nc.vector.tensor_scalar(dst[:, m, :, h, :], src[:, m, :].rearrange("p (s q) -> p s q", s=GSEQ),
                                           hm[:, h:h + 1], None, ALU.mult)
    if chain_event is not None:
        last.then_inc(chain_event.sem, 1)


class Norm:

    def __init__(self, es, nc, fx, x, continues=None):
        self.fx = fx

        self.events = {}

        def ev(name):
            self.events[name] = Event(es, nc, f"{x}{name}", TG, continues=continues and continues.events[name])
            return self.events[name]

        self.stats = ev("stats")
        self.rstd = ev("rstd")
        self.done = ev("done")

    def moments(self, nc, dve, g, t, x, st, mv, chain):
        chain.link(dve, g, nc.vector.bn_stats(st[:, t, :], x))
        settle(dve, self.fx.dve_passed)
        nc.vector.bn_aggr(mv[:, t, :], st[:, t, :]).then_inc(self.stats.sem, 1)

    def root(self, nc, pool, g, t, mv, rs, neghalf, chain):
        pool.wait_ge(self.stats.sem, self.stats.at(g, t))
        settle(pool, self.fx.pool_passed)
        chain.link(pool, g, nc.gpsimd.tensor_scalar(rs[:, t:t + 1], mv[:, t, 1:2], EPS_LN, None, ALU.add))
        nc.gpsimd.tensor_tensor(rs[:, t:t + 1], rs[:, t:t + 1], neghalf[:, 0:1], ALU.pow).then_inc(self.rstd.sem, 1)

    def apply(self, nc, dve, g, t, x, mv, rs):
        dve.wait_ge(self.rstd.sem, self.rstd.at(g, t))
        nc.vector.tensor_scalar(x, x, mv[:, t, 0:1], rs[:, t:t + 1], ALU.subtract,
                                ALU.mult).then_inc(self.done.sem, 1)


def softmax_scores(nc, dve, g, c, t, S, W, mx, chain, cneg):
    for b in range(2):
        u = 2 * t + b
        dve.wait_ge(c.s_full.sem, c.s_full.at(g, u))
        src, dst = heads(S[u % 4][:], 8), W[:, t % 2, 8 * b:8 * b + 8, :]
        top = mx[:, t, 8 * b:8 * b + 8]
        if cneg is not None:
            chain.link(dve, g, nc.vector.tensor_tensor(dst, src, cneg[:].unsqueeze(1).broadcast_to([P, 8, SEQ]),
                                                       ALU.add))
            src = dst
        chain.link(dve, g, nc.vector.tensor_reduce(top, src, AX, ALU.max))
        nc.vector.tensor_tensor(dst, src, top.unsqueeze(2).broadcast_to([P, 8, SEQ]),
                                ALU.subtract).then_inc(c.s_used.sem, 1)


def softmax_act(nc, act, g, c, ring, S, W, WT, OT, scale):
    for step in range(TG + c.lag + 1):
        if step < TG:
            for b in range(2):
                act.wait_ge(c.s_used.sem, c.s_used.at(g, 2 * step + b))
                part = W[:, step % 2, 8 * b:8 * b + 8, :]
                nc.scalar.activation(part, part, ACT.Exp, scale=scale).then_inc(c.p_ready.sem, 1)
        if 0 <= step - 1 < TG:
            for b in range(2):
                u = 2 * (step - 1) + b
                act.wait_ge(c.pt_full.sem, c.pt_full.at(g, u))
                nc.scalar.activation(WT[:, (step - 1) % 2, 4 * b:4 * b + 4, :],
                                     S[u % 4][:].rearrange("p (j q) -> p j q", j=4),
                                     ACT.Copy).then_inc(c.pt_used.sem, 1)
        if 0 <= step - c.lag - 1 < TG:
            core_turned_output(nc, act, g, c, step - c.lag - 1, ring, OT)


def turned(nc, act, g, ring, name, dst, n):
    ring.wait_full(act, g, name)
    nc.scalar.activation(dst, ring.bank(name)[:, 0:n * P].rearrange("p (m q) -> p m q", m=n),
                         ACT.Copy).then_inc(ring.emptied["A"].sem, 1)


def turn(nc, pe, g, ring, name, sources, ident):
    for m, src in enumerate(sources):
        last = nc.tensor.transpose(ring.bank(name)[:, m * P:(m + 1) * P], src, ident[:])
    last.then_inc(ring.full.sem, 1)


def product(nc, dst, stills, movings):
    n = len(stills)
    for i in range(n):
        last = nc.tensor.matmul(dst, stills[i], movings[i], start=i == 0, stop=i == n - 1)
    return last


def chunks(x, t):
    return [x[:, m, t * P:(t + 1) * P] for m in range(KC)]


def layer0(nc, es, io, fx):
    PJ, SB, OB = fx.PJ, fx.SB, fx.OB
    la = Core(es, nc, "la_", H16, D16, True)
    xa = Core(es, nc, "xa_", H16, D16, False)
    xq_steps = staggered(("xa_xtr", 0), ("xa_q", 1), ("xa_trq", 3))
    fx.linear_core, fx.softmax_core = la, xa
    rt_steps = staggered(("r_xtr", 0), ("r_logit", 1))
    eng = {"xa_xtr": "A", "xa_q": "D", "xa_trq": "A", "r_xtr": "A", "r_logit": "D"}
    uses = [((n, t), e) for n, e in (("la_qk", "D"), ("la_v", "A"), ("xa_k", "D"), ("xa_v", "D"), ("la_tr", "A"),
                                     ("xa_trk", "A")) for t in range(TG)]
    uses += la.uses() + [((n, t), eng[n]) for n, t in xq_steps] + xa.uses() + [((n, t), eng[n]) for n, t in rt_steps]

    def ev(name, per, primed=False, step=1):
        return Event(es, nc, "l0_" + name, per, primed, step)

    full = ev("full", len(uses), True)
    emptied = {k: ev("emptied" + k, sum(e == k for _, e in uses), True) for k in "AD"}
    ring = Ring(PJ, full, emptied, uses)
    fold = es.enter_context(nc.semaphore("l0_fold"))
    folded = es.enter_context(nc.semaphore("l0_folded"))
    zeroed = es.enter_context(nc.semaphore("l0_zeroed"))
    ld_w = es.enter_context(nc.semaphore("l0_ld_w"))
    ld_n = es.enter_context(nc.semaphore("l0_ld_n"))
    ld_x, ld_xt, ld_c = ev("ld_x", 1, step=16), ev("ld_xt", 1, step=16), ev("ld_c", 1, step=16)
    sq = ev("sq", TG)
    ss = ev("ss", 1)
    root = ev("root", 1)
    qn = ev("qn", TG)
    ssk, ssq = ev("ssk", TG), ev("ssq", TG)
    kr, qr = ev("kr", TG), ev("qr", TG)
    kn2, qn2 = ev("kn2", TG), ev("qn2", TG)
    kept_x = ev("kept_x", 1, True, 16 * SHARED)
    ln1, ln2 = Norm(es, nc, fx, "l0n1_"), Norm(es, nc, fx, "l0n2_")
    fx.norms = (ln1, ln2)
    dve_chain = Chain(es, nc, "l0_dve_chain", 33)
    pool_chain = Chain(es, nc, "l0_pool_chain", 4 * TG)
    WLOADS, NLOADS = 4 * 16, 13 * 16

    with ExitStack() as mem:
        def sb(name, shape):
            return mem.enter_context(nc.sbuf_tensor("l0_" + name, shape, F32))

        wqk, wv = sb("wqk", [P, KC, 2 * DIM]), sb("wv", [P, KC, DIM])
        wo, wg = sb("wo", [P, KC, DIM]), sb("wg", [P, KC, E0])
        xwq, xwk, xwv, xwo = (sb("xw" + n, [P, KC, DIM]) for n in "qkvo")
        centre, gcentre = sb("centre", [P, P]), sb("gcentre", [P, P])
        gb, betab, cb = sb("gb", [P, 2]), sb("betab", [P, P]), sb("cb", [P, P])
        qb, kb, vb, ob = sb("qb", [P, DIM]), sb("kb", [P, DIM]), sb("vb", [P, P]), sb("ob", [P, DIM])
        nq, nk = sb("nq", [P, DIM]), sb("nk", [P, DIM])
        XIN, XTIN, CT = sb("XIN", [P, TG, DIM]), sb("XTIN", [P, KC, GTOK]), sb("CT", [P, KC, GTOK])
        X, XT = sb("X", [P, TG, DIM]), sb("XT", [P, KC, GTOK])
        QB, QN = sb("QB", [P, TG, 2 * DIM]), sb("QN", [P, TG, 2 * DIM])
        wnat = QN[:].rearrange("p (n m) o -> p n m o", n=2)[:, :, :, 0:DIM]
        QB2 = sb("QB2", [P, TG, 2 * DIM])
        QKT, QKT2 = sb("QKT", [P, 2 * KC, GTOK]), sb("QKT2", [P, 2 * KC, GTOK])
        QM, KM = sb("QM", [P, KC, GSEQ, 8, SEQ]), sb("KM", [P, KC, GSEQ, 8, SEQ])
        W, WT = sb("W", [P, 2, H16, SEQ]), sb("WT", [P, 2, H16 // 2, P])
        SQ = WT[:].rearrange("p a j q -> p (a j q)").rearrange("p (t o) -> p t o", t=TG)
        V, V2 = sb("V", [P, TG, H16, 2 * 17]), sb("V2", [P, TG, PER, 8, 2 * 17])
        O, OT = sb("O", [P, 2, DIM]), sb("OT", [P, KC, GTOK])
        SS, RS = sb("SS", [P, TG, 32]), sb("RS", [P, TG, 32])
        s1, s2 = sb("s1", [P, 2 * TG]), sb("s2", [P, 2 * TG])
        st, mv, rs = sb("st", [P, TG, 6]), sb("mv", [P, TG, 2]), sb("rs", [P, TG])
        den, mx = sb("den", [P, TG, H16]), sb("mx", [P, TG, H16])

        with nc.Block() as block:
            @block.sync
            def _(sp):
                sp.dma_start(wnat[:, 0], io["la_wq"].rearrange("(m p) i -> p m i", p=P)).then_inc(ld_w, 16)
                sp.dma_start(wnat[:, 1], io["la_wk"].rearrange("(m p) i -> p m i", p=P)).then_inc(ld_w, 16)
                sp.dma_start(centre[:], io["centre"]).then_inc(ld_w, 16)
                sp.dma_start(gb[:], io["gb"]).then_inc(ld_w, 16)
                for dst, src in ((wv, io["la_wv"]), (wo, io["la_wo"]), (xwq, io["xa_wq"]), (xwk, io["xa_wk"]),
                                 (xwv, io["xa_wv"]), (xwo, io["xa_wo"]), (wg, io["wg"])):
                    sp.dma_start(dst[:], src.rearrange("(m p) o -> p m o", p=P)).then_inc(ld_n, 16)
                for dst, src in ((qb, io["qb"]), (kb, io["kb"]), (vb, io["vb"]), (ob, io["ob"]), (nq, io["nq"]), (nk, io["nk"])):
                    sp.dma_start(dst[:], src).then_inc(ld_n, 16)
                with sp.Fori(0, GROUPS) as g:
                    ring.wait_filled_before(sp, g, ("la_v", TG - 1))
                    sp.dma_start(XTIN[:], io["xT"][:, bass.ds(g * GTOK, GTOK)].rearrange(
                        "(m p) t -> p m t", p=P)).then_inc(ld_xt.sem, 16)
                    ring.wait_filled_before(sp, g, ("xa_v", TG - 1))
                    sp.dma_start(CT[:], io["cT"][:, bass.ds(g * GTOK, GTOK)].rearrange(
                        "(m p) t -> p m t", p=P)).then_inc(ld_c.sem, 16)
                    ring.wait_emptied_before(sp, g, ("la_out", TG - 1))
                    sp.dma_start(XIN[:], io["x"][bass.ds(g * GTOK, GTOK), :].rearrange(
                        "(t p) d -> p t d", p=P)).then_inc(ld_x.sem, 16)

            @block.gpsimd
            def _(pool):
                nc.gpsimd.memset(V[:], 0.0)
                nc.gpsimd.memset(V2[:], 0.0).then_inc(zeroed, 1)
                pool.wait_ge(zeroed, 1)
                for a in range(2):
                    half = slice(a * SEQ, (a + 1) * SEQ)
                    nc.gpsimd.memset(V[half, :, :, a * 17 + 16:a * 17 + 17], 1.0)
                    last = nc.gpsimd.memset(V2[half, :, :, :, a * 17 + 16:a * 17 + 17].rearrange(
                        "p t s j o -> p (t s) j o"), 1.0)
                last.then_inc(zeroed, 1)

                def roots(g, t, sums, src, dst, done):
                    pool.wait_ge(sums.sem, sums.at(g, t))
                    settle(pool, fx.pool_passed)
                    pool_chain.link(pool, g, nc.gpsimd.tensor_scalar(dst, src, 1.0 / DIM, EPS_RMS, ALU.mult, ALU.add))
                    nc.gpsimd.tensor_tensor(dst, dst, fx.neghalf[:, 0:1], ALU.pow).then_inc(done.sem, 1)

                with pool.Fori(0, GROUPS) as g:
                    for t in range(TG):
                        roots(g, t, ssk, s1[:, t:t + 1], s2[:, t:t + 1], kr)
                    for t in range(TG):
                        ln1.root(nc, pool, g, t, mv, rs, fx.neghalf, pool_chain)
                    for t in range(TG):
                        roots(g, t, ssq, s1[:, TG + t:TG + t + 1], s2[:, TG + t:TG + t + 1], qr)
                    for t in range(TG):
                        ln2.root(nc, pool, g, t, mv, rs, fx.neghalf, pool_chain)
                pool_chain.close()

            @block.scalar
            def _(act):
                emptied["A"].prime(act)
                kept_x.prime(act)
                act.wait_ge(fx.ready, fx.READY)
                act.wait_ge(zeroed, 2)
                with act.Fori(0, GROUPS) as g:
                    for t in range(TG):
                        ring.wait_emptied(act, g, ("la_qk", t))
                        nc.scalar.activation(SQ[:, t, :], QB[:, t, :], ACT.Square).then_inc(sq.sem, 1)
                    for t in range(TG):
                        name = ("la_v", t)
                        ring.wait_full(act, g, name)
                        for s in range(PER):
                            half = slice(s * SEQ, (s + 1) * SEQ)
                            last = nc.scalar.activation(V[half, t, :, s * 17:s * 17 + 16],
                                                        heads(ring.bank(name)[half, 0:DIM], H16), ACT.Copy)
                        last.then_inc(emptied["A"].sem, 1)
                    act.wait_ge(ss.sem, ss.at(g, 0))
                    nc.scalar.activation(RS[:], SS[:], ACT.Sqrt, bias=fx.epsln[:, 0:1],
                                         scale=1.0 / D16).then_inc(root.sem, 1)
                    for t in range(TG):
                        ring.wait_emptied(act, g, ("xa_k", t))
                        nc.scalar.activation(SQ[:, t, 0:DIM], QB2[:, t, DIM:2 * DIM], ACT.Square,
                                             accum_out=s1[:, t:t + 1]).then_inc(ssk.sem, 1)
                    for t in range(TG):
                        turned(nc, act, g, ring, ("la_tr", t), QKT[:, :, t * P:(t + 1) * P], 2 * KC)
                    for t in range(TG):
                        turned(nc, act, g, ring, ("xa_trk", t), QKT2[:, KC:2 * KC, t * P:(t + 1) * P], KC)
                    for step in range(TG + la.lag + 1):
                        if step < TG:
                            for b in range(la.nb):
                                act.wait_ge(la.s_used.sem, la.s_used.at(g, step * la.nb + b))
                                part = W[:, step % 2, 8 * b:8 * b + 8, :]
                                nc.scalar.activation(part, part, ACT.Square, scale=0.25).then_inc(la.p_ready.sem, 1)
                        if 0 <= step - la.lag - 1 < TG:
                            core_turned_output(nc, act, g, la, step - la.lag - 1, ring, OT)
                    for n, t in xq_steps:
                        if n == "xa_xtr":
                            turned(nc, act, g, ring, (n, t), XT[:, :, t * P:(t + 1) * P], KC)
                        elif n == "xa_q":
                            ring.wait_emptied(act, g, (n, t))
                            nc.scalar.activation(SQ[:, t, 0:DIM], QB2[:, t, 0:DIM], ACT.Square,
                                                 accum_out=s1[:, TG + t:TG + t + 1]).then_inc(ssq.sem, 1)
                        else:
                            turned(nc, act, g, ring, (n, t), QKT2[:, 0:KC, t * P:(t + 1) * P], KC)
                    softmax_act(nc, act, g, xa, ring, SB, W, WT, OT, 0.25)
                    for n, t in rt_steps:
                        if n == "r_xtr":
                            turned(nc, act, g, ring, (n, t), XT[:, :, t * P:(t + 1) * P], KC)
                    act.wait_ge(ln2.done.sem, ln2.done.at(g, TG - 1))
                    for n in range(SHARED):
                        act.dma_start(fx.xs[bass.ds(g * GTOK + n * TOKENS, GTOK), :].rearrange(
                            "(t p) d -> p t d", p=P), X[:]).then_inc(kept_x.sem, 16)
                act.wait_ge(kept_x.sem, 16 * SHARED * (GROUPS + 1))

            @block.vector
            def _(dve):
                emptied["D"].prime(dve)
                dve.wait_ge(fx.ready, fx.READY)
                dve.wait_ge(ld_w, WLOADS)
                nc.vector.tensor_scalar(gcentre[:], centre[:], gb[:, 0:1], None, ALU.mult)
                nc.vector.tensor_scalar(betab[:], fx.ones[:], gb[:, 1:2], None, ALU.mult).then_inc(folded, 1)
                dve.wait_ge(fold, 1)
                nc.vector.tensor_copy(cb[:], OB[0][:, 0:P])
                for n in range(2):
                    for m in range(KC):
                        last = nc.vector.tensor_copy(
                            wqk[:, m, n * DIM:(n + 1) * DIM], SB[2 * n + m][:, 0:DIM])
                last.then_inc(folded, 1)
                dve.wait_ge(folded, 2)
                dve.wait_ge(ld_n, NLOADS)
                dve.wait_ge(zeroed, 2)

                with dve.Fori(0, GROUPS) as g:
                    def residual(name, t, old, norm):
                        ring.wait_full(dve, g, (name, t))
                        nc.vector.tensor_tensor(X[:, t, :], ring.bank((name, t))[:, 0:DIM], old,
                                                ALU.add).then_inc(emptied["D"].sem, 1)
                        ring.wait_emptied(dve, g, (name, t))
                        if norm is ln2:
                            dve_chain.link(dve, g, nc.vector.tensor_tensor(X[:, t, :], X[:, t, :], ob[:], ALU.add))
                        norm.moments(nc, dve, g, t, X[:, t, :], st, mv, dve_chain)

                    for t in range(TG):
                        name = ("la_qk", t)
                        ring.wait_full(dve, g, name)
                        nc.vector.tensor_tensor(QB[:, t, :].rearrange("p (n o) -> p n o", o=P),
                                                ring.bank(name)[:].rearrange("p (n o) -> p n o", o=P),
                                                cb[:].unsqueeze(1).broadcast_to([P, 4, P]),
                                                ALU.add).then_inc(emptied["D"].sem, 1)
                    for t in range(TG):
                        dve.wait_ge(sq.sem, sq.at(g, t))
                        last = nc.vector.tensor_reduce(SS[:, t, :], heads(SQ[:, t, :], 32), AX, ALU.add)
                    last.then_inc(ss.sem, 1)
                    for t in range(TG):
                        name = ("xa_k", t)
                        ring.wait_full(dve, g, name)
                        nc.vector.tensor_tensor(QB2[:, t, DIM:2 * DIM], ring.bank(name)[:, 0:DIM], kb[:],
                                                ALU.add).then_inc(emptied["D"].sem, 1)
                    for t in range(TG):
                        name = ("xa_v", t)
                        ring.wait_full(dve, g, name)
                        for a in range(2):
                            half = slice(a * SEQ, (a + 1) * SEQ)
                            last = nc.vector.tensor_tensor(
                                V2[half, t, :, :, a * 17:a * 17 + 16],
                                ring.bank(name)[half, 0:DIM].rearrange("p (s j d) -> p s j d", s=PER, d=16),
                                heads(vb[half, :], 8).unsqueeze(1).broadcast_to([SEQ, PER, 8, 16]), ALU.add)
                        last.then_inc(emptied["D"].sem, 1)
                    dve.wait_ge(root.sem, root.at(g, 0))
                    dve_chain.link(dve, g, nc.vector.reciprocal(RS[:], RS[:]))
                    for t in range(TG):
                        nc.vector.tensor_tensor(heads(QN[:, t, :], 32), heads(QB[:, t, :], 32),
                                                RS[:, t, :].unsqueeze(2).broadcast_to([P, 32, 16]),
                                                ALU.mult).then_inc(qn.sem, 1)
                    for t in range(TG):
                        dve.wait_ge(kr.sem, kr.at(g, t))
                        nc.vector.scalar_tensor_tensor(out=QB2[:, t, DIM:2 * DIM], in0=QB2[:, t, DIM:2 * DIM],
                                                       scalar=s2[:, t:t + 1], in1=nk[:], op0=ALU.mult,
                                                       op1=ALU.mult).then_inc(kn2.sem, 1)
                    ring.wait_emptied(dve, g, ("la_tr", TG - 1))
                    mask_heads(nc, dve, QM, QKT, fx.hm16, 8, la.masked)
                    ring.wait_emptied(dve, g, ("xa_trk", TG - 1))
                    for step in range(TG + la.lag + 3):
                        if step < TG:
                            for b in range(la.nb):
                                u = step * la.nb + b
                                dve.wait_ge(la.s_full.sem, la.s_full.at(g, u))
                                nc.vector.tensor_tensor(W[:, step % 2, 8 * b:8 * b + 8, :], heads(SB[u % 4][:], 8),
                                                        fx.cmask[:].unsqueeze(1).broadcast_to([P, 8, SEQ]),
                                                        ALU.mult).then_inc(la.s_used.sem, 1)
                            mask_heads(nc, dve, KM, QKT2[:, KC:2 * KC], fx.hm16, 8,
                                       xa.masked if step == TG - 1 else None, range(2 * step, 2 * step + 2))
                        if 0 <= step - la.lag < TG:
                            core_outputs(nc, dve, g, la, step - la.lag, OB, O, den, dve_chain, EPS_LN)
                        if 0 <= step - la.lag - 2 < TG:
                            t = step - la.lag - 2
                            if t == 0:
                                dve.wait_ge(ld_x.sem, ld_x.at(g, 0))
                                dve.wait_ge(kept_x.sem, kept_x.at(g, -1))
                            residual("la_out", t, XIN[:, t, :], ln1)
                        if 0 <= step - la.lag - 3 < TG:
                            ln1.apply(nc, dve, g, step - la.lag - 3, X[:, step - la.lag - 3, :], mv, rs)
                    for n, t in xq_steps:
                        if n == "xa_q":
                            ring.wait_full(dve, g, (n, t))
                            nc.vector.tensor_tensor(QB2[:, t, 0:DIM], ring.bank((n, t))[:, 0:DIM], qb[:],
                                                    ALU.add).then_inc(emptied["D"].sem, 1)
                        elif n == "xa_trq":
                            dve.wait_ge(qr.sem, qr.at(g, t))
                            nc.vector.scalar_tensor_tensor(out=QB2[:, t, 0:DIM], in0=QB2[:, t, 0:DIM],
                                                           scalar=s2[:, TG + t:TG + t + 1], in1=nq[:],
                                                           op0=ALU.mult, op1=ALU.mult).then_inc(qn2.sem, 1)
                    for step in range(TG + xa.lag + 3):
                        if step < TG:
                            softmax_scores(nc, dve, g, xa, step, SB, W, mx, dve_chain, None)
                        if 0 <= step - xa.lag < TG:
                            core_outputs(nc, dve, g, xa, step - xa.lag, OB, O, den, dve_chain, None)
                        if 0 <= step - xa.lag - 2 < TG:
                            t = step - xa.lag - 2
                            residual("xa_out", t, X[:, t, :], ln2)
                        if 0 <= step - xa.lag - 3 < TG:
                            ln2.apply(nc, dve, g, step - xa.lag - 3, X[:, step - xa.lag - 3, :], mv, rs)
                    for t in range(TG):
                        name = ("r_logit", t)
                        ring.wait_full(dve, g, name)
                        nc.vector.tensor_scalar(fx.LG[:, bass.ds(g * TG + t, 1), :], ring.bank(name)[:, 0:E0].unsqueeze(1),
                                                1.0, None, ALU.mult).then_inc(emptied["D"].sem, 1)
                dve_chain.close()

            @block.tensor
            def _(pe):
                full.prime(pe)
                pe.wait_ge(fx.ready, fx.READY)
                pe.wait_ge(ld_w, WLOADS)
                pe.wait_ge(folded, 1)
                nc.tensor.matmul(OB[0][:, 0:P], betab[:], centre[:], start=True, stop=True)
                for n in range(2):
                    for i in range(KC):
                        for m in range(KC):
                            last = nc.tensor.matmul(SB[2 * n + i][:, m * P:(m + 1) * P],
                                                    wnat[:, n, m, i * P:(i + 1) * P], gcentre[:],
                                                    start=True, stop=True)
                last.then_inc(fold, 1)
                pe.wait_ge(folded, 2)
                pe.wait_ge(ld_n, NLOADS)
                with pe.Fori(0, GROUPS) as g:
                    def project(name, t, x, w, wait=None):
                        ring.before_fill(pe, g, (name, t))
                        dst = ring.bank((name, t))[:, 0:w.shape[2]]
                        product(nc, dst, chunks(x, t), [w[:, m, :] for m in range(KC)]).then_inc(full.sem, 1)

                    pe.wait_ge(ld_xt.sem, ld_xt.at(g, 0))
                    for t in range(TG):
                        project("la_qk", t, XTIN, wqk)
                    for t in range(TG):
                        project("la_v", t, XTIN, wv)
                    pe.wait_ge(ld_c.sem, ld_c.at(g, 0))
                    for t in range(TG):
                        project("xa_k", t, CT, xwk)
                    for t in range(TG):
                        ring.before_fill(pe, g, ("xa_v", t))
                        bank = ring.bank(("xa_v", t))
                        for s in range(PER):
                            tok = slice(t * P + s * SEQ, t * P + (s + 1) * SEQ)
                            for a in range(2):
                                last = product(nc, bank[a * SEQ:(a + 1) * SEQ, s * P:(s + 1) * P],
                                               [CT[:, m, tok] for m in range(KC)],
                                               [xwv[:, m, a * P:(a + 1) * P] for m in range(KC)])
                        last.then_inc(full.sem, 1)
                    for t in range(TG):
                        ring.before_fill(pe, g, ("la_tr", t))
                        pe.wait_ge(qn.sem, qn.at(g, t))
                        turn(nc, pe, g, ring, ("la_tr", t), [QN[:, t, i * P:(i + 1) * P] for i in range(4)], fx.ident)
                    for t in range(TG):
                        ring.before_fill(pe, g, ("xa_trk", t))
                        pe.wait_ge(kn2.sem, kn2.at(g, t))
                        turn(nc, pe, g, ring, ("xa_trk", t),
                             [QB2[:, t, DIM + m * P:DIM + (m + 1) * P] for m in range(KC)], fx.ident)

                    def out_la(bank, t):
                        return product(nc, bank[:, 0:DIM], chunks(OT, t), [wo[:, m, :] for m in range(KC)])

                    core_pe(nc, pe, g, la, ring, QKT[:, KC:2 * KC], QM, SB, OB, W, None, V, O, OT, fx.ident, out_la)
                    for n, t in xq_steps:
                        if n == "xa_q":
                            ring.before_fill(pe, g, (n, t))
                            ring.wait_emptied(pe, g, ("xa_xtr", t))
                            dst = ring.bank((n, t))[:, 0:DIM]
                            product(nc, dst, chunks(XT, t), [xwq[:, m, :] for m in range(KC)]).then_inc(full.sem, 1)
                        else:
                            ring.before_fill(pe, g, (n, t))
                            if n == "xa_xtr":
                                pe.wait_ge(ln1.done.sem, ln1.done.at(g, t))
                                src = X
                            else:
                                pe.wait_ge(qn2.sem, qn2.at(g, t))
                                src = QB2
                            turn(nc, pe, g, ring, (n, t), [src[:, t, m * P:(m + 1) * P] for m in range(KC)], fx.ident)
                    ring.wait_emptied(pe, g, ("xa_trq", TG - 1))

                    def out_xa(bank, t):
                        return product(nc, bank[:, 0:DIM], chunks(OT, t), [xwo[:, m, :] for m in range(KC)])

                    core_pe(nc, pe, g, xa, ring, QKT2[:, 0:KC], KM, SB, OB, W, WT, V2, O, OT, fx.ident, out_xa)
                    for n, t in rt_steps:
                        ring.before_fill(pe, g, (n, t))
                        if n == "r_xtr":
                            pe.wait_ge(ln2.done.sem, ln2.done.at(g, t))
                            turn(nc, pe, g, ring, (n, t), [X[:, t, m * P:(m + 1) * P] for m in range(KC)], fx.ident)
                        else:
                            ring.wait_emptied(pe, g, ("r_xtr", t))
                            product(nc, ring.bank((n, t))[:, 0:E0], chunks(XT, t),
                                    [wg[:, m, :] for m in range(KC)]).then_inc(full.sem, 1)


I32 = mybir.dt.int32


class Steps:

    def __init__(self, es, nc, name):
        self.sem, self.k = es.enter_context(nc.semaphore(name)), 0

    def __call__(self, engine, instruction):
        self.k += 1
        instruction.then_inc(self.sem, 1)
        engine.wait_ge(self.sem, self.k)


class Route:

    def __init__(self, es, nc, mem, kept, x, e, k, groups, slot_tiles, first_tile,
                 row_shift):
        self.e, self.k, self.groups, self.slot_tiles, self.first_tile = e, k, groups, slot_tiles, first_tile
        self.row_shift = row_shift
        sb = lambda n, shape, dt=F32: mem.enter_context(nc.sbuf_tensor(x + n, shape, dt))
        self.prob = sb("prob", [P, TILES, e])
        self.masked = sb("masked", [P, TILES, e])
        self.cmp = sb("cmp", [P, TILES, e, e])
        self.cmp2 = sb("cmp2", [P, TILES, e, e])
        self.rank = sb("rank", [P, TILES, e])
        self.sel = sb("sel", [P, TILES, e])
        self.slot = sb("slot", [P, TILES, e])
        self.a, self.b = sb("sa", [P, TILES, e]), sb("sb", [P, TILES, e])
        self.one = sb("one", [P, TILES])
        self.gmax, self.grank = sb("gmax", [P, TILES, max(groups, 1)]), sb("grank", [P, TILES, max(groups, 1)])
        self.nt, self.ends = sb("nt", [P, e]), sb("ends", [P, e])
        self.ends2 = sb("ends2", [P, e])
        self.hot = sb("hot", [P, k, TILES, e])
        self.pick = sb("pick", [P, TILES, e])
        self.posf = sb("posf", [P, TILES, k])
        self.pos, self.wt = kept
        self.row = sb("row", [P, TILES, k], U32) if row_shift else self.pos
        self.tcmp = sb("tcmp", [P, slot_tiles, e])
        self.texpf = sb("texpf", [P, slot_tiles])
        self.texp = sb("texp", [P, first_tile + slot_tiles], I32)
        sem = lambda n: es.enter_context(nc.semaphore(x + n))
        self.shifted, self.exped = sem("shifted"), sem("exped")
        self.chosen, self.counted = sem("chosen"), sem("counted")
        self.placed = sem("placed")
        self.steps = Steps(es, nc, x + "steps")

    def on_act(self, nc, act):
        act.wait_ge(self.shifted, 1)
        nc.scalar.activation(self.prob[:], self.prob[:], ACT.Exp).then_inc(self.exped, 1)

    def on_pe(self, nc, pe, before, ones, rank_bank, total_bank):
        pe.wait_ge(self.chosen, 1)
        n = TILES * self.e
        flat = self.sel[:].rearrange("p t e -> p (t e)")
        nc.tensor.matmul(rank_bank[:, 0:n], before[:], flat, start=True, stop=True)
        nc.tensor.matmul(total_bank[:, 0:n], ones[:], flat, start=True, stop=True).then_inc(self.counted, 1)

    def ranks(self, do, dve, nc, value, rank, n, c1, c2, tri):
        mine = value.unsqueeze(3).broadcast_to([P, TILES, n, n])
        other = value.unsqueeze(2).broadcast_to([P, TILES, n, n])
        do(dve, nc.vector.tensor_tensor(c1, other, mine, ALU.is_equal))
        do(dve, nc.vector.tensor_tensor(c1, c1, tri.unsqueeze(1).broadcast_to([P, TILES, n, n]), ALU.mult))
        do(dve, nc.vector.tensor_tensor(c2, other, mine, ALU.is_gt))
        do(dve, nc.vector.tensor_tensor(c1, c1, c2, ALU.add))
        do(dve, nc.vector.tensor_reduce(rank, c1, AX, ALU.add))

    def on_dve(self, nc, dve, logits, tri, thresholds, tile_row, rank_bank, total_bank):
        do, e, k, v = self.steps, self.e, self.k, nc.vector
        one = self.one[:]
        over = lambda ap, n: ap.unsqueeze(2).broadcast_to([P, TILES, n])
        do(dve, v.tensor_reduce(one, logits, AX, ALU.max))
        v.tensor_tensor(self.prob[:], logits, over(one, e), ALU.subtract).then_inc(self.shifted, 1)
        dve.wait_ge(self.exped, 1)
        do(dve, v.tensor_reduce(one, self.prob[:], AX, ALU.add))
        do(dve, v.reciprocal(one, one))
        do(dve, v.tensor_tensor(self.prob[:], self.prob[:], over(one, e), ALU.mult))
        value = self.prob[:]
        if self.groups:
            ng, per = self.groups, e // self.groups
            do(dve, v.tensor_reduce(self.gmax[:].rearrange("p t g -> p (t g)"), self.prob[:].rearrange("p t (g j) -> p (t g) j", g=ng), AX, ALU.max))
            c = [x[:].rearrange("p t a b -> p (t a b)")[:, 0:TILES * ng * ng].rearrange(
                "p (t a b) -> p t a b", a=ng, b=ng) for x in (self.cmp, self.cmp2)]
            self.ranks(do, dve, nc, self.gmax[:], self.grank[:], ng, c[0], c[1], tri[:, 0:ng, 0:ng])
            do(dve, v.tensor_scalar(self.grank[:], self.grank[:], float(TOPG), None, ALU.is_lt))
            split = lambda x: x.rearrange("p t (g j) -> p (t g) j", j=per)
            keep = self.grank[:].rearrange("p t g -> p (t g)").unsqueeze(2).broadcast_to([P, TILES * ng, per])
            do(dve, v.tensor_tensor(split(self.masked[:]), split(self.prob[:]), keep, ALU.mult))
            do(dve, v.tensor_scalar(self.grank[:], self.grank[:], 1.0, None, ALU.subtract))
            do(dve, v.tensor_tensor(split(self.masked[:]), split(self.masked[:]), keep, ALU.add))
            value = self.masked[:]
        self.ranks(do, dve, nc, value, self.rank[:], e, self.cmp[:], self.cmp2[:], tri[:, 0:e, 0:e])
        v.tensor_scalar(self.sel[:], self.rank[:], float(k), None, ALU.is_lt).then_inc(self.chosen, 1)
        for i in range(k):
            do(dve, v.tensor_scalar(self.hot[:, i], self.rank[:], float(i), None, ALU.is_equal))
            do(dve, v.tensor_tensor(self.pick[:], self.hot[:, i], self.prob[:], ALU.mult))
            do(dve, v.tensor_reduce(self.wt[:, :, i], self.pick[:], AX, ALU.add))
        self.hot_step = do.k
        dve.wait_ge(self.counted, 1)
        total = total_bank[:, 0:TILES * e].rearrange("p (t e) -> p t e", e=e)
        do(dve, v.tensor_copy(self.a[:], total))
        src, dst, d = self.a, self.b, 1
        while d < TILES:
            do(dve, v.tensor_copy(dst[:, 0:d], src[:, 0:d]))
            do(dve, v.tensor_tensor(dst[:, d:], src[:, d:], src[:, 0:TILES - d], ALU.add))
            src, dst, d = dst, src, 2 * d
        count = src[:, TILES - 1, :]
        c = self.cmp[:].rearrange("p t a b -> p (t a b)")[:, 0:e * TILES].rearrange("p (e j) -> p e j", e=e)
        do(dve, v.tensor_tensor(c, count.unsqueeze(2).broadcast_to([P, e, TILES]),
                                thresholds.unsqueeze(1).broadcast_to([P, e, TILES]), ALU.is_gt))
        do(dve, v.tensor_reduce(self.nt[:], c, AX, ALU.add))
        do(dve, v.tensor_tensor(dst[:], src[:], total, ALU.subtract))
        slots = dst
        src, dst, d = self.nt, self.ends, 1
        while d < e:
            do(dve, v.tensor_copy(dst[:, 0:d], src[:, 0:d]))
            do(dve, v.tensor_tensor(dst[:, d:], src[:, d:], src[:, 0:e - d], ALU.add))
            src, dst, d = dst, (self.ends2 if dst is self.ends else self.ends), 2 * d
        ends, first = src, dst
        do(dve, v.tensor_tensor(first[:], ends[:], self.nt[:], ALU.subtract))
        do(dve, v.tensor_scalar(first[:], first[:], float(P), float(P * self.first_tile), ALU.mult, ALU.add))
        do(dve, v.tensor_tensor(self.slot[:], slots[:], first[:].unsqueeze(1).broadcast_to([P, TILES, e]), ALU.add))
        do(dve, v.tensor_tensor(self.slot[:], self.slot[:],
                                rank_bank[:, 0:TILES * e].rearrange("p (t e) -> p t e", e=e), ALU.add))
        for i in range(k):
            do(dve, v.tensor_tensor(self.pick[:], self.hot[:, i], self.slot[:], ALU.mult))
            do(dve, v.tensor_reduce(self.posf[:, :, i], self.pick[:], AX, ALU.add))
        do(dve, v.tensor_copy(self.pos[:], self.posf[:]))
        if self.row_shift:
            do(dve, v.tensor_scalar(self.row[:], self.posf[:], float(self.row_shift), None, ALU.add))
        n = self.slot_tiles
        do(dve, v.tensor_tensor(self.tcmp[:], tile_row[:, 0:n].unsqueeze(2).broadcast_to([P, n, e]),
                                ends[:].unsqueeze(1).broadcast_to([P, n, e]), ALU.is_ge))
        do(dve, v.tensor_reduce(self.texpf[:], self.tcmp[:], AX, ALU.add))
        do(dve, v.tensor_scalar(self.texpf[:], self.texpf[:], float(e - 1), None, ALU.min))
        v.tensor_copy(self.texp[:, self.first_tile:], self.texpf[:]).then_inc(self.placed, 1)


def tile_pipeline(engine, step, n, split, at_split):
    if split:
        with engine.Fori(0, split // 4) as i:
            for b in range(4):
                step(i * 4 + b, b, None)
        at_split()
    with engine.Fori(split // 4, n // 4 - 1) as i:
        for b in range(4):
            step(i * 4 + b, b, None)
    for b in range(4):
        step(n - 4 + b, b, 3 - b)


def moe0(nc, es, io, fx):
    NS, NSH = fx.NS0, SHARED * TILES
    NT = NSH + NS
    SPLIT = NSH - 4
    IW, KI = 2 * I0, I0 - P
    with ExitStack() as mem:
        def sb(name, shape, dt=F32):
            return mem.enter_context(nc.sbuf_tensor("m0_" + name, shape, dt))

        def sem(name):
            return es.enter_context(nc.semaphore("m0_" + name))

        r = Route(es, nc, mem, (fx.pos0, fx.wt0), "r0_", E0, TOP0, NGRP, NS, NSH, 0)
        W13 = sb("W13", [P, KC, EALL, IW])
        W2A, W2B = sb("W2A", [P, EALL, DIM]), sb("W2B", [P, EALL, DIM])
        XG, XGT = sb("XG", [P, 4, DIM]), sb("XGT", [P, 2, KC * P])
        SG, H, HT = sb("SG", [P, 2, I0]), sb("H", [P, 2, I0]), sb("HT", [P, 2, 2, P])
        Y = sb("Y", [P, 2, DIM])
        XD = sb("XD", [P, TILES, DIM])
        shared_set = sem("shared_set")
        BT, BH, BU, BY = fx.PJ, fx.SB[0:2], fx.SB[2:4], fx.OB
        ld_sh, ld_w = sem("ld_sh"), sem("ld_w")
        ld_xd, sent = sem("ld_xd"), sem("sent")
        ld_x = [sem(f"ld_x{b}") for b in range(4)]
        t_full, t_used = sem("t_full"), sem("t_used")
        u_full, gate, h_done = sem("u_full"), sem("gate"), sem("h_done")
        ht_full, ht_used = sem("ht_full"), sem("ht_used")
        y_full, y_used = sem("y_full"), sem("y_used")
        stored = [sem(f"stored{b}") for b in range(2)]

        with nc.Block() as block:
            @block.sync
            def _(sp):
                for b in range(2):
                    sp.sem_inc(stored[b], 16)

                def load(j, b):
                    sp.wait_ge(t_full, j + 1)
                    sp.dma_start(XG[:, b, :], fx.xs[bass.ds(j * P, P), :]).then_inc(ld_x[b], 16)

                for j in range(4):
                    load(j, j)
                for m in range(KC):
                    sp.dma_start(W13[:, m, E0:EALL, :], io["w13"][m, :, E0:EALL, :]).then_inc(ld_sh, 16)
                sp.dma_start(W2A[:, E0:EALL, :], io["w2"][0:P, E0:EALL, :]).then_inc(ld_sh, 16)
                sp.dma_start(W2B[0:KI, E0:EALL, :], io["w2"][P:I0, E0:EALL, :]).then_inc(ld_sh, 16)
                sp.dma_start(XD[:], fx.xs[0:TOKENS, :].rearrange("(t p) d -> p t d", p=P)).then_inc(ld_xd, 16)
                for m in range(KC):
                    sp.dma_start(W13[:, m, 0:E0, :], io["w13"][m, :, 0:E0, :]).then_inc(ld_w, 16)
                sp.dma_start(W2A[:, 0:E0, :], io["w2"][0:P, 0:E0, :]).then_inc(ld_w, 16)
                sp.dma_start(W2B[0:KI, 0:E0, :], io["w2"][P:I0, 0:E0, :]).then_inc(ld_w, 16)

                def step(j, b, ahead):
                    if ahead is None:
                        load(j + 4, b)
                    sp.wait_ge(y_used, j + 1)
                    sp.dma_start(fx.ys[bass.ds(j * P, P), :], Y[:, b % 2, :]).then_inc(stored[b % 2], 16)

                tile_pipeline(sp, step, NT, SPLIT, lambda: sp.wait_ge(sent, 16 * TILES * TOP0))
                for b in range(2):
                    sp.wait_ge(stored[b], 16 + 8 * NT)

            @block.gpsimd
            def _(pool):
                pool.wait_ge(ld_xd, 16)
                pool.wait_ge(fx.slots_zeroed, 16)
                pool.wait_ge(r.placed, 1)
                for t in range(TILES):
                    for k in range(TOP0):
                        pool.indirect_dma_start(
                            out=fx.xs, out_offset=bass.IndirectOffsetOnAxis(ap=r.pos[:, t, k:k + 1], axis=0),
                            in_=XD[:, t, :], in_offset=None).then_inc(sent, 16)

            @block.scalar
            def _(act):
                r.on_act(nc, act)

                def rows(j, b):
                    act.wait_ge(t_full, j + 5)
                    nc.scalar.activation(XGT[:, b % 2, :], BT[b % 2][:, 0:KC * P], ACT.Copy).then_inc(t_used, 1)

                def silu(j, b):
                    act.wait_ge(u_full, j + 1)
                    nc.scalar.activation(SG[:, b % 2, :], BU[b % 2][:, 0:I0], ACT.Silu).then_inc(gate, 1)

                def step(j, b, ahead):
                    if ahead is None or ahead >= 2:
                        rows(j + 2, b)
                    act.wait_ge(ht_full, j + 1)
                    nc.scalar.activation(HT[:, b % 2, 0, :], BH[b % 2][:, 0:P], ACT.Copy)
                    nc.scalar.activation(HT[0:KI, b % 2, 1, :], BH[b % 2][0:KI, P:2 * P], ACT.Copy).then_inc(ht_used, 1)
                    if ahead is None or ahead >= 1:
                        silu(j + 1, b + 1)

                rows(0, 0)
                rows(1, 1)
                silu(0, 0)
                tile_pipeline(act, step, NT, SPLIT, lambda: None)

            @block.vector
            def _(dve):
                for n in range(SHARED):
                    last = nc.vector.memset(r.texp[:, n * TILES:(n + 1) * TILES], E0 + n)
                last.then_inc(shared_set, 1)
                r.on_dve(nc, dve, fx.LG[:], fx.tri16[:], fx.thresholds[:], fx.tile_row[:], BH[0], BH[1])

                def product(j, b):
                    dve.wait_ge(gate, j + 1)
                    nc.vector.tensor_tensor(H[:, b % 2, :], BU[b % 2][:, I0:IW], SG[:, b % 2, :],
                                            ALU.mult).then_inc(h_done, 1)

                def step(j, b, ahead):
                    if ahead is None or ahead >= 1:
                        product(j + 1, b + 1)
                    dve.wait_ge(y_full, j + 1)
                    dve.wait_ge(stored[b % 2], 8 * (j + (2 - b % 2)))
                    nc.vector.tensor_copy(Y[:, b % 2, :], BY[b % 2][:, 0:DIM]).then_inc(y_used, 1)

                product(0, 0)
                tile_pipeline(dve, step, NT, SPLIT, lambda: None)

            @block.tensor
            def _(pe):
                pe.sem_inc(t_full, 4)
                r.on_pe(nc, pe, fx.before, fx.ones, BH[0], BH[1])

                def expert(j):
                    return pe.value_load(r.texp[0:1, bass.ds(j, 1)], min_val=0, max_val=EALL - 1)

                def rows(j, b):
                    pe.wait_ge(ld_x[b], 4 * (j - b) + 16)
                    for m in range(KC):
                        last = nc.tensor.transpose(BT[b % 2][:, m * P:(m + 1) * P], XG[:, b, m * P:(m + 1) * P],
                                                   fx.ident[:])
                    last.then_inc(t_full, 1)

                def gate_up(j, b):
                    e = expert(j)
                    pe.wait_ge(t_used, j + 1)
                    for m in range(KC):
                        last = nc.tensor.matmul(BU[b % 2][:, 0:IW], XGT[:, b % 2, m * P:(m + 1) * P],
                                                W13[:, m, bass.ds(e, 1), :], start=m == 0, stop=m == KC - 1)
                    last.then_inc(u_full, 1)

                def step(j, b, ahead):
                    if ahead is None or ahead >= 2:
                        rows(j + 2, (b + 2) % 4)
                    pe.wait_ge(h_done, j + 1)
                    nc.tensor.transpose(BH[b % 2][:, 0:P], H[:, b % 2, 0:P], fx.ident[:])
                    nc.tensor.transpose(BH[b % 2][0:KI, P:2 * P], H[:, b % 2, P:I0], fx.ident[:]).then_inc(ht_full, 1)
                    if ahead is None or ahead >= 1:
                        gate_up(j + 1, b + 1)
                    e = expert(j)
                    pe.wait_ge(ht_used, j + 1)
                    nc.tensor.matmul(BY[b % 2][:, 0:DIM], HT[:, b % 2, 0, :], W2A[:, bass.ds(e, 1), :],
                                     start=True, stop=False)
                    nc.tensor.matmul(BY[b % 2][:, 0:DIM], HT[0:KI, b % 2, 1, :], W2B[0:KI, bass.ds(e, 1), :],
                                     start=False, stop=True).then_inc(y_full, 1)

                def routed():
                    pe.wait_ge(r.placed, 1)
                    pe.wait_ge(ld_w, 64)

                pe.wait_ge(shared_set, 1)
                rows(0, 0)
                rows(1, 1)
                pe.wait_ge(ld_sh, 64)
                gate_up(0, 0)
                tile_pipeline(pe, step, NT, SPLIT, routed)


def layer1(nc, es, io, fx):
    PJ, SB, OB = fx.PJ, fx.SB, fx.OB
    sa = Core(es, nc, "sa_", H16, D16, False, fx.softmax_core)
    xb = Core(es, nc, "xb_", H32, D32, True, fx.linear_core)
    xb.s_used = xb.p_ready
    xq_steps = staggered(("xb_xtr", 0), ("xb_q", 1))
    engine_of = {"xb_out": "D", "sa_out": "D", "r1_logit": "D"}
    names = [(n, t) for n in ("xb_k", "xb_v", "sa_xtr") for t in range(TG)]
    names += [(n, m) for n in ("sa_q", "sa_k") for m in range(KC)]
    names += [(n, t) for n in ("sa_v", "xb_trk") for t in range(TG)]
    names += [n for n, _ in sa.uses()] + xq_steps + [("xb_trq", t) for t in range(TG)]
    names += [n for n, _ in xb.uses()] + [("r1_xtr", t) for t in range(TG)] + [("r1_h", 0), ("r1_logit", 0)]
    uses = [(n, engine_of.get(n[0], "A")) for n in names]

    def ev(name, per, primed=False, step=1):
        return Event(es, nc, "l1_" + name, per, primed, step)

    full = ev("full", len(uses), True)
    emptied = {k: ev("emptied" + k, sum(e == k for _, e in uses), True) for k in "AD"}
    ring = Ring(PJ, full, emptied, uses)
    zeroed = es.enter_context(nc.semaphore("l1_zeroed"))
    ld_n = es.enter_context(nc.semaphore("l1_ld_n"))
    ld_c = ev("ld_c", 1, step=16)
    ld_r = ev("ld_r", 1, step=48)
    slots_read = ev("slots_read", 1)
    gathered = ev("gathered", TG, step=16 * TOP0)
    combined = ev("combined", 1, True)
    ssk, ssq = ev("ssk", 1), ev("ssq", 1)
    kr, qr = ev("kr", 1), ev("qr", 1)
    kn, qn = ev("kn", TG), ev("qn", TG)
    kept_x = ev("kept_x", 1, True, 16)
    ln0, (ln1, ln2) = Norm(es, nc, fx, "l1n0_"), (Norm(es, nc, fx, None, n) for n in fx.norms)
    dve_chain = Chain(es, nc, "l1_dve_chain", 6 + 3 * TG + 2 + 2 * 2 * TG + 2 * TG)
    pool_chain = Chain(es, nc, "l1_pool_chain", 3 * TG)
    NLOADS = 7 * 16

    with ExitStack() as mem:
        def sb(name, shape, dt=F32):
            return mem.enter_context(nc.sbuf_tensor("l1_" + name, shape, dt))

        wq, wk, wv, wo = sb("wq", [P, KC, DIM]), sb("wk", [P, KC, DIM]), sb("wv", [P, KC, SEQ]), sb("wo", [P, KC, DIM])
        xwq, xwkv = sb("xwq", [P, KC, DIM]), sb("xwkv", [P, KC, 2 * DIM])
        rw1, rw2 = sb("rw1", [P, KC, P]), sb("rw2", [P, E1])
        XIN, SH, GA = sb("XIN", [P, TG, DIM]), sb("SH", [P, SHARED, TG, DIM]), sb("GA", [P, TG, TOP0, DIM])
        slots, weight = sb("slots", [P, TG, TOP0], U32), sb("weight", [P, TG, TOP0])
        CT, X, XT = sb("CT", [P, KC, GTOK]), sb("X", [P, TG, DIM]), sb("XT", [P, KC, GTOK])
        QKT, KN, QN = sb("QKT", [P, 2 * KC, GTOK]), sb("KN", [P, TG, DIM]), sb("QN", [P, TG, DIM])
        KT, QT = sb("KT", [P, KC, GTOK]), sb("QT", [P, KC, GTOK])
        QM = sb("QM", [P, KC, GSEQ, 16, SEQ])
        KM = QM[:].rearrange("p m s h q -> p (m s h q)")[:, 0:KC * GSEQ * 8 * SEQ].rearrange(
            "p (m s h q) -> p m s h q", m=KC, s=GSEQ, h=8)
        W, WT = sb("W", [P, 2, H32, SEQ]), sb("WT", [P, 2, H16 // 2, P])
        VS, VX = sb("VS", [P, TG, PER, 8, 2 * 17]), sb("VX", [P, TG, H32, 2 * 9])
        O, OT, HR = sb("O", [P, 2, DIM]), sb("OT", [P, KC, GTOK]), sb("HR", [P, GTOK])
        SK, SQH, RK, RQ = (sb(n, [P, TG, H32]) for n in ("SK", "SQH", "RK", "RQ"))
        st, mv, rs = sb("st", [P, TG, 6]), sb("mv", [P, TG, 2]), sb("rs", [P, TG])
        den, mx = sb("den", [P, TG, H32]), sb("mx", [P, TG, H16])
        SQ = WT[:].rearrange("p a j q -> p (a j q)")[:, 0:TG * DIM].rearrange("p (t o) -> p t o", t=TG)
        WS = W[:, :, 0:H16, :]

        with nc.Block() as block:
            @block.sync
            def _(sp):
                for dst, src in ((xwkv, io["xb_wkv"]), (wq, io["sa_wq"]), (wk, io["sa_wk"]), (wv, io["sa_wv"]), (wo, io["sa_wo"]),
                                 (xwq, io["xb_wq"]), (rw1, io["rw1"])):
                    sp.dma_start(dst[:], src.rearrange("(m p) o -> p m o", p=P)).then_inc(ld_n, 16)
                sp.dma_start(rw2[:], io["rw2"]).then_inc(ld_n, 16)
                with sp.Fori(0, GROUPS) as g:
                    ring.wait_filled_before(sp, g, ("xb_v", TG - 1))
                    sp.dma_start(CT[:], io["cT"][:, bass.ds(g * GTOK, GTOK)].rearrange(
                        "(m p) t -> p m t", p=P)).then_inc(ld_c.sem, 16)
                    sp.wait_ge(combined.sem, combined.at(g, -1))
                    for dst, src, first in ((XIN[:], fx.xs, 0), (SH[:, 0], fx.ys, 0), (SH[:, 1], fx.ys, TOKENS)):
                        sp.dma_start(dst, src[bass.ds(g * GTOK + first, GTOK), :].rearrange(
                            "(t p) d -> p t d", p=P)).then_inc(ld_r.sem, 16)

            @block.gpsimd
            def _(pool):
                nc.gpsimd.memset(VS[:], 0.0)
                nc.gpsimd.memset(VX[:], 0.0).then_inc(zeroed, 1)
                pool.wait_ge(zeroed, 1)
                for a in range(2):
                    half = slice(a * SEQ, (a + 1) * SEQ)
                    nc.gpsimd.memset(VS[half, :, :, :, a * 17 + 16:a * 17 + 17].rearrange(
                        "p t s j o -> p (t s) j o"), 1.0)
                    last = nc.gpsimd.memset(VX[half, :, :, a * 9 + 8:a * 9 + 9], 1.0)
                last.then_inc(zeroed, 1)

                def gather(g):
                    pool.wait_ge(combined.sem, combined.at(g, -1))
                    nc.gpsimd.tensor_copy(slots[:], fx.pos0[:, bass.ds(g * TG, TG), :]).then_inc(slots_read.sem, 1)
                    pool.wait_ge(slots_read.sem, slots_read.at(g, 0))
                    settle(pool, fx.pool_passed)
                    for t in range(TG):
                        for k in range(TOP0):
                            pool.indirect_dma_start(
                                out=GA[:, t, k, :], out_offset=None, in_=fx.ys,
                                in_offset=bass.IndirectOffsetOnAxis(ap=slots[:, t, k:k + 1], axis=0),
                            ).then_inc(gathered.sem, 16)

                def norms(g, which):
                    for t in range(TG):
                        which.root(nc, pool, g, t, mv, rs, fx.neghalf, pool_chain)

                pool.wait_ge(zeroed, 2)
                gather(0)
                with pool.Fori(0, GROUPS - 1) as g:
                    norms(g, ln0)
                    pool.wait_ge(ln0.rstd.sem, ln0.rstd.at(g, TG - 1))
                    gather(g + 1)
                    norms(g, ln1)
                    norms(g, ln2)
                pool_chain.close()
                pool_chain.k = 0
                for which in (ln0, ln1, ln2):
                    norms(GROUPS - 1, which)

            @block.scalar
            def _(act):
                emptied["A"].prime(act)
                kept_x.prime(act)
                act.wait_ge(zeroed, 2)
                with act.Fori(0, GROUPS) as g:
                    def copy_and_square(name, t, dst):
                        ring.wait_full(act, g, (name, t))
                        src = ring.bank((name, t))[:, 0:DIM]
                        nc.scalar.activation(dst[:, t, :], src, ACT.Copy)
                        nc.scalar.activation(SQ[:, t, :], src, ACT.Square).then_inc(emptied["A"].sem, 1)

                    for t in range(TG):
                        copy_and_square("xb_k", t, KN)
                    for t in range(TG):
                        name = ("xb_v", t)
                        ring.wait_full(act, g, name)
                        for s in range(PER):
                            half = slice(s * SEQ, (s + 1) * SEQ)
                            last = nc.scalar.activation(VX[half, t, :, s * 9:s * 9 + 8],
                                                        heads(ring.bank(name)[half, 0:DIM], H32), ACT.Copy)
                        last.then_inc(emptied["A"].sem, 1)
                    act.wait_ge(ssk.sem, ssk.at(g, 0))
                    nc.scalar.activation(RK[:], SK[:], ACT.Sqrt, bias=fx.epsrms[:, 0:1],
                                         scale=1.0 / D32).then_inc(kr.sem, 1)
                    for t in range(TG):
                        turned(nc, act, g, ring, ("sa_xtr", t), XT[:, :, t * P:(t + 1) * P], KC)
                    for i, name in enumerate(("sa_q", "sa_k")):
                        for m in range(KC):
                            ring.wait_full(act, g, (name, m))
                            nc.scalar.activation(QKT[:, i * KC + m, :], ring.bank((name, m))[:],
                                                 ACT.Copy).then_inc(emptied["A"].sem, 1)
                    for t in range(TG):
                        name = ("sa_v", t)
                        ring.wait_full(act, g, name)
                        for a in range(2):
                            half = slice(a * SEQ, (a + 1) * SEQ)
                            last = nc.scalar.activation(
                                VS[half, t, :, :, a * 17:a * 17 + 16].rearrange("p s (v i) d -> p (s v) i d", i=2),
                                ring.bank(name)[half, 0:PER * SEQ].rearrange("p (v d) -> p v d", d=16).unsqueeze(
                                    2).broadcast_to([SEQ, PER * 4, 2, 16]), ACT.Copy)
                        last.then_inc(emptied["A"].sem, 1)
                    for t in range(TG):
                        turned(nc, act, g, ring, ("xb_trk", t), KT[:, :, t * P:(t + 1) * P], KC)
                    softmax_act(nc, act, g, sa, ring, SB, WS, WT, OT, 0.25)
                    for n, t in xq_steps:
                        if n == "xb_xtr":
                            turned(nc, act, g, ring, (n, t), XT[:, :, t * P:(t + 1) * P], KC)
                        else:
                            copy_and_square(n, t, QN)
                    act.wait_ge(ssq.sem, ssq.at(g, 0))
                    nc.scalar.activation(RQ[:], SQH[:], ACT.Sqrt, bias=fx.epsrms[:, 0:1],
                                         scale=1.0 / D32).then_inc(qr.sem, 1)
                    for t in range(TG):
                        turned(nc, act, g, ring, ("xb_trq", t), QT[:, :, t * P:(t + 1) * P], KC)
                    for step in range(TG + xb.lag + 1):
                        if step < TG:
                            for b in range(xb.nb):
                                u = step * xb.nb + b
                                act.wait_ge(xb.s_full.sem, xb.s_full.at(g, u))
                                nc.scalar.activation(W[:, step % 2, 8 * b:8 * b + 8, :], heads(SB[u % 4][:], 8),
                                                     ACT.Exp, scale=D32 ** -0.5).then_inc(xb.p_ready.sem, 1)
                        if 0 <= step - xb.lag - 1 < TG:
                            core_turned_output(nc, act, g, xb, step - xb.lag - 1, ring, OT)
                    for t in range(TG):
                        turned(nc, act, g, ring, ("r1_xtr", t), XT[:, :, t * P:(t + 1) * P], KC)
                    act.wait_ge(ln2.done.sem, ln2.done.at(g, TG - 1))
                    act.dma_start(fx.xs1[bass.ds(g * GTOK, GTOK), :].rearrange(
                        "(t p) d -> p t d", p=P), X[:]).then_inc(kept_x.sem, 16)
                    ring.wait_full(act, g, ("r1_h", 0))
                    nc.scalar.activation(HR[:], ring.bank(("r1_h", 0))[:], ACT.Gelu).then_inc(emptied["A"].sem, 1)
                act.wait_ge(kept_x.sem, 16 * (GROUPS + 1))

            @block.vector
            def _(dve):
                emptied["D"].prime(dve)
                combined.prime(dve)
                with dve.Fori(0, GROUPS) as g:
                    def residual(name, t, norm, order):
                        ring.wait_full(dve, g, (name, t))
                        x = X[:, t, :].rearrange(order, a=2, d=D32) if order else X[:, t, :]
                        y = ring.bank((name, t))[:, 0:DIM]
                        y = y.rearrange("p (a j d) -> p a j d", a=2, d=D32) if order else y
                        nc.vector.tensor_tensor(x, y, x, ALU.add).then_inc(emptied["D"].sem, 1)
                        ring.wait_emptied(dve, g, (name, t))
                        norm.moments(nc, dve, g, t, X[:, t, :], st, mv, dve_chain)

                    def inverse_roots(ss, sums, names, root, roots, values, done):
                        for t in range(TG):
                            ring.wait_emptied(dve, g, (names, t))
                            last = nc.vector.tensor_reduce(sums[:, t, :], heads(SQ[:, t, :], H32), AX, ALU.add)
                        last.then_inc(ss.sem, 1)
                        yield
                        dve.wait_ge(root.sem, root.at(g, 0))
                        dve_chain.link(dve, g, nc.vector.reciprocal(roots[:], roots[:]))
                        for t in range(TG):
                            nc.vector.tensor_tensor(heads(values[:, t, :], H32), heads(values[:, t, :], H32),
                                                    roots[:, t, :].unsqueeze(2).broadcast_to([P, H32, D32]),
                                                    ALU.mult).then_inc(done.sem, 1)
                        yield

                    dve_chain.link(dve, g, nc.vector.tensor_scalar(weight[:], fx.wt0[:, bass.ds(g * TG, TG), :],
                                                                   1.0, None, ALU.mult))
                    dve.wait_ge(ld_r.sem, ld_r.at(g, 0))
                    dve.wait_ge(kept_x.sem, kept_x.at(g, -1))
                    dve_chain.link(dve, g, nc.vector.tensor_tensor(X[:], XIN[:], SH[:, 0], ALU.add))
                    dve_chain.link(dve, g, nc.vector.tensor_tensor(X[:], X[:], SH[:, 1], ALU.add))
                    dve.wait_ge(gathered.sem, gathered.at(g, TG - 1))
                    for k in range(TOP0):
                        for t in range(TG):
                            last = nc.vector.scalar_tensor_tensor(out=X[:, t, :], in0=GA[:, t, k, :],
                                                                  scalar=weight[:, t, k:k + 1], in1=X[:, t, :],
                                                                  op0=ALU.mult, op1=ALU.add)
                        if k < TOP0 - 1:
                            dve_chain.link(dve, g, last)
                    last.then_inc(combined.sem, 1)
                    dve.wait_ge(combined.sem, combined.at(g, 0))
                    for t in range(TG):
                        ln0.moments(nc, dve, g, t, X[:, t, :], st, mv, dve_chain)
                    k_norm = inverse_roots(ssk, SK, "xb_k", kr, RK, KN, kn)
                    next(k_norm)
                    for t in range(TG):
                        ln0.apply(nc, dve, g, t, X[:, t, :], mv, rs)
                    next(k_norm)
                    ring.wait_emptied(dve, g, ("sa_k", KC - 1))
                    mask_heads(nc, dve, KM, QKT[:, KC:2 * KC], fx.hm16, 8, sa.masked)
                    for step in range(TG + sa.lag + 3):
                        if step < TG:
                            softmax_scores(nc, dve, g, sa, step, SB, WS, mx, dve_chain, fx.cneg)
                        if 0 <= step - sa.lag < TG:
                            core_outputs(nc, dve, g, sa, step - sa.lag, OB, O, den, dve_chain, None)
                        if 0 <= step - sa.lag - 2 < TG:
                            residual("sa_out", step - sa.lag - 2, ln1, None)
                        if 0 <= step - sa.lag - 3 < TG:
                            ln1.apply(nc, dve, g, step - sa.lag - 3, X[:, step - sa.lag - 3, :], mv, rs)
                    q_norm = inverse_roots(ssq, SQH, "xb_q", qr, RQ, QN, qn)
                    next(q_norm)
                    next(q_norm)
                    ring.wait_emptied(dve, g, ("xb_trq", TG - 1))
                    mask_heads(nc, dve, QM, QT, fx.hm8, 16, xb.masked)
                    for step in range(TG + xb.lag + 3):
                        if 0 <= step - xb.lag < TG:
                            core_outputs(nc, dve, g, xb, step - xb.lag, OB, O, den, dve_chain, None)
                        if 0 <= step - xb.lag - 2 < TG:
                            residual("xb_out", step - xb.lag - 2, ln2, "p (j a d) -> p a j d")
                        if 0 <= step - xb.lag - 3 < TG:
                            ln2.apply(nc, dve, g, step - xb.lag - 3, X[:, step - xb.lag - 3, :], mv, rs)
                    name = ("r1_logit", 0)
                    ring.wait_full(dve, g, name)
                    nc.vector.tensor_scalar(fx.LG1[:, bass.ds(g * TG, TG), :],
                                            ring.bank(name)[:, 0:TG * E1].rearrange("p (t e) -> p t e", e=E1),
                                            1.0, None, ALU.mult).then_inc(emptied["D"].sem, 1)
                dve_chain.close()

            @block.tensor
            def _(pe):
                full.prime(pe)
                pe.wait_ge(ld_n, NLOADS + 16)
                with pe.Fori(0, GROUPS) as g:
                    def fill(name, t, stills, movings, width):
                        ring.before_fill(pe, g, (name, t))
                        product(nc, ring.bank((name, t))[:, 0:width], stills, movings).then_inc(full.sem, 1)

                    def turn_rows(name, t, done, src):
                        ring.before_fill(pe, g, (name, t))
                        pe.wait_ge(done.sem, done.at(g, t))
                        turn(nc, pe, g, ring, (name, t), [src[:, t, m * P:(m + 1) * P] for m in range(KC)], fx.ident)

                    pe.wait_ge(ld_c.sem, ld_c.at(g, 0))
                    for i, name in enumerate(("xb_k", "xb_v")):
                        for t in range(TG):
                            fill(name, t, chunks(CT, t), [xwkv[:, m, i * DIM:(i + 1) * DIM] for m in range(KC)], DIM)
                    for t in range(TG):
                        turn_rows("sa_xtr", t, ln0.done, X)
                    ring.wait_emptied(pe, g, ("sa_xtr", TG - 1))
                    for name, w in (("sa_q", wq), ("sa_k", wk)):
                        for o in range(KC):
                            fill(name, o, [w[:, m, o * P:(o + 1) * P] for m in range(KC)],
                                 [XT[:, m, :] for m in range(KC)], GTOK)
                    for t in range(TG):
                        ring.before_fill(pe, g, ("sa_v", t))
                        bank = ring.bank(("sa_v", t))
                        for s in range(PER):
                            tok = slice(t * P + s * SEQ, t * P + (s + 1) * SEQ)
                            for a in range(2):
                                last = product(nc, bank[a * SEQ:(a + 1) * SEQ, s * SEQ:(s + 1) * SEQ],
                                               [XT[:, m, tok] for m in range(KC)], [wv[:, m, :] for m in range(KC)])
                        last.then_inc(full.sem, 1)
                    for t in range(TG):
                        turn_rows("xb_trk", t, kn, KN)

                    def out_sa(bank, t):
                        return product(nc, bank[:, 0:DIM], chunks(OT, t), [wo[:, m, :] for m in range(KC)])

                    core_pe(nc, pe, g, sa, ring, QKT[:, 0:KC], KM, SB, OB, WS, WT, VS, O, OT, fx.ident, out_sa)
                    for n, t in xq_steps:
                        if n == "xb_xtr":
                            turn_rows(n, t, ln1.done, X)
                        else:
                            ring.wait_emptied(pe, g, ("xb_xtr", t))
                            fill(n, t, chunks(XT, t), [xwq[:, m, :] for m in range(KC)], DIM)
                    for t in range(TG):
                        turn_rows("xb_trq", t, qn, QN)

                    def out_xb(bank, t):
                        for a in range(2):
                            last = nc.tensor.transpose(bank[:, a * P:(a + 1) * P], OT[:, a, t * P:(t + 1) * P],
                                                       fx.ident[:])
                        return last

                    core_pe(nc, pe, g, xb, ring, KT, QM, SB, OB, W, None, VX, O, OT, fx.ident, out_xb)
                    for t in range(TG):
                        turn_rows("r1_xtr", t, ln2.done, X)
                    ring.wait_emptied(pe, g, ("r1_xtr", TG - 1))
                    fill("r1_h", 0, [rw1[:, m, :] for m in range(KC)], [XT[:, m, :] for m in range(KC)], GTOK)
                    name = ("r1_logit", 0)
                    ring.before_fill(pe, g, name)
                    ring.wait_emptied(pe, g, ("r1_h", 0))
                    for t in range(TG):
                        last = nc.tensor.matmul(ring.bank(name)[:, t * E1:(t + 1) * E1], HR[:, t * P:(t + 1) * P],
                                                rw2[:], start=True, stop=True)
                    last.then_inc(full.sem, 1)


def moe1(nc, es, io, fx):
    NS, CH = fx.NS1, I1 // P
    E2 = 2 * E1
    HALF, HC = I1 // 2, CH // 2
    with ExitStack() as kept:
        def keep(name, shape):
            return kept.enter_context(nc.sbuf_tensor("m1_" + name, shape, F32))

        def sem(name):
            return es.enter_context(nc.semaphore("m1_" + name))

        AC, ZB = keep("AC", [P, TILES, E2]), keep("ZB", [P, DIM])
        z_done = sem("z_done")
        with ExitStack() as mem:
            def sb(name, shape):
                return mem.enter_context(nc.sbuf_tensor("m1_" + name, shape, F32))

            r = Route(es, nc, mem, (fx.pos1, fx.wt1), "r1_", E1, TOP1, 0, NS, 0, TOKENS)
            w1, w2 = sb("w1", [P, KC, E1, I1]), sb("w2", [P, E1, CH, DIM])
            b1 = sb("b1", [P, E1, I1])
            b1T, b2 = sb("b1T", [P, E1, CH]), sb("b2", [P, DIM])
            eye = sb("eye", [P, E1, E2])
            GB = r.cmp[:].rearrange("p t a b -> p (t a b)").rearrange(
                "p (e c f) -> p e c f", e=E1, c=CH)
            work = sb("work", [P, 4 * DIM + 2 * KC * P + I1 + 2 * I1 + 2 * DIM])
            XD = work[:, 0:TILES * DIM].rearrange("p (t d) -> p t d", t=TILES)
            at = [0]

            def part(n):
                at[0] += n
                return work[:, at[0] - n:at[0]]

            XG = part(4 * DIM).rearrange("p (b d) -> p b d", b=4)
            XGT = part(2 * KC * P).rearrange("p (b d) -> p b d", b=2)
            H = part(I1)
            HT = part(2 * I1).rearrange("p (b c q) -> p b c q", b=2, c=CH)
            Y = part(2 * DIM).rearrange("p (b d) -> p b d", b=2)
            used, term = sb("used", [P, TOP1, E1]), sb("term", [P, TILES, E1])
            BT, BU, BH, BY = fx.PJ, fx.SB[0:2], fx.SB[2:4], fx.OB
            ld_s, ld_xd = sem("ld_s"), sem("ld_xd")
            ld_w = [sem(f"ld_w{e}") for e in range(E1)]
            weights_in = sem("weights_in")
            sent = sem("sent")
            ld_x = [sem(f"ld_x{b}") for b in range(4)]
            z_gelu, z_parts, z_full = sem("z_gelu"), sem("z_parts"), sem("z_full")
            used_full = sem("used_full")
            t_full, t_used = sem("t_full"), sem("t_used")
            u_full, h_done = sem("u_full"), sem("h_done")
            ht_full, ht_used = sem("ht_full"), sem("ht_used")
            y_full, y_used = sem("y_full"), sem("y_used")
            stored = [sem(f"stored{b}") for b in range(2)]

            with nc.Block() as block:
                @block.sync
                def _(sp):
                    for b in range(2):
                        sp.sem_inc(stored[b], 16)
                    for dst, src in ((b1T, io["b1T"]), (eye, io["eye"])):
                        sp.dma_start(dst[:], src).then_inc(ld_s, 16)
                    sp.dma_start(b2[0:E2, :], io["b2"]).then_inc(ld_s, 16)
                    sp.dma_start(XD, fx.xs1[0:TOKENS, :].rearrange("(t p) d -> p t d", p=P)).then_inc(ld_xd, 16)
                    for e in range(E1):
                        sp.dma_start(w2[:, e], io["m1_w2"][:, e]).then_inc(ld_w[e], 16)
                        sp.dma_start(w1[:, :, e, :], io["m1_w1"][:, :, e, :]).then_inc(ld_w[e], 16)
                        sp.dma_start(b1[:, e, :], io["b1"][:, e, :]).then_inc(ld_w[e], 16)
                    sp.wait_ge(sent, 16 * TILES * TOP1)

                    def load(j, b):
                        sp.wait_ge(t_full, j + 1)
                        sp.dma_start(XG[:, b, :], fx.xs1[bass.ds(TOKENS + j * P, P), :]).then_inc(ld_x[b], 16)

                    for j in range(4):
                        load(j, j)

                    def step(j, b, ahead):
                        if ahead is None:
                            load(j + 4, b)
                        sp.wait_ge(y_used, j + 1)
                        sp.dma_start(fx.ys1[bass.ds(j * P, P), :], Y[:, b % 2, :]).then_inc(stored[b % 2], 16)

                    tile_pipeline(sp, step, NS, 0, None)
                    for b in range(2):
                        sp.wait_ge(stored[b], 16 + 8 * NS)

                @block.gpsimd
                def _(pool):
                    pool.wait_ge(ld_xd, 16)
                    pool.wait_ge(fx.slots_zeroed1, 16)
                    pool.wait_ge(r.placed, 1)
                    for t in range(TILES):
                        for k in range(TOP1):
                            pool.indirect_dma_start(
                                out=fx.xs1, out_offset=bass.IndirectOffsetOnAxis(ap=r.row[:, t, k:k + 1], axis=0),
                                in_=XD[:, t, :], in_offset=None).then_inc(sent, 16)
                    for e in range(E1):
                        pool.wait_ge(ld_w[e], 48)
                        pool.sem_inc(weights_in, 1)

                @block.scalar
                def _(act):
                    r.on_act(nc, act)
                    act.wait_ge(ld_s, 48)
                    nc.scalar.activation(b1T[:], b1T[:], ACT.Gelu).then_inc(z_gelu, 1)

                    def rows(j, b):
                        act.wait_ge(t_full, j + 5)
                        nc.scalar.activation(XGT[:, b % 2, :], BT[b % 2][:, 0:KC * P], ACT.Copy).then_inc(t_used, 1)

                    def step(j, b, ahead):
                        if ahead is None or ahead >= 2:
                            rows(j + 2, b)
                        for i in range(2):
                            act.wait_ge(ht_full, 2 * j + i + 1)
                            nc.scalar.activation(HT[:, b % 2, i * HC:(i + 1) * HC, :].rearrange("p c q -> p (c q)"),
                                                 BH[i][:], ACT.Gelu).then_inc(ht_used, 1)

                    rows(0, 0)
                    rows(1, 1)
                    tile_pipeline(act, step, NS, 0, None)

                @block.vector
                def _(dve):
                    dve.wait_ge(ld_s, 48)
                    r.on_dve(nc, dve, fx.LG1[:], fx.tri16[:], fx.thresholds[:], fx.tile_row[:], BH[0], BH[1])
                    do = r.steps
                    dve.wait_ge(z_gelu, 1)
                    nc.vector.tensor_tensor(GB, b1T[:].unsqueeze(3).broadcast_to([P, E1, CH, E2]),
                                            eye[:].unsqueeze(2).broadcast_to([P, E1, CH, E2]),
                                            ALU.mult).then_inc(z_parts, 1)
                    dve.wait_ge(used_full, 1)
                    do(dve, nc.vector.tensor_reduce(
                        used[:], BU[1][:, 0:TOP1 * TILES * E1].rearrange("p (k t e) -> p k e t", k=TOP1, t=TILES), AX,
                        ALU.max))
                    do(dve, nc.vector.tensor_scalar(used[:], used[:], 0.0, None, ALU.is_gt))
                    for k in range(TOP1):
                        weight = r.wt[:, :, k].unsqueeze(2).broadcast_to([P, TILES, E1])
                        for lo, x, op in ((0, used[:, k].unsqueeze(1).broadcast_to([P, TILES, E1]), ALU.add),
                                          (E1, r.hot[:, k], ALU.subtract)):
                            out = AC[:, :, lo:lo + E1]
                            if k == 0 and op == ALU.add:
                                do(dve, nc.vector.tensor_tensor(out, x, weight, ALU.mult))
                                continue
                            do(dve, nc.vector.tensor_tensor(term[:], x, weight, ALU.mult))
                            if k == 0:
                                do(dve, nc.vector.tensor_scalar(out, term[:], -1.0, None, ALU.mult))
                            else:
                                do(dve, nc.vector.tensor_tensor(out, out, term[:], op))

                    def expert(j):
                        return dve.value_load(r.texp[0:1, bass.ds(j, 1)], min_val=0, max_val=E1 - 1)

                    def bias(j, b):
                        e = expert(j)
                        for i in range(2):
                            dve.wait_ge(u_full, 2 * j + i + 1)
                            nc.vector.tensor_tensor(H[:, i * HALF:(i + 1) * HALF].unsqueeze(1), BU[i][:].unsqueeze(1),
                                                    b1[:, bass.ds(e, 1), i * HALF:(i + 1) * HALF],
                                                    ALU.add).then_inc(h_done, 1)

                    def step(j, b, ahead):
                        if ahead is None or ahead >= 1:
                            bias(j + 1, b + 1)
                        dve.wait_ge(y_full, j + 1)
                        dve.wait_ge(stored[b % 2], 8 * (j + (2 - b % 2)))
                        nc.vector.tensor_copy(Y[:, b % 2, :], BY[b % 2][:, 0:DIM]).then_inc(y_used, 1)

                    dve.wait_ge(z_full, 1)
                    nc.vector.tensor_tensor(ZB[0:E2, :], BY[1][0:E2, 0:DIM], b2[0:E2, :], ALU.add).then_inc(z_done, 1)
                    bias(0, 0)
                    tile_pipeline(dve, step, NS, 0, None)

                @block.tensor
                def _(pe):
                    pe.sem_inc(t_full, 4)
                    r.on_pe(nc, pe, fx.before, fx.ones, BH[0], BH[1])
                    pe.wait_ge(r.steps.sem, r.hot_step)
                    nc.tensor.matmul(BU[1][:, 0:TOP1 * TILES * E1], fx.ones[:], r.hot[:].rearrange("p k t e -> p (k t e)"),
                                     start=True, stop=True).then_inc(used_full, 1)
                    pe.wait_ge(z_parts, 1)
                    for e in range(E1):
                        pe.wait_ge(ld_w[e], 48)
                        for c in range(CH):
                            last = nc.tensor.matmul(BY[1][0:E2, 0:DIM], GB[:, e, c, :], w2[:, e, c, :],
                                                    start=e == 0 and c == 0, stop=e == E1 - 1 and c == CH - 1)
                    last.then_inc(z_full, 1)
                    pe.wait_ge(z_done, 1)
                    pe.wait_ge(r.placed, 1)

                    def expert(j):
                        return pe.value_load(r.texp[0:1, bass.ds(j, 1)], min_val=0, max_val=E1 - 1)

                    def rows(j, b):
                        pe.wait_ge(ld_x[b], 4 * (j - b) + 16)
                        for m in range(KC):
                            last = nc.tensor.transpose(BT[b % 2][:, m * P:(m + 1) * P],
                                                       XG[:, b, m * P:(m + 1) * P], fx.ident[:])
                        last.then_inc(t_full, 1)

                    def up(j, b):
                        e = expert(j)
                        pe.wait_ge(t_used, j + 1)
                        for i in range(2):
                            for m in range(KC):
                                last = nc.tensor.matmul(BU[i][:], XGT[:, b % 2, m * P:(m + 1) * P],
                                                        w1[:, m, bass.ds(e, 1), i * HALF:(i + 1) * HALF],
                                                        start=m == 0, stop=m == KC - 1)
                            last.then_inc(u_full, 1)

                    def step(j, b, ahead):
                        if ahead is None or ahead >= 2:
                            rows(j + 2, (b + 2) % 4)
                        for i in range(2):
                            pe.wait_ge(h_done, 2 * j + i + 1)
                            for c in range(HC):
                                lo = (i * HC + c) * P
                                last = nc.tensor.transpose(BH[i][:, c * P:(c + 1) * P], H[:, lo:lo + P], fx.ident[:])
                            last.then_inc(ht_full, 1)
                        if ahead is None or ahead >= 1:
                            up(j + 1, b + 1)
                        e = expert(j)
                        for i in range(2):
                            pe.wait_ge(ht_used, 2 * j + i + 1)
                            for c in range(i * HC, (i + 1) * HC):
                                last = nc.tensor.matmul(BY[b % 2][:, 0:DIM], HT[:, b % 2, c, :],
                                                        w2[:, bass.ds(e, 1), c, :], start=c == 0, stop=c == CH - 1)
                        last.then_inc(y_full, 1)

                    rows(0, 0)
                    rows(1, 1)
                    up(0, 0)
                    tile_pipeline(pe, step, NS, 0, None)

        def ev(name, per, primed=False, step=1):
            return Event(es, nc, "fin_" + name, per, primed, step)

        gathered = [sem(f"gathered{b}") for b in range(2)]
        spread = ev("spread", 1)
        ac_full, ac_used = ev("ac_full", 1), ev("ac_used", 1)
        rest_full = ev("rest_full", 1)
        rest_used = ev("rest_used", 1)
        measured, root, normed = ev("measured", 1), ev("root", 1), ev("normed", 1)
        written = [ev(f"written{b}", 1, True, 16) for b in range(2)]
        chain = Chain(es, nc, "fin_chain", TOP1 + 2)
        with ExitStack() as mem:
            def sb(name, shape):
                return mem.enter_context(nc.sbuf_tensor("fin_" + name, shape, F32))

            XD = sb("XD", [P, TILES, DIM])
            ld_xd = sem("ld_x_again")
            GA = sb("GA", [P, TILES, TOP1, DIM])
            X, ACG, ACT_T = sb("X", [P, 2, TG, DIM]), sb("ACG", [P, 2, TG, E2]), sb("ACT_T", [P, 2, GTOK])
            st, mv, rs = sb("st", [P, TG, 6]), sb("mv", [P, TG, 2]), sb("rs", [P, 2, TG])

            def groups(engine, body):
                with engine.Fori(0, GROUPS // 2) as i:
                    for b in range(2):
                        body(i, b, i * 2 + b)

            with nc.Block() as block:
                @block.gpsimd
                def _(pool):
                    for g in range(GROUPS):
                        if g >= 2:
                            pool.wait_ge(gathered[g % 2], 16 * TG * TOP1 * (g // 2))
                        for t in range(g * TG, (g + 1) * TG):
                            for k in range(TOP1):
                                pool.indirect_dma_start(
                                    out=GA[:, t, k, :], out_offset=None, in_=fx.ys1,
                                    in_offset=bass.IndirectOffsetOnAxis(ap=fx.pos1[:, t, k:k + 1], axis=0),
                                ).then_inc(gathered[g % 2], 16)

                @block.sync
                def _(sp):
                    sp.dma_start(XD[:], fx.xs1[0:TOKENS, :].rearrange("(t p) d -> p t d", p=P)).then_inc(ld_xd, 16)
                    for b in range(2):
                        written[b].prime(sp)

                    def write(i, b, g):
                        sp.wait_ge(normed.sem, normed.at(g, 0))
                        sp.dma_start(io["out"][bass.ds(g * GTOK, GTOK), :].rearrange("(t p) d -> p t d", p=P),
                                     X[:, b]).then_inc(written[b].sem, 16)

                    groups(sp, write)
                    for b in range(2):
                        sp.wait_ge(written[b].sem, 16 * (GROUPS // 2 + 1))

                @block.scalar
                def _(act):
                    def body(i, b, g):
                        act.wait_ge(ac_full.sem, ac_full.at(g, 0))
                        nc.scalar.activation(ACT_T[0:E2, b, :], fx.PJ[b][0:E2, :], ACT.Copy).then_inc(ac_used.sem, 1)
                        act.wait_ge(measured.sem, measured.at(g, 0))
                        nc.scalar.activation(rs[:, b, :], mv[:, :, 1], ACT.Sqrt,
                                             bias=fx.epsln[:, 0:1]).then_inc(root.sem, 1)

                    groups(act, body)

                @block.vector
                def _(dve):
                    def body(i, b, g):
                        chain.k = 0
                        nc.vector.tensor_scalar(ACG[:, b], AC[:, bass.ds(g * TG, TG), :], 1.0, None,
                                                ALU.mult).then_inc(spread.sem, 1)
                        dve.wait_ge(written[b].sem, written[b].at(i, -1))
                        dve.wait_ge(rest_full.sem, rest_full.at(g, 0))
                        for h in range(2):
                            last = nc.vector.tensor_tensor(X[:, b, 2 * h:2 * h + 2, :],
                                                           fx.SB[2 * b + h][:].rearrange("p (t d) -> p t d", t=2),
                                                           XD[:, bass.ds(g * TG + 2 * h, 2), :], ALU.add)
                        last.then_inc(rest_used.sem, 1)
                        dve.wait_ge(rest_used.sem, rest_used.at(g, 0))
                        dve.wait_ge(gathered[b], i * (16 * TG * TOP1) + 16 * TG * TOP1)
                        for k in range(TOP1):
                            for t in range(TG):
                                last = nc.vector.scalar_tensor_tensor(
                                    out=X[:, b, t:t + 1, :], in0=GA[:, bass.ds(g * TG + t, 1), k, :],
                                    scalar=fx.wt1[:, bass.ds(g * TG + t, 1), k], in1=X[:, b, t:t + 1, :],
                                    op0=ALU.mult, op1=ALU.add)
                            chain.link(dve, g, last)
                        for t in range(TG):
                            last = nc.vector.bn_stats(st[:, t, :], X[:, b, t, :])
                        chain.link(dve, g, last)
                        settle(dve, fx.dve_passed)
                        for t in range(TG):
                            last = nc.vector.bn_aggr(mv[:, t, :], st[:, t, :])
                        last.then_inc(measured.sem, 1)
                        dve.wait_ge(root.sem, root.at(g, 0))
                        chain.link(dve, g, nc.vector.reciprocal(rs[:, b, :], rs[:, b, :]))
                        for t in range(TG):
                            x = X[:, b, t, :]
                            last = nc.vector.tensor_scalar(x, x, mv[:, t, 0:1], rs[:, b, t:t + 1], ALU.subtract, ALU.mult)
                        last.then_inc(normed.sem, 1)
                        chain.close()

                    dve.wait_ge(ld_xd, 16)
                    groups(dve, body)

                @block.tensor
                def _(pe):
                    def body(i, b, g):
                        pe.wait_ge(spread.sem, spread.at(g, 0))
                        for t in range(TG):
                            last = nc.tensor.transpose(fx.PJ[b][0:E2, t * P:(t + 1) * P], ACG[:, b, t, :], fx.ident[:])
                        last.then_inc(ac_full.sem, 1)
                        pe.wait_ge(ac_used.sem, ac_used.at(g, 0))
                        for t in range(TG):
                            last = nc.tensor.matmul(fx.SB[2 * b + t // 2][:, t % 2 * DIM:(t % 2 + 1) * DIM],
                                                    ACT_T[0:E2, b, t * P:(t + 1) * P], ZB[0:E2, :], start=True, stop=True)
                        last.then_inc(rest_full.sem, 1)

                    groups(pe, body)


class Fixed:
    pass


def decoder(nc, io):
    es = ExitStack()
    with es:
        fx = Fixed()

        def sb(name, shape):
            return es.enter_context(nc.sbuf_tensor(name, shape, F32))

        banks = [es.enter_context(nc.psum_tensor(f"bank{i}", [P, 512], F32)) for i in range(8)]
        fx.PJ, fx.SB, fx.OB = banks[0:2], banks[2:6], banks[6:8]
        fx.ident, fx.ones = sb("ident", [P, P]), sb("ones", [P, P])
        fx.cmask = sb("cmask", [P, SEQ])
        fx.cneg = sb("cneg", [P, SEQ])
        fx.hm16 = sb("hm16", [P, 8])
        fx.hm8 = sb("hm8", [P, 16])
        fx.neghalf, fx.epsln, fx.epsrms = sb("neghalf", [P, 1]), sb("epsln", [P, 1]), sb("epsrms", [P, 1])
        fx.NS0 = -(-((TOKENS * TOP0 + E0 * (P - 1)) // P) // 4) * 4
        fx.NS1 = -(-((TOKENS * TOP1 + E1 * (P - 1)) // P) // 4) * 4
        rows = SHARED * TOKENS + fx.NS0 * P
        fx.xs, fx.ys = (nc.dram_tensor(n, (rows, DIM), F32).ap() for n in ("xs", "ys"))
        fx.xs1, fx.ys1 = (nc.dram_tensor(n, (rows, DIM), F32).ap() for n, rows in
                          (("xs1", TOKENS + fx.NS1 * P), ("ys1", fx.NS1 * P)))
        fx.tri16 = sb("tri16", [P, E0, E0])
        fx.before = sb("before", [P, P])
        fx.thresholds = sb("thresholds", [P, TILES])
        fx.tile_row = sb("tile_row", [P, fx.NS0])
        fx.zeros = sb("zeros", [P, DIM])
        fx.slots_zeroed = es.enter_context(nc.semaphore("slots_zeroed"))
        fx.slots_zeroed1 = es.enter_context(nc.semaphore("slots_zeroed1"))
        fx.LG, fx.LG1 = sb("LG", [P, TILES, E0]), sb("LG1", [P, TILES, E1])
        (fx.pos0, fx.wt0), (fx.pos1, fx.wt1) = (
            (es.enter_context(nc.sbuf_tensor(n + "pos", [P, TILES, k], U32)), sb(n + "wt", [P, TILES, k]))
            for n, k in (("r0_", TOP0), ("r1_", TOP1)))
        fx.ready = es.enter_context(nc.semaphore("constants"))
        fx.READY = 14 * 16
        fx.dve_passed, fx.pool_passed = (es.enter_context(nc.semaphore(n)) for n in ("dve_passed", "pool_passed"))
        with nc.Block() as block:
            @block.scalar
            def _(act):
                for dst, src in ((fx.ident, io["ident"]), (fx.ones, io["ones"]), (fx.cmask, io["cmask"]), (fx.cneg, io["cneg"]),
                                 (fx.hm16, io["hm16"]), (fx.hm8, io["hm8"]), (fx.neghalf, io["neghalf"]),
                                 (fx.epsln, io["epsln"]), (fx.epsrms, io["epsrms"]), (fx.tri16, io["tri16"]), (fx.before, io["before"]),
                                 (fx.thresholds, io["thresholds"]), (fx.tile_row, io["tile_row"]), (fx.zeros, io["zeros"])):
                    act.dma_start(dst[:], src).then_inc(fx.ready, 16)
                act.wait_ge(fx.ready, fx.READY)
                for dst, done, n in ((fx.xs[SHARED * TOKENS:, :], fx.slots_zeroed, fx.NS0),
                                     (fx.xs1[TOKENS:, :], fx.slots_zeroed1, fx.NS1)):
                    act.dma_start(dst.rearrange("(n p) d -> p n d", p=P),
                                  fx.zeros[:].unsqueeze(1).broadcast_to([P, n, DIM])).then_inc(done, 16)
        layer0(nc, es, io, fx)
        moe0(nc, es, io, fx)
        layer1(nc, es, io, fx)
        moe1(nc, es, io, fx)


def layouts(a):
    f = np.float32
    ar = {}
    x, c = a["x"].reshape(TOKENS, DIM), a["ctx_2048"].reshape(TOKENS, DIM)
    ar["x"], ar["xT"], ar["cT"] = x, x.T, c.T
    ar["la_wq"], ar["la_wk"], ar["la_wv"] = a["L0_attn_Wq"], a["L0_attn_Wk"], a["L0_attn_Wv"].T
    ar["la_wo"] = a["L0_attn_Wo"].T.reshape(8, 2, 16, DIM).transpose(1, 0, 2, 3).reshape(DIM, DIM)
    ar["gb"] = np.stack([np.tile(a["L0_attn_gamma"], 8), np.tile(a["L0_attn_beta"], 8)], 1)
    ar["xa_wq"], ar["xa_wk"], ar["xa_wo"] = a["L0_xattn_q_w"].T, a["L0_xattn_k_img_w"].T, a["L0_xattn_o_w"].T
    ar["xa_wv"] = a["L0_xattn_v_img_w"].T.reshape(DIM, 8, 2, 16).transpose(0, 2, 1, 3).reshape(DIM, DIM)
    vb = a["L0_xattn_v_img_b"].reshape(8, 2, 16).transpose(1, 0, 2).reshape(2, 1, P)
    ar["vb"] = np.tile(vb, (1, SEQ, 1)).reshape(P, P)
    for n, k in (("qb", "q_b"), ("kb", "k_img_b"), ("ob", "o_b"), ("nq", "norm_q_w"), ("nk", "norm_k_img_w")):
        ar[n] = np.tile(a["L0_xattn_" + k][None, :], (P, 1))
    ar["wg"] = a["L0_ffn_Wg"].T
    p, q = np.arange(P)[:, None], np.arange(SEQ)[None, :]
    ar["ident"], ar["ones"] = np.eye(P, dtype=f), np.ones((P, P), f)
    ar["cmask"] = (p % SEQ <= q).astype(f)
    ar["cneg"] = np.where(q <= p % SEQ, f(0), f(NEG)).astype(f)
    ar["hm16"] = (p // 16 == np.arange(8)).astype(f)
    ar["hm8"] = (p // 8 == np.arange(16)).astype(f)
    ar["neghalf"], ar["epsln"], ar["epsrms"] = (np.full((P, 1), v, f) for v in (-0.5, EPS_LN, EPS_RMS))
    e = np.arange(E0)
    ar["tri16"] = np.tile((e[None, :] < e[:, None]).astype(f), (P, 1, 1))
    t = np.arange(P)
    ar["before"] = (t[:, None] < t[None, :]).astype(f)
    ar["thresholds"] = np.tile(np.arange(TILES, dtype=f) * P, (P, 1))
    ar["tile_row"] = np.tile(np.arange(-(-((TOKENS * TOP0 + E0 * (P - 1)) // P) // 4) * 4, dtype=f), (P, 1))
    ar["zeros"] = np.zeros((P, DIM), f)
    ar["sa_wq"], ar["sa_wv"], ar["sa_wo"] = a["L1_attn_Wq"], a["L1_attn_Wv"], a["L1_attn_Wo"]
    ar["sa_wk"] = np.repeat(a["L1_attn_Wk"].reshape(DIM, 4, 1, 16), 4, 2).reshape(DIM, DIM)
    kv = np.concatenate([a["L1_xattn_Wk"], a["L1_xattn_Wv"]])
    ar["xb_wq"], ar["xb_wkv"] = a["L1_xattn_Wq"].T, np.concatenate([kv[0::2], kv[1::2]]).T
    ar["rw1"], ar["rw2"] = a["L1_ffn_rw1"], a["L1_ffn_rw2"]
    both = [np.concatenate([a["L0_ffn_" + n], a["L0_ffn_" + m].reshape(SHARED, I0, DIM)]) for n, m in
            (("W1", "Ws1"), ("W3", "Ws3"))]
    w13 = np.concatenate(both, 1)
    ar["w13"] = w13.transpose(2, 0, 1).reshape(KC, P, EALL, 2 * I0)
    w2 = np.concatenate([a["L0_ffn_W2"], a["L0_ffn_Ws2"].reshape(DIM, SHARED, I0).transpose(1, 0, 2)])
    ar["w2"] = w2.transpose(2, 0, 1)
    ar["m1_w1"] = a["L1_ffn_w1"].reshape(E1, KC, P, I1).transpose(2, 1, 0, 3)
    ar["m1_w2"] = a["L1_ffn_w2"].reshape(E1, I1 // P, P, DIM).transpose(2, 0, 1, 3)
    ar["b1"] = np.tile(a["L1_ffn_b1"][None], (P, 1, 1))
    ar["b1T"] = a["L1_ffn_b1"].reshape(E1, I1 // P, P).transpose(2, 0, 1)
    ar["b2"] = np.concatenate([a["L1_ffn_b2"], np.zeros((E1, DIM), f)])
    ar["eye"] = np.tile(np.concatenate([np.eye(E1, dtype=f)] * 2, 1), (P, 1, 1))
    ar["centre"] = (np.eye(P) - (p // 16 == np.arange(P) // 16) / 16).astype(f)
    return {k: np.ascontiguousarray(v) for k, v in ar.items()}


def kernel(**inputs):
    import concourse.bacc as _bacc
    from concourse.bass_utils import run_bass_kernel_spmd as _run

    arrays = layouts({k: np.asarray(v) for k, v in inputs.items()})
    nc = _bacc.Bacc("TRN2", target_bir_lowering=False, num_devices=1)
    io = {}
    for name, v in arrays.items():
        io[name] = nc.dram_tensor("in_" + name, v.shape, mybir.dt.from_np(v.dtype), kind="ExternalInput").ap()
    io["out"] = nc.dram_tensor("out", (TOKENS, DIM), F32, kind="ExternalOutput").ap()
    decoder(nc, io)
    r = _run(nc, [{"in_" + k: v for k, v in arrays.items()}], core_ids=[0])
    return r.results[0]["out"].reshape(BATCH, SEQ, DIM)
```

```python
import concourse.bass as bass
from concourse import mybir
from contextlib import ExitStack
import numpy as np

F32 = mybir.dt.float32
U32 = mybir.dt.uint32
ACT = mybir.ActivationFunctionType
ALU = mybir.AluOpType
AX = mybir.AxisListType.X

BATCH, SEQ, DIM = 32, 64, 256
TOKENS = BATCH * SEQ
P = 128
TILES = TOKENS // P
TG = 4
GROUPS = TILES // TG
GTOK = TG * P
KC = DIM // P
PER = P // SEQ
GSEQ = TG * PER
E0, I0, SHARED = 16, 176, 2
EALL = E0 + SHARED
NGRP, TOPG, TOP0 = 4, 2, 4
E1, I1, TOP1 = 8, 1024, 2
H16, D16 = 16, 16
H32, D32 = 32, 8
EPS_LN, EPS_RMS = 1e-5, 1e-6
NEG = -1.0e30


class Event:

    def __init__(self, es, nc, name, per, primed=False, step=1, continues=None):
        self.per, self.step, self.primed = per, step, primed
        if continues is None:
            self.sem, self.base = es.enter_context(nc.semaphore(name)), 0
        else:
            assert not primed and not continues.primed and not continues.base
            self.sem, self.base = continues.sem, GROUPS * continues.per * continues.step

    def prime(self, engine):
        engine.sem_inc(self.sem, self.per * self.step)

    def at(self, g, k):
        return g * (self.per * self.step) + (k + 1 + (self.per if self.primed else 0)) * self.step + self.base


class Chain:

    def __init__(self, es, nc, name, per):
        self.sem, self.per, self.k = es.enter_context(nc.semaphore(name)), per, 0

    def link(self, engine, g, instruction):
        self.k += 1
        instruction.then_inc(self.sem, 1)
        engine.wait_ge(self.sem, g * self.per + self.k)

    def close(self):
        assert self.k == self.per, (self.k, self.per)


class Steps:

    def __init__(self, sem, k=0):
        self.sem, self.k = sem, k

    def __call__(self, engine, instruction):
        self.k += 1
        instruction.then_inc(self.sem, 1)
        engine.wait_ge(self.sem, self.k)

    def link(self, engine, _, instruction):
        self(engine, instruction)


class Ring:

    def __init__(self, banks, full, emptied, uses):
        self.banks, self.full, self.emptied, self.uses = banks, full, emptied, uses
        self.at = {name: i for i, (name, _) in enumerate(uses)}
        self.next = 0
        assert len(uses) % 2 == 0 and len(self.at) == len(uses) == full.per

    def bank(self, name):
        return self.banks[self.at[name] % 2]

    def rank(self, i):
        return sum(e == self.uses[i][1] for _, e in self.uses[:i])

    def before_fill(self, pe, g, name):
        i = self.at[name]
        assert i == self.next, (name, i, self.next)
        self.next += 1
        e = self.emptied[self.uses[i - 2][1]]
        if i >= 2:
            pe.wait_ge(e.sem, e.at(g, self.rank(i - 2)))
        else:
            pe.wait_ge(e.sem, e.at(g, self.rank(len(self.uses) + i - 2) - e.per))

    def begin(self, name):
        self.next = self.at[name] if name else 0

    def skip(self, engine, count, g, first, end):
        a, b = self.at[first] if first else 0, self.at[end] if end else len(self.uses)
        before, n = (sum(count is self.full or self.emptied[e] is count for _, e in part)
                     for part in (self.uses[:a], self.uses[a:b]))
        if n == 0:
            return
        if a:
            engine.wait_ge(count.sem, count.at(g, before - 1))
        engine.sem_inc(count.sem, n)

    def wait_filled_before(self, engine, g, name):
        engine.wait_ge(self.full.sem, self.full.at(g, self.at[name] - self.full.per))

    def wait_emptied_before(self, engine, g, name):
        i = self.at[name]
        e = self.emptied[self.uses[i][1]]
        engine.wait_ge(e.sem, e.at(g, self.rank(i) - e.per))

    def wait_full(self, engine, g, name):
        engine.wait_ge(self.full.sem, self.full.at(g, self.at[name]))

    def wait_emptied(self, engine, g, name):
        i = self.at[name]
        e = self.emptied[self.uses[i][1]]
        engine.wait_ge(e.sem, e.at(g, self.rank(i)))


def settle(engine, passed):
    engine.sem_inc(passed, 1)


def heads(ap, h):
    return ap.rearrange("p (h d) -> p h d", h=h)


def staggered(*stages):
    last = max(lag for _, lag in stages)
    return [(name, step - lag) for step in range(TG + last) for name, lag in stages if 0 <= step - lag < TG]


class Core:

    def __init__(self, es, nc, x, h, d, keys_first, act_masks, continues=None):
        self.x, self.h, self.d, self.keys_first, self.act_masks = x, h, d, keys_first, act_masks
        self.nb = h // 8
        self.values_ahead = 0
        self.fillers = {}
        self.lag = 1 if keys_first else 2
        self.w = PER * (d + 1)

        self.events = {}

        def ev(name, per):
            self.events[name] = Event(es, nc, x + name, per, continues=continues and continues.events[name])
            return self.events[name]

        self.masked = ev("masked", self.nb)
        if act_masks:
            self.masked_act = ev("masked_act", self.nb)
        self.s_full = ev("s_full", TG * self.nb)
        self.s_used = ev("s_used", TG * self.nb)
        self.p_ready = ev("p_ready", TG * self.nb)
        if not keys_first:
            self.pt_full = ev("pt_full", TG * 2)
            self.pt_used = ev("pt_used", TG * 2)
        self.o_full = ev("o_full", TG)
        self.o_done = ev("o_done", TG)

    def names(self):
        out = []
        for s in range(TG + self.lag + 2):
            out += self.fillers.get(s, [])
            out += [(self.x + n, s - self.lag - k) for n, k in (("otr", 1), ("out", 2)) if 0 <= s - self.lag - k < TG]
        return out


def core_pe(nc, pe, g, c, ring, still, masked, S, OB, weights, turned, values, O, OT, ident, out_product,
            fill=None):
    hc = c.h // KC
    for step in range(TG + c.lag + 2):
        if step < TG:
            t = step
            for b in range(c.nb):
                u = t * c.nb + b
                if t == 0:
                    pe.wait_ge(c.masked.sem, c.masked.at(g, b))
                    if c.act_masks:
                        pe.wait_ge(c.masked_act.sem, c.masked_act.at(g, b))
                if u >= 4 and c.keys_first:
                    pe.wait_ge(c.s_used.sem, c.s_used.at(g, u - 4))
                if not c.keys_first and t >= 2 and b == 0:
                    pe.wait_ge(c.pt_used.sem, c.pt_used.at(g, 2 * (t - 2) + 1))
                m, lo = divmod(8 * b, hc)
                for s in range(PER):
                    last = nc.tensor.matmul(S[u % 4][s * SEQ:(s + 1) * SEQ, :],
                                            still[:, m, t * P + s * SEQ:t * P + (s + 1) * SEQ],
                                            masked[:, m, t * PER + s, lo:lo + 8, :], start=True, stop=True)
                last.then_inc(c.s_full.sem, 1)
        for name in c.fillers.get(step, []):
            fill(*name)
        if not c.keys_first and 0 <= step - 1 < TG:
            t = step - 1
            for b in range(2):
                pe.wait_ge(c.p_ready.sem, c.p_ready.at(g, 2 * t + b))
                for j in range(4):
                    last = nc.tensor.transpose(S[(2 * t + b) % 4][:, j * P:(j + 1) * P],
                                               weights[:, t % 2, 8 * b + 2 * j:8 * b + 2 * j + 2, :], ident[:])
                last.then_inc(c.pt_full.sem, 1)
        if 0 <= step - c.lag < TG:
            t = step - c.lag
            o = OB[t % 2]
            if t >= 2:
                pe.wait_ge(c.o_done.sem, c.o_done.at(g, t - 2))
            if c.keys_first:
                pe.wait_ge(c.p_ready.sem, c.p_ready.at(g, c.nb * t + c.nb - 1))
                ring.wait_emptied(pe, g - c.values_ahead, (c.x + "v", t))
                for h in range(c.h):
                    j, a = divmod(h, 2)
                    last = nc.tensor.matmul(o[a * SEQ:(a + 1) * SEQ, j * c.w:(j + 1) * c.w],
                                            weights[:, t % 2, h, :], values[:, t, h, :], start=True, stop=True)
            else:
                pe.wait_ge(c.pt_used.sem, c.pt_used.at(g, 2 * t + 1))
                ring.wait_emptied(pe, g - c.values_ahead, (c.x + "v", t))
                for j in range(c.h // 2):
                    for s in range(PER):
                        last = nc.tensor.matmul(o[s * SEQ:(s + 1) * SEQ, j * c.w:(j + 1) * c.w],
                                                turned[:, t % 2, j, s * SEQ:(s + 1) * SEQ], values[:, t, s, j, :],
                                                start=True, stop=True)
            last.then_inc(c.o_full.sem, 1)
        if 0 <= step - c.lag - 1 < TG:
            t = step - c.lag - 1
            ring.before_fill(pe, g, (c.x + "otr", t))
            pe.wait_ge(c.o_done.sem, c.o_done.at(g, t))
            for m in range(KC):
                last = nc.tensor.transpose(ring.bank((c.x + "otr", t))[:, m * P:(m + 1) * P],
                                           O[:, t % 2, m * P:(m + 1) * P], ident[:])
            last.then_inc(ring.full.sem, 1)
        if 0 <= step - c.lag - 2 < TG:
            t = step - c.lag - 2
            ring.before_fill(pe, g, (c.x + "out", t))
            ring.wait_emptied(pe, g, (c.x + "otr", t))
            out_product(ring.bank((c.x + "out", t)), t).then_inc(ring.full.sem, 1)


def core_outputs(nc, dve, g, c, t, OB, O, den, chain, eps):
    dve.wait_ge(c.o_full.sem, c.o_full.at(g, t))
    n, w = c.h // 2, c.d + 1
    got = OB[t % 2][:, 0:n * 2 * w].rearrange("p (j s w) -> p j s w", j=n, s=2)
    sums = den[:, t, 0:2 * n].rearrange("p (j s) -> p j s", s=2)
    if eps:
        chain.link(dve, g, nc.vector.tensor_scalar(sums, got[:, :, :, c.d], eps, None, ALU.add))
        chain.link(dve, g, nc.vector.reciprocal(sums, sums))
    else:
        chain.link(dve, g, nc.vector.reciprocal(sums, got[:, :, :, c.d]))
    if c.keys_first:
        to = O[:, t % 2, :].rearrange("p (s j d) -> p j s d", s=2, d=c.d)
    else:
        to = O[:, t % 2, :].rearrange("p (j s d) -> p j s d", s=2, d=c.d)
    nc.vector.tensor_tensor(to, got[:, :, :, 0:c.d], sums.unsqueeze(3).broadcast_to([P, n, 2, c.d]),
                            ALU.mult).then_inc(c.o_done.sem, 1)


def core_turned_output(nc, act, g, c, t, ring, OT):
    name = (c.x + "otr", t)
    ring.wait_full(act, g, name)
    src = ring.bank(name)[:, 0:KC * P]
    if c.keys_first:
        src = src.rearrange("p (s a q) -> p a s q", s=PER, a=2)
        dst = OT[:, :, t * P:(t + 1) * P].rearrange("p a (s q) -> p a s q", s=PER)
    else:
        src = src.rearrange("p (m q) -> p m q", m=KC)
        dst = OT[:, :, t * P:(t + 1) * P]
    nc.scalar.activation(dst, src, ACT.Copy).then_inc(ring.emptied["A"].sem, 1)


DVE_MASKS = 5


def mask_bank(nc, act, dst, src, hm, c, b, which):
    m, lo = divmod(8 * b, c.h // KC)
    for h in which:
        to, x, mask = dst[:, m, :, lo + h, :], src[:, m, :].rearrange("p (s q) -> p s q", s=GSEQ), hm[:, lo + h:lo + h + 1]
        if act:
            last = nc.scalar.activation(to, x, ACT.Copy, scale=mask)
        else:
            last = nc.vector.tensor_scalar(to, x, mask, None, ALU.mult)
    return last


def masks_dve(nc, g, dst, src, hm, c):
    for b in range(c.nb):
        mask_bank(nc, False, dst, src, hm, c, b, range(DVE_MASKS)).then_inc(c.masked.sem, 1)


def masks_act(nc, act, g, ring, last_turned, dst, src, hm, c):
    ring.wait_emptied(act, g, last_turned)
    for b in range(c.nb):
        mask_bank(nc, True, dst, src, hm, c, b, range(DVE_MASKS, 8)).then_inc(c.masked_act.sem, 1)


class Norm:

    def __init__(self, es, nc, fx, x, continues=None):
        self.fx = fx

        self.events = {}

        def ev(name):
            self.events[name] = Event(es, nc, f"{x}{name}", TG, continues=continues and continues.events[name])
            return self.events[name]

        self.stats = ev("stats")
        self.rstd = ev("rstd")
        self.done = ev("done")

    def moments(self, nc, dve, g, t, x, st, mv, chain):
        chain.link(dve, g, nc.vector.bn_stats(st[:, t, :], x))
        settle(dve, self.fx.dve_passed)
        nc.vector.bn_aggr(mv[:, t, :], st[:, t, :]).then_inc(self.stats.sem, 1)

    def root(self, nc, pool, g, t, mv, rs, neghalf, chain, of=0):
        pool.wait_ge(self.stats.sem, self.stats.at(g + of, t))
        settle(pool, self.fx.pool_passed)
        chain.link(pool, g, nc.gpsimd.tensor_scalar(rs[:, t:t + 1], mv[:, t, 1:2], EPS_LN, None, ALU.add))
        nc.gpsimd.tensor_tensor(rs[:, t:t + 1], rs[:, t:t + 1], neghalf[:, 0:1], ALU.pow).then_inc(self.rstd.sem, 1)

    def apply(self, nc, dve, g, t, x, mv, rs):
        dve.wait_ge(self.rstd.sem, self.rstd.at(g, t))
        nc.vector.tensor_scalar(x, x, mv[:, t, 0:1], rs[:, t:t + 1], ALU.subtract,
                                ALU.mult).then_inc(self.done.sem, 1)


def softmax_scores(nc, dve, g, c, t, S, W, mx, chain, cneg):
    for b in range(2):
        u = 2 * t + b
        dve.wait_ge(c.s_full.sem, c.s_full.at(g, u))
        src, dst = heads(S[u % 4][:], 8), W[:, t % 2, 8 * b:8 * b + 8, :]
        top = mx[:, t, 8 * b:8 * b + 8]
        if cneg is not None:
            chain.link(dve, g, nc.vector.tensor_tensor(dst, src, cneg[:].unsqueeze(1).broadcast_to([P, 8, SEQ]),
                                                       ALU.add))
            src = dst
        chain.link(dve, g, nc.vector.tensor_reduce(top, src, AX, ALU.max))
        nc.vector.tensor_tensor(dst, src, top.unsqueeze(2).broadcast_to([P, 8, SEQ]),
                                ALU.subtract).then_inc(c.s_used.sem, 1)


def softmax_act(nc, act, g, c, ring, S, W, WT, OT, scale, empty=None):
    for step in range(TG + c.lag + 1):
        if step < TG:
            for b in range(2):
                act.wait_ge(c.s_used.sem, c.s_used.at(g, 2 * step + b))
                part = W[:, step % 2, 8 * b:8 * b + 8, :]
                nc.scalar.activation(part, part, ACT.Exp, scale=scale).then_inc(c.p_ready.sem, 1)
        for name in c.fillers.get(step, []):
            empty(*name)
        if 0 <= step - 1 < TG:
            for b in range(2):
                u = 2 * (step - 1) + b
                act.wait_ge(c.pt_full.sem, c.pt_full.at(g, u))
                nc.scalar.activation(WT[:, (step - 1) % 2, 4 * b:4 * b + 4, :],
                                     S[u % 4][:].rearrange("p (j q) -> p j q", j=4),
                                     ACT.Copy).then_inc(c.pt_used.sem, 1)
        if 0 <= step - c.lag - 1 < TG:
            core_turned_output(nc, act, g, c, step - c.lag - 1, ring, OT)


def turned(nc, act, g, ring, name, dst, n):
    ring.wait_full(act, g, name)
    nc.scalar.activation(dst, ring.bank(name)[:, 0:n * P].rearrange("p (m q) -> p m q", m=n),
                         ACT.Copy).then_inc(ring.emptied["A"].sem, 1)


def turn(nc, pe, g, ring, name, sources, ident):
    for m, src in enumerate(sources):
        last = nc.tensor.transpose(ring.bank(name)[:, m * P:(m + 1) * P], src, ident[:])
    last.then_inc(ring.full.sem, 1)


def product(nc, dst, stills, movings):
    n = len(stills)
    for i in range(n):
        last = nc.tensor.matmul(dst, stills[i], movings[i], start=i == 0, stop=i == n - 1)
    return last


def chunks(x, t):
    return [x[:, m, t * P:(t + 1) * P] for m in range(KC)]


def layer0(nc, es, io, fx):
    PJ, SB, OB = fx.PJ, fx.SB, fx.OB
    la = Core(es, nc, "la_", H16, D16, True, True)
    xa = Core(es, nc, "xa_", H16, D16, False, True)
    xq_steps = staggered(("xa_xtr", 0), ("xa_q", 1), ("xa_trq", 3))
    fx.linear_core, fx.softmax_core = la, xa
    PAIRS = TG // 2
    eng = {"xa_xtr": "A", "xa_q": "D", "xa_trq": "A", "r_xtr": "A", "r_logit": "D"}
    la.values_ahead = 1
    la.fillers = {step: [(n, t), (n, t + 1)] for step, n, t in (
        (0, "xa_v", 0), (1, "xa_v", 2), (2, "xa_trk", 0), (3, "xa_trk", 2))}
    uses = []
    core_eng = {"xa_k": "D", "xa_v": "D", "xa_trk": "A", "la_otr": "A", "la_out": "D", "xa_otr": "A", "xa_out": "D"}
    uses += [(n, core_eng[n[0]]) for n in la.names()] + [((n, t), eng[n]) for n, t in xq_steps]
    uses += [(n, core_eng[n[0]]) for n in xa.names()]
    ahead = [((n, t), e) for n, e in (("la_qk", "D"), ("xa_k", "D"), ("la_v", "A")) for t in range(TG)]
    uses += ahead + [(("r_xtr", i), "A") for i in range(PAIRS)] + [(("la_tr", t), "A") for t in range(TG)]
    uses += [(("r_logit", i), "D") for i in range(PAIRS)]
    AHEAD, ROUTER, TURN, LOGITS = ahead[0][0], ("r_xtr", 0), ("la_tr", 0), ("r_logit", 0)

    def ev(name, per, primed=False, step=1):
        return Event(es, nc, "l0_" + name, per, primed, step)

    full = ev("full", len(uses), True)
    emptied = {k: ev("emptied" + k, sum(e == k for _, e in uses), True) for k in "AD"}
    ring = Ring(PJ, full, emptied, uses)
    fold = es.enter_context(nc.semaphore("l0_fold"))
    folded = es.enter_context(nc.semaphore("l0_folded"))
    zeroed = es.enter_context(nc.semaphore("l0_zeroed"))
    ld_w = es.enter_context(nc.semaphore("l0_ld_w"))
    ld_n = es.enter_context(nc.semaphore("l0_ld_n"))
    ld_x, ld_xt, ld_c = ev("ld_x", 1, step=16), ev("ld_xt", 1, step=16), ev("ld_c", 1, step=16)
    sq = ev("sq", TG)
    ss = ev("ss", 1)
    root = ev("root", 1)
    qn = ev("qn", TG)
    ssk, ssq = ev("ssk", TG), ev("ssq", TG)
    kr, qr = ev("kr", TG), ev("qr", TG)
    kn2, qn2 = ev("kn2", TG), ev("qn2", TG)
    kept_x = ev("kept_x", 1, True, 16 * SHARED)
    ln1, ln2 = Norm(es, nc, fx, "l0n1_"), Norm(es, nc, fx, "l0n2_")
    fx.norms = (ln1, ln2)
    dve_chain = Chain(es, nc, "l0_dve_chain", 33)
    pool_chain = Chain(es, nc, "l0_pool_chain", 4 * TG)
    WLOADS, NLOADS = 4 * 16, 13 * 16

    with ExitStack() as mem:
        def sb(name, shape):
            return mem.enter_context(nc.sbuf_tensor("l0_" + name, shape, F32))

        wqk, wv = sb("wqk", [P, KC, 2 * DIM]), sb("wv", [P, KC, DIM])
        wo, wg = sb("wo", [P, KC, DIM]), sb("wg", [P, KC, E0])
        xwq, xwk, xwv, xwo = (sb("xw" + n, [P, KC, DIM]) for n in "qkvo")
        centre, gcentre = sb("centre", [P, P]), sb("gcentre", [P, P])
        gb, betab, cb = sb("gb", [P, 2]), sb("betab", [P, P]), sb("cb", [P, P])
        qb, kb, vb, ob = sb("qb", [P, DIM]), sb("kb", [P, DIM]), sb("vb", [P, P]), sb("ob", [P, DIM])
        nq, nk = sb("nq", [P, DIM]), sb("nk", [P, DIM])
        XIN, XTIN, CT = sb("XIN", [P, TG, DIM]), sb("XTIN", [P, KC, GTOK]), sb("CT", [P, KC, GTOK])
        X, XT = sb("X", [P, TG, DIM]), sb("XT", [P, KC, GTOK])
        QB, QN = sb("QB", [P, TG, 2 * DIM]), sb("QN", [P, TG, 2 * DIM])
        wnat = QN[:].rearrange("p (n m) o -> p n m o", n=2)[:, :, :, 0:DIM]
        QB2 = sb("QB2", [P, TG, 2 * DIM])
        QKT, QKT2 = sb("QKT", [P, 2 * KC, GTOK]), sb("QKT2", [P, 2 * KC, GTOK])
        QM, KM = sb("QM", [P, KC, GSEQ, 8, SEQ]), sb("KM", [P, KC, GSEQ, 8, SEQ])
        W, WT = sb("W", [P, 2, H16, SEQ]), sb("WT", [P, 2, H16 // 2, P])
        SQ = WT[:].rearrange("p a j q -> p (a j q)").rearrange("p (t o) -> p t o", t=TG)
        V, V2 = sb("V", [P, TG, H16, 2 * 17]), sb("V2", [P, TG, PER, 8, 2 * 17])
        O, OT = sb("O", [P, 2, DIM]), sb("OT", [P, KC, GTOK])
        SS, RS = sb("SS", [P, TG, 32]), sb("RS", [P, TG, 32])
        s1, s2 = sb("s1", [P, 2 * TG]), sb("s2", [P, 2 * TG])
        st, mv, rs = sb("st", [P, TG, 6]), sb("mv", [P, TG, 2]), sb("rs", [P, TG])
        den, mx = sb("den", [P, TG, H16]), sb("mx", [P, TG, H16])

        def some_masks(dst, src, c, t, heads_of_bank, act):
            todo = [(b, h) for b in range(2) for h in heads_of_bank]
            for i in range(len(todo) * t // TG, len(todo) * (t + 1) // TG):
                b, h = todo[i]
                last = mask_bank(nc, act, dst, src, fx.hm16, c, b, [h])
                if h == heads_of_bank[-1]:
                    last.then_inc((c.masked_act if act else c.masked).sem, 1)

        with nc.Block() as block:
            @block.sync
            def _(sp):
                sp.dma_start(wnat[:, 0], io["la_wq"].rearrange("(m p) i -> p m i", p=P)).then_inc(ld_w, 16)
                sp.dma_start(wnat[:, 1], io["la_wk"].rearrange("(m p) i -> p m i", p=P)).then_inc(ld_w, 16)
                sp.dma_start(centre[:], io["centre"]).then_inc(ld_w, 16)
                sp.dma_start(gb[:], io["gb"]).then_inc(ld_w, 16)
                for dst, src in ((wv, io["la_wv"]), (wo, io["la_wo"]), (xwq, io["xa_wq"]), (xwk, io["xa_wk"]),
                                 (xwv, io["xa_wv"]), (xwo, io["xa_wo"]), (wg, io["wg"])):
                    sp.dma_start(dst[:], src.rearrange("(m p) o -> p m o", p=P)).then_inc(ld_n, 16)
                for dst, src in ((qb, io["qb"]), (kb, io["kb"]), (vb, io["vb"]), (ob, io["ob"]), (nq, io["nq"]), (nk, io["nk"])):
                    sp.dma_start(dst[:], src).then_inc(ld_n, 16)

                def load(g, again):
                    if again:
                        ring.wait_filled_before(sp, g - 1, ("la_v", TG - 1))
                    sp.dma_start(XTIN[:], io["xT"][:, bass.ds(g * GTOK, GTOK)].rearrange(
                        "(m p) t -> p m t", p=P)).then_inc(ld_xt.sem, 16)
                    if again:
                        ring.wait_filled_before(sp, g, ("xa_v", TG - 1))
                    sp.dma_start(CT[:], io["cT"][:, bass.ds(g * GTOK, GTOK)].rearrange(
                        "(m p) t -> p m t", p=P)).then_inc(ld_c.sem, 16)
                    if again:
                        ring.wait_emptied_before(sp, g, ("la_out", TG - 1))
                    sp.dma_start(XIN[:], io["x"][bass.ds(g * GTOK, GTOK), :].rearrange(
                        "(t p) d -> p t d", p=P)).then_inc(ld_x.sem, 16)


                load(0, False)
                with sp.Fori(1, GROUPS) as g:
                    load(g, True)
                sp.wait_ge(fx.ready, fx.READY)
                for dst, done, n in ((fx.xs[SHARED * TOKENS:, :], fx.slots_zeroed, fx.NS0),
                                     (fx.xs1[TOKENS:, :], fx.slots_zeroed1, fx.NS1)):
                    sp.dma_start(dst.rearrange("(n p) d -> p n d", p=P),
                                 fx.zeros[:].unsqueeze(1).broadcast_to([P, n, DIM])).then_inc(done, 16)

            @block.gpsimd
            def _(pool):
                nc.gpsimd.memset(V[:], 0.0)
                nc.gpsimd.memset(V2[:], 0.0).then_inc(zeroed, 1)
                pool.wait_ge(zeroed, 1)
                for a in range(2):
                    half = slice(a * SEQ, (a + 1) * SEQ)
                    nc.gpsimd.memset(V[half, :, :, a * 17 + 16:a * 17 + 17], 1.0)
                    last = nc.gpsimd.memset(V2[half, :, :, :, a * 17 + 16:a * 17 + 17].rearrange(
                        "p t s j o -> p (t s) j o"), 1.0)
                last.then_inc(zeroed, 1)

                def roots(g, t, sums, src, dst, done, chain, at):
                    pool.wait_ge(sums.sem, sums.at(g, t))
                    settle(pool, fx.pool_passed)
                    chain.link(pool, at, nc.gpsimd.tensor_scalar(dst, src, 1.0 / DIM, EPS_RMS, ALU.mult, ALU.add))
                    nc.gpsimd.tensor_tensor(dst, dst, fx.neghalf[:, 0:1], ALU.pow).then_inc(done.sem, 1)

                def context_roots(g, chain, at):
                    for t in range(TG):
                        roots(g, t, ssk, s1[:, t:t + 1], s2[:, t:t + 1], kr, chain, at)

                def group(g):
                    for t in range(TG):
                        ln1.root(nc, pool, g, t, mv, rs, fx.neghalf, pool_chain)
                    for t in range(TG):
                        roots(g, t, ssq, s1[:, TG + t:TG + t + 1], s2[:, TG + t:TG + t + 1], qr, pool_chain, g)
                    for t in range(TG):
                        ln2.root(nc, pool, g, t, mv, rs, fx.neghalf, pool_chain)

                context_roots(0, Steps(zeroed, 2), 0)
                with pool.Fori(0, GROUPS - 1) as g:
                    group(g)
                    context_roots(g + 1, pool_chain, g)
                pool_chain.close()
                pool_chain.k = 0
                group(GROUPS - 1)

            @block.scalar
            def _(act):
                kept_x.prime(act)
                act.wait_ge(fx.ready, fx.READY)
                act.wait_ge(zeroed, 2)

                def inputs(g):
                    for t in range(TG):
                        ring.wait_emptied(act, g - 1, ("la_qk", t))
                        nc.scalar.activation(SQ[:, t, :], QB[:, t, :], ACT.Square).then_inc(sq.sem, 1)
                    act.wait_ge(ss.sem, ss.at(g, 0))
                    nc.scalar.activation(RS[:], SS[:], ACT.Sqrt, bias=fx.epsln[:, 0:1],
                                         scale=1.0 / D16).then_inc(root.sem, 1)
                    for t in range(TG):
                        name = ("la_v", t)
                        ring.wait_full(act, g - 1, name)
                        for s in range(PER):
                            half = slice(s * SEQ, (s + 1) * SEQ)
                            last = nc.scalar.activation(V[half, t, :, s * 17:s * 17 + 16],
                                                        heads(ring.bank(name)[half, 0:DIM], H16), ACT.Copy)
                        last.then_inc(emptied["A"].sem, 1)

                def turn_inputs(g):
                    for t in range(TG):
                        turned(nc, act, g - 1, ring, ("la_tr", t), QKT[:, :, t * P:(t + 1) * P], 2 * KC)
                    masks_act(nc, act, g - 1, ring, ("la_tr", TG - 1), QM, QKT, fx.hm16, la)

                def group(g):
                    for t in range(TG):
                        ring.wait_emptied(act, g - 1, ("xa_k", t))
                        nc.scalar.activation(SQ[:, t, 0:DIM], QB2[:, t, DIM:2 * DIM], ACT.Square,
                                             accum_out=s1[:, t:t + 1]).then_inc(ssk.sem, 1)
                    for step in range(TG + la.lag + 2):
                        if step < TG:
                            for b in range(la.nb):
                                act.wait_ge(la.s_used.sem, la.s_used.at(g, step * la.nb + b))
                                part = W[:, step % 2, 8 * b:8 * b + 8, :]
                                nc.scalar.activation(part, part, ACT.Square, scale=0.25).then_inc(la.p_ready.sem, 1)
                        for name, t in la.fillers.get(step, []):
                            if name == "xa_trk":
                                turned(nc, act, g, ring, (name, t), QKT2[:, KC:2 * KC, t * P:(t + 1) * P], KC)
                        if 0 <= step - la.lag - 1 < TG:
                            core_turned_output(nc, act, g, la, step - la.lag - 1, ring, OT)
                    for n, t in xq_steps:
                        if n == "xa_xtr":
                            turned(nc, act, g, ring, (n, t), XT[:, :, t * P:(t + 1) * P], KC)
                        elif n == "xa_q":
                            ring.wait_emptied(act, g, (n, t))
                            nc.scalar.activation(SQ[:, t, 0:DIM], QB2[:, t, 0:DIM], ACT.Square,
                                                 accum_out=s1[:, TG + t:TG + t + 1]).then_inc(ssq.sem, 1)
                            some_masks(KM, QKT2[:, KC:2 * KC], xa, t, range(DVE_MASKS, 8), True)
                        else:
                            turned(nc, act, g, ring, (n, t), QKT2[:, 0:KC, t * P:(t + 1) * P], KC)
                    softmax_act(nc, act, g, xa, ring, SB, W, WT, OT, 0.25)

                def router(g):
                    for i in range(PAIRS):
                        ring.wait_full(act, g, ("r_xtr", i))
                        nc.scalar.activation(
                            XT[:, :, 2 * i * P:2 * (i + 1) * P].rearrange("p m (t q) -> p t m q", t=2),
                            ring.bank(("r_xtr", i))[:].rearrange("p (t m q) -> p t m q", t=2, m=KC),
                            ACT.Copy).then_inc(emptied["A"].sem, 1)
                    act.wait_ge(ln2.done.sem, ln2.done.at(g, TG - 1))
                    for n in range(SHARED):
                        act.dma_start(fx.xs[bass.ds(g * GTOK + n * TOKENS, GTOK), :].rearrange(
                            "(t p) d -> p t d", p=P), X[:]).then_inc(kept_x.sem, 16)

                ring.skip(act, emptied["A"], -1, None, AHEAD)
                inputs(0)
                ring.skip(act, emptied["A"], -1, ROUTER, TURN)
                turn_inputs(0)
                with act.Fori(0, GROUPS - 1) as g:
                    group(g)
                    inputs(g + 1)
                    router(g)
                    turn_inputs(g + 1)
                group(GROUPS - 1)
                ring.skip(act, emptied["A"], GROUPS - 1, AHEAD, ROUTER)
                router(GROUPS - 1)
                ring.skip(act, emptied["A"], GROUPS - 1, TURN, LOGITS)
                act.wait_ge(kept_x.sem, 16 * SHARED * (GROUPS + 1))

            @block.vector
            def _(dve):
                dve.wait_ge(fx.ready, fx.READY)
                dve.wait_ge(ld_w, WLOADS)
                nc.vector.tensor_scalar(gcentre[:], centre[:], gb[:, 0:1], None, ALU.mult)
                nc.vector.tensor_scalar(betab[:], fx.ones[:], gb[:, 1:2], None, ALU.mult).then_inc(folded, 1)
                dve.wait_ge(fold, 1)
                nc.vector.tensor_copy(cb[:], OB[0][:, 0:P])
                for n in range(2):
                    for m in range(KC):
                        last = nc.vector.tensor_copy(
                            wqk[:, m, n * DIM:(n + 1) * DIM], SB[2 * n + m][:, 0:DIM])
                last.then_inc(folded, 1)
                dve.wait_ge(folded, 2)
                dve.wait_ge(ld_n, NLOADS)
                dve.wait_ge(zeroed, 2)

                def inputs(g, chain, at):
                    for t in range(TG):
                        name = ("la_qk", t)
                        ring.wait_full(dve, g - 1, name)
                        nc.vector.tensor_tensor(QB[:, t, :].rearrange("p (n o) -> p n o", o=P),
                                                ring.bank(name)[:].rearrange("p (n o) -> p n o", o=P),
                                                cb[:].unsqueeze(1).broadcast_to([P, 4, P]),
                                                ALU.add).then_inc(emptied["D"].sem, 1)
                    for t in range(TG):
                        dve.wait_ge(sq.sem, sq.at(g, t))
                        last = nc.vector.tensor_reduce(SS[:, t, :], heads(SQ[:, t, :], 32), AX, ALU.add)
                    last.then_inc(ss.sem, 1)
                    for t in range(TG):
                        name = ("xa_k", t)
                        ring.wait_full(dve, g - 1, name)
                        nc.vector.tensor_tensor(QB2[:, t, DIM:2 * DIM], ring.bank(name)[:, 0:DIM], kb[:],
                                                ALU.add).then_inc(emptied["D"].sem, 1)
                    dve.wait_ge(root.sem, root.at(g, 0))
                    chain.link(dve, at, nc.vector.reciprocal(RS[:], RS[:]))
                    for t in range(TG):
                        nc.vector.tensor_tensor(heads(QN[:, t, :], 32), heads(QB[:, t, :], 32),
                                                RS[:, t, :].unsqueeze(2).broadcast_to([P, 32, 16]),
                                                ALU.mult).then_inc(qn.sem, 1)

                def mask_inputs(g):
                    ring.wait_emptied(dve, g - 1, ("la_tr", TG - 1))
                    masks_dve(nc, g, QM, QKT, fx.hm16, la)

                def group(g):
                    def residual(name, t, old, norm):
                        ring.wait_full(dve, g, (name, t))
                        nc.vector.tensor_tensor(X[:, t, :], ring.bank((name, t))[:, 0:DIM], old,
                                                ALU.add).then_inc(emptied["D"].sem, 1)
                        ring.wait_emptied(dve, g, (name, t))
                        if norm is ln2:
                            dve_chain.link(dve, g, nc.vector.tensor_tensor(X[:, t, :], X[:, t, :], ob[:], ALU.add))
                        norm.moments(nc, dve, g, t, X[:, t, :], st, mv, dve_chain)

                    for step in range(TG + la.lag + 3):
                        if step < TG:
                            for b in range(la.nb):
                                u = step * la.nb + b
                                dve.wait_ge(la.s_full.sem, la.s_full.at(g, u))
                                nc.vector.tensor_tensor(W[:, step % 2, 8 * b:8 * b + 8, :], heads(SB[u % 4][:], 8),
                                                        fx.cmask[:].unsqueeze(1).broadcast_to([P, 8, SEQ]),
                                                        ALU.mult).then_inc(la.s_used.sem, 1)
                        for name, t in la.fillers.get(step, []):
                            bank = ring.bank((name, t))
                            if name == "xa_v":
                                ring.wait_full(dve, g, (name, t))
                                for a in range(2):
                                    half = slice(a * SEQ, (a + 1) * SEQ)
                                    last = nc.vector.tensor_tensor(
                                        V2[half, t, :, :, a * 17:a * 17 + 16],
                                        bank[half, 0:DIM].rearrange("p (s j d) -> p s j d", s=PER, d=16),
                                        heads(vb[half, :], 8).unsqueeze(1).broadcast_to([SEQ, PER, 8, 16]), ALU.add)
                                last.then_inc(emptied["D"].sem, 1)
                        if step == 0:
                            for t in range(TG):
                                dve.wait_ge(kr.sem, kr.at(g, t))
                                nc.vector.scalar_tensor_tensor(
                                    out=QB2[:, t, DIM:2 * DIM], in0=QB2[:, t, DIM:2 * DIM], scalar=s2[:, t:t + 1],
                                    in1=nk[:], op0=ALU.mult, op1=ALU.mult).then_inc(kn2.sem, 1)
                        if 0 <= step - la.lag < TG:
                            core_outputs(nc, dve, g, la, step - la.lag, OB, O, den, dve_chain, EPS_LN)
                        if 0 <= step - la.lag - 2 < TG:
                            t = step - la.lag - 2
                            if t == 0:
                                dve.wait_ge(ld_x.sem, ld_x.at(g, 0))
                                dve.wait_ge(kept_x.sem, kept_x.at(g, -1))
                            residual("la_out", t, XIN[:, t, :], ln1)
                        if 0 <= step - la.lag - 3 < TG:
                            ln1.apply(nc, dve, g, step - la.lag - 3, X[:, step - la.lag - 3, :], mv, rs)
                    for n, t in xq_steps:
                        if n == "xa_q":
                            ring.wait_full(dve, g, (n, t))
                            nc.vector.tensor_tensor(QB2[:, t, 0:DIM], ring.bank((n, t))[:, 0:DIM], qb[:],
                                                    ALU.add).then_inc(emptied["D"].sem, 1)
                            if t == 0:
                                ring.wait_emptied(dve, g, ("xa_trk", TG - 1))
                            some_masks(KM, QKT2[:, KC:2 * KC], xa, t, range(DVE_MASKS), False)
                        elif n == "xa_trq":
                            dve.wait_ge(qr.sem, qr.at(g, t))
                            nc.vector.scalar_tensor_tensor(out=QB2[:, t, 0:DIM], in0=QB2[:, t, 0:DIM],
                                                           scalar=s2[:, TG + t:TG + t + 1], in1=nq[:],
                                                           op0=ALU.mult, op1=ALU.mult).then_inc(qn2.sem, 1)
                    for step in range(TG + xa.lag + 3):
                        if step < TG:
                            softmax_scores(nc, dve, g, xa, step, SB, W, mx, dve_chain, None)
                        if 0 <= step - xa.lag < TG:
                            core_outputs(nc, dve, g, xa, step - xa.lag, OB, O, den, dve_chain, None)
                        if 0 <= step - xa.lag - 2 < TG:
                            t = step - xa.lag - 2
                            residual("xa_out", t, X[:, t, :], ln2)
                        if 0 <= step - xa.lag - 3 < TG:
                            ln2.apply(nc, dve, g, step - xa.lag - 3, X[:, step - xa.lag - 3, :], mv, rs)

                def router(g):
                    for i in range(PAIRS):
                        name = ("r_logit", i)
                        ring.wait_full(dve, g, name)
                        nc.vector.tensor_scalar(fx.LG[:, bass.ds(g * TG + 2 * i, 2), :],
                                                ring.bank(name)[:, 0:2 * E0].rearrange("p (t e) -> p t e", t=2),
                                                1.0, None, ALU.mult).then_inc(emptied["D"].sem, 1)

                ring.skip(dve, emptied["D"], -1, None, AHEAD)
                inputs(0, Steps(folded, 2), 0)
                ring.skip(dve, emptied["D"], -1, LOGITS, None)
                mask_inputs(0)
                with dve.Fori(0, GROUPS - 1) as g:
                    group(g)
                    inputs(g + 1, dve_chain, g)
                    router(g)
                    mask_inputs(g + 1)
                dve_chain.close()
                dve_chain.k = 0
                group(GROUPS - 1)
                ring.skip(dve, emptied["D"], GROUPS - 1, AHEAD, ROUTER)
                router(GROUPS - 1)

            @block.tensor
            def _(pe):
                pe.wait_ge(fx.ready, fx.READY)
                pe.wait_ge(ld_w, WLOADS)
                pe.wait_ge(folded, 1)
                nc.tensor.matmul(OB[0][:, 0:P], betab[:], centre[:], start=True, stop=True)
                for n in range(2):
                    for i in range(KC):
                        for m in range(KC):
                            last = nc.tensor.matmul(SB[2 * n + i][:, m * P:(m + 1) * P],
                                                    wnat[:, n, m, i * P:(i + 1) * P], gcentre[:],
                                                    start=True, stop=True)
                last.then_inc(fold, 1)
                pe.wait_ge(folded, 2)
                pe.wait_ge(ld_n, NLOADS)
                def project(g, name, t, x, w):
                    ring.before_fill(pe, g, (name, t))
                    dst = ring.bank((name, t))[:, 0:w.shape[2]]
                    product(nc, dst, chunks(x, t), [w[:, m, :] for m in range(KC)]).then_inc(full.sem, 1)

                def inputs(g):
                    pe.wait_ge(ld_xt.sem, ld_xt.at(g, 0))
                    for t in range(TG):
                        project(g - 1, "la_qk", t, XTIN, wqk)
                    pe.wait_ge(ld_c.sem, ld_c.at(g, 0))
                    for t in range(TG):
                        project(g - 1, "xa_k", t, CT, xwk)
                    for t in range(TG):
                        project(g - 1, "la_v", t, XTIN, wv)

                def turn_inputs(g):
                    for t in range(TG):
                        ring.before_fill(pe, g - 1, ("la_tr", t))
                        pe.wait_ge(qn.sem, qn.at(g, t))
                        turn(nc, pe, g - 1, ring, ("la_tr", t), [QN[:, t, i * P:(i + 1) * P] for i in range(4)],
                             fx.ident)

                def group(g):
                    ring.begin(None)
                    def context(name, t):
                        ring.before_fill(pe, g, (name, t))
                        if name == "xa_trk":
                            pe.wait_ge(kn2.sem, kn2.at(g, t))
                            return turn(nc, pe, g, ring, (name, t),
                                        [QB2[:, t, DIM + m * P:DIM + (m + 1) * P] for m in range(KC)], fx.ident)
                        bank = ring.bank((name, t))
                        for s in range(PER):
                            tok = slice(t * P + s * SEQ, t * P + (s + 1) * SEQ)
                            for a in range(2):
                                last = product(nc, bank[a * SEQ:(a + 1) * SEQ, s * P:(s + 1) * P],
                                               [CT[:, m, tok] for m in range(KC)],
                                               [xwv[:, m, a * P:(a + 1) * P] for m in range(KC)])
                        last.then_inc(full.sem, 1)

                    def out_la(bank, t):
                        return product(nc, bank[:, 0:DIM], chunks(OT, t), [wo[:, m, :] for m in range(KC)])

                    core_pe(nc, pe, g, la, ring, QKT[:, KC:2 * KC], QM, SB, OB, W, None, V, O, OT, fx.ident, out_la,
                            context)
                    for n, t in xq_steps:
                        if n == "xa_q":
                            ring.before_fill(pe, g, (n, t))
                            ring.wait_emptied(pe, g, ("xa_xtr", t))
                            dst = ring.bank((n, t))[:, 0:DIM]
                            product(nc, dst, chunks(XT, t), [xwq[:, m, :] for m in range(KC)]).then_inc(full.sem, 1)
                        else:
                            ring.before_fill(pe, g, (n, t))
                            if n == "xa_xtr":
                                pe.wait_ge(ln1.done.sem, ln1.done.at(g, t))
                                src = X
                            else:
                                pe.wait_ge(qn2.sem, qn2.at(g, t))
                                src = QB2
                            turn(nc, pe, g, ring, (n, t), [src[:, t, m * P:(m + 1) * P] for m in range(KC)], fx.ident)
                    ring.wait_emptied(pe, g, ("xa_trq", TG - 1))

                    def out_xa(bank, t):
                        return product(nc, bank[:, 0:DIM], chunks(OT, t), [xwo[:, m, :] for m in range(KC)])

                    core_pe(nc, pe, g, xa, ring, QKT2[:, 0:KC], KM, SB, OB, W, WT, V2, O, OT, fx.ident, out_xa)

                def router(g):
                    for i in range(PAIRS):
                        ring.before_fill(pe, g, ("r_xtr", i))
                        pe.wait_ge(ln2.done.sem, ln2.done.at(g, 2 * i + 1))
                        turn(nc, pe, g, ring, ("r_xtr", i),
                             [X[:, t, m * P:(m + 1) * P] for t in (2 * i, 2 * i + 1) for m in range(KC)], fx.ident)

                def logits(g):
                    for i in range(PAIRS):
                        ring.before_fill(pe, g, ("r_logit", i))
                        ring.wait_emptied(pe, g, ("r_xtr", i))
                        for j in range(2):
                            last = product(nc, ring.bank(("r_logit", i))[:, j * E0:(j + 1) * E0],
                                           chunks(XT, 2 * i + j), [wg[:, m, :] for m in range(KC)])
                        last.then_inc(full.sem, 1)

                ring.skip(pe, full, -1, None, AHEAD)
                ring.begin(AHEAD)
                inputs(0)
                ring.skip(pe, full, -1, ROUTER, TURN)
                ring.begin(TURN)
                ring.wait_emptied(pe, -1, ("la_v", TG - 1))
                turn_inputs(0)
                ring.skip(pe, full, -1, LOGITS, None)
                ring.wait_emptied(pe, -1, ("la_tr", TG - 1))
                with pe.Fori(0, GROUPS - 1) as g:
                    group(g)
                    inputs(g + 1)
                    router(g)
                    turn_inputs(g + 1)
                    logits(g)
                group(GROUPS - 1)
                ring.skip(pe, full, GROUPS - 1, AHEAD, ROUTER)
                ring.begin(ROUTER)
                ring.wait_emptied(pe, GROUPS - 1, ("xa_out", TG - 1))
                router(GROUPS - 1)
                ring.skip(pe, full, GROUPS - 1, TURN, LOGITS)
                ring.begin(LOGITS)
                logits(GROUPS - 1)


I32 = mybir.dt.int32


class Route:

    def __init__(self, es, nc, mem, kept, x, e, k, groups, slot_tiles, first_tile,
                 row_shift):
        self.e, self.k, self.groups, self.slot_tiles, self.first_tile = e, k, groups, slot_tiles, first_tile
        self.row_shift = row_shift
        sb = lambda n, shape, dt=F32: mem.enter_context(nc.sbuf_tensor(x + n, shape, dt))
        self.prob = sb("prob", [P, TILES, e])
        self.masked = sb("masked", [P, TILES, e])
        self.cmp, self.cmp2 = (sb(n, [P, TILES * max(e, groups * groups)]) for n in ("cmp", "cmp2"))
        self.sel = sb("sel", [P, TILES, e])
        self.slot = sb("slot", [P, TILES, e])
        self.a, self.b = sb("sa", [P, TILES, e]), sb("sb", [P, TILES, e])
        self.one = sb("one", [P, TILES])
        self.gmax, self.grank = sb("gmax", [P, TILES, max(groups, 1)]), sb("grank", [P, TILES, max(groups, 1)])
        self.nt, self.ends = sb("nt", [P, e]), sb("ends", [P, e])
        self.ends2 = sb("ends2", [P, e])
        self.hot = sb("hot", [P, k, TILES, e])
        self.pick = sb("pick", [P, TILES, e])
        self.posf = sb("posf", [P, TILES, k])
        self.pos, self.wt = kept
        self.row = sb("row", [P, TILES, k], U32) if row_shift else self.pos
        self.tcmp = sb("tcmp", [P, slot_tiles, e])
        self.texpf = sb("texpf", [P, slot_tiles])
        self.texp = sb("texp", [P, first_tile + slot_tiles], I32)
        sem = lambda n: es.enter_context(nc.semaphore(x + n))
        self.shifted, self.exped = sem("shifted"), sem("exped")
        self.counted = sem("counted")
        self.placed = sem("placed")
        self.steps = Steps(sem("steps"))

    def on_act(self, nc, act):
        act.wait_ge(self.shifted, 1)
        nc.scalar.activation(self.prob[:], self.prob[:], ACT.Exp).then_inc(self.exped, 1)

    def on_pe(self, nc, pe, before, ones, rank_bank, total_bank):
        pe.wait_ge(self.steps.sem, self.hot_step)
        n = TILES * self.e
        flat = self.sel[:].rearrange("p t e -> p (t e)")
        nc.tensor.matmul(rank_bank[:, 0:n], before[:], flat, start=True, stop=True)
        nc.tensor.matmul(total_bank[:, 0:n], ones[:], flat, start=True, stop=True).then_inc(self.counted, 1)

    def ranks(self, do, dve, nc, value, rank, n, c1, c2, tri):
        mine = value.unsqueeze(3).broadcast_to([P, TILES, n, n])
        other = value.unsqueeze(2).broadcast_to([P, TILES, n, n])
        do(dve, nc.vector.tensor_tensor(c1, other, mine, ALU.is_equal))
        do(dve, nc.vector.tensor_tensor(c1, c1, tri.unsqueeze(1).broadcast_to([P, TILES, n, n]), ALU.mult))
        do(dve, nc.vector.tensor_tensor(c2, other, mine, ALU.is_gt))
        do(dve, nc.vector.tensor_tensor(c1, c1, c2, ALU.add))
        do(dve, nc.vector.tensor_reduce(rank, c1, AX, ALU.add))

    def on_dve(self, nc, dve, logits, tri, last_first, thresholds, tile_row, rank_bank, total_bank):
        do, e, k, v = self.steps, self.e, self.k, nc.vector
        one = self.one[:]
        over = lambda ap, n: ap.unsqueeze(2).broadcast_to([P, TILES, n])
        do(dve, v.tensor_reduce(one, logits, AX, ALU.max))
        v.tensor_tensor(self.prob[:], logits, over(one, e), ALU.subtract).then_inc(self.shifted, 1)
        dve.wait_ge(self.exped, 1)
        do(dve, v.tensor_reduce(one, self.prob[:], AX, ALU.add))
        do(dve, v.reciprocal(one, one))
        do(dve, v.tensor_tensor(self.prob[:], self.prob[:], over(one, e), ALU.mult))
        value = self.prob[:]
        if self.groups:
            ng, per = self.groups, e // self.groups
            do(dve, v.tensor_reduce(self.gmax[:].rearrange("p t g -> p (t g)"),
                                    self.prob[:].rearrange("p t (g j) -> p (t g) j", g=ng), AX, ALU.max))
            c = [x[:, 0:TILES * ng * ng].rearrange(
                "p (t a b) -> p t a b", a=ng, b=ng) for x in (self.cmp, self.cmp2)]
            self.ranks(do, dve, nc, self.gmax[:], self.grank[:], ng, c[0], c[1], tri)
            do(dve, v.tensor_scalar(self.grank[:], self.grank[:], float(TOPG), None, ALU.is_lt))
            split = lambda x: x.rearrange("p t (g j) -> p (t g) j", j=per)
            keep = self.grank[:].rearrange("p t g -> p (t g)").unsqueeze(2).broadcast_to([P, TILES * ng, per])
            do(dve, v.tensor_tensor(split(self.masked[:]), split(self.prob[:]), keep, ALU.mult))
            do(dve, v.tensor_scalar(self.grank[:], self.grank[:], 1.0, None, ALU.subtract))
            do(dve, v.tensor_tensor(split(self.masked[:]), split(self.masked[:]), keep, ALU.add))
            value = self.masked[:]
        index = last_first.unsqueeze(1).broadcast_to([P, TILES, e])
        for i in range(k):
            hot = self.hot[:, i]
            do(dve, v.tensor_reduce(self.wt[:, :, i], value, AX, ALU.max))
            do(dve, v.tensor_tensor(hot, value, over(self.wt[:, :, i], e), ALU.is_equal))
            do(dve, v.tensor_tensor(hot, hot, index, ALU.mult))
            do(dve, v.tensor_reduce(one, hot, AX, ALU.max))
            do(dve, v.tensor_tensor(hot, hot, over(one, e), ALU.is_equal))
            if i:
                do(dve, v.tensor_tensor(self.sel[:], self.sel[:], hot, ALU.add))
            else:
                do(dve, v.tensor_copy(self.sel[:], hot))
            if i < k - 1:
                do(dve, v.scalar_tensor_tensor(out=self.masked[:], in0=hot, scalar=-4.0, in1=value, op0=ALU.mult,
                                               op1=ALU.add))
                value = self.masked[:]
        self.hot_step = do.k
        dve.wait_ge(self.counted, 1)
        total = total_bank[:, 0:TILES * e].rearrange("p (t e) -> p t e", e=e)
        do(dve, v.tensor_copy(self.a[:], total))
        src, dst, d = self.a, self.b, 1
        while d < TILES:
            do(dve, v.tensor_copy(dst[:, 0:d], src[:, 0:d]))
            do(dve, v.tensor_tensor(dst[:, d:], src[:, d:], src[:, 0:TILES - d], ALU.add))
            src, dst, d = dst, src, 2 * d
        count = src[:, TILES - 1, :]
        c = self.cmp[:, 0:e * TILES].rearrange("p (e j) -> p e j", e=e)
        do(dve, v.tensor_tensor(c, count.unsqueeze(2).broadcast_to([P, e, TILES]),
                                thresholds.unsqueeze(1).broadcast_to([P, e, TILES]), ALU.is_gt))
        do(dve, v.tensor_reduce(self.nt[:], c, AX, ALU.add))
        do(dve, v.tensor_tensor(dst[:], src[:], total, ALU.subtract))
        slots = dst
        src, dst, d = self.nt, self.ends, 1
        while d < e:
            do(dve, v.tensor_copy(dst[:, 0:d], src[:, 0:d]))
            do(dve, v.tensor_tensor(dst[:, d:], src[:, d:], src[:, 0:e - d], ALU.add))
            src, dst, d = dst, (self.ends2 if dst is self.ends else self.ends), 2 * d
        ends, first = src, dst
        do(dve, v.tensor_tensor(first[:], ends[:], self.nt[:], ALU.subtract))
        do(dve, v.tensor_scalar(first[:], first[:], float(P), float(P * self.first_tile), ALU.mult, ALU.add))
        do(dve, v.tensor_tensor(self.slot[:], slots[:], first[:].unsqueeze(1).broadcast_to([P, TILES, e]), ALU.add))
        do(dve, v.tensor_tensor(self.slot[:], self.slot[:],
                                rank_bank[:, 0:TILES * e].rearrange("p (t e) -> p t e", e=e), ALU.add))
        for i in range(k):
            do(dve, v.tensor_tensor(self.pick[:], self.hot[:, i], self.slot[:], ALU.mult))
            do(dve, v.tensor_reduce(self.posf[:, :, i], self.pick[:], AX, ALU.add))
        do(dve, v.tensor_copy(self.pos[:], self.posf[:]))
        if self.row_shift:
            do(dve, v.tensor_scalar(self.row[:], self.posf[:], float(self.row_shift), None, ALU.add))
        n = self.slot_tiles
        do(dve, v.tensor_tensor(self.tcmp[:], tile_row[:, 0:n].unsqueeze(2).broadcast_to([P, n, e]),
                                ends[:].unsqueeze(1).broadcast_to([P, n, e]), ALU.is_ge))
        do(dve, v.tensor_reduce(self.texpf[:], self.tcmp[:], AX, ALU.add))
        do(dve, v.tensor_scalar(self.texpf[:], self.texpf[:], float(e - 1), None, ALU.min))
        v.tensor_copy(self.texp[:, self.first_tile:], self.texpf[:]).then_inc(self.placed, 1)


PEEL = 8


def tile_pipeline(engine, step, n, split=0, at_split=None):
    if split:
        with engine.Fori(0, split // 4) as i:
            for b in range(4):
                step(i * 4 + b, b, None)
        at_split()
    with engine.Fori(split // 4, (n - PEEL) // 4) as i:
        for b in range(4):
            step(i * 4 + b, b, None)
    for j in range(n - PEEL, n):
        step(j, j % 4, n - 1 - j)


def follows(ahead, k):
    return ahead is None or ahead >= k


def moe0(nc, es, io, fx):
    NS, NSH = fx.NS0, SHARED * TILES
    NT = NSH + NS
    IW, KI = 2 * I0, I0 - P
    with ExitStack() as mem:
        def sb(name, shape, dt=F32):
            return mem.enter_context(nc.sbuf_tensor("m0_" + name, shape, dt))

        def sem(name):
            return es.enter_context(nc.semaphore("m0_" + name))

        r = Route(es, nc, mem, (fx.pos0, fx.wt0), "r0_", E0, TOP0, NGRP, NS, NSH, 0)
        W13 = sb("W13", [P, KC, EALL, IW])
        W2A, W2B = sb("W2A", [P, EALL, DIM]), sb("W2B", [P, EALL, DIM])
        XG, XGT = sb("XG", [P, 4, DIM]), sb("XGT", [P, 2, KC * P])
        SG, H, HT = sb("SG", [P, 2, I0]), sb("H", [P, 2, I0]), sb("HT", [P, 2, 2, P])
        Y = sb("Y", [P, 2, DIM])
        XD = sb("XD", [P, TILES, DIM])
        shared_set = sem("shared_set")
        BT, BH, BU, BY = fx.PJ, fx.SB[0:2], fx.SB[2:4], fx.OB
        ld_sh, ld_w = sem("ld_sh"), sem("ld_w")
        ld_xd, sent = sem("ld_xd"), sem("sent")
        ld_x = [sem(f"ld_x{b}") for b in range(4)]
        t_full, t_used = sem("t_full"), sem("t_used")
        u_full, gate, h_done = sem("u_full"), sem("gate"), sem("h_done")
        ht_full, ht_used = sem("ht_full"), sem("ht_used")
        y_full, y_used = sem("y_full"), sem("y_used")
        stored = [sem(f"stored{b}") for b in range(2)]

        with nc.Block() as block:
            @block.sync
            def _(sp):
                for b in range(2):
                    sp.sem_inc(stored[b], 16)

                def load(j, b):
                    sp.wait_ge(t_full, j + 1)
                    sp.dma_start(XG[:, b, :], fx.xs[bass.ds(j * P, P), :]).then_inc(ld_x[b], 16)

                for j in range(4):
                    load(j, j)
                for m in range(KC):
                    sp.dma_start(W13[:, m, E0:EALL, :], io["w13"][m, :, E0:EALL, :]).then_inc(ld_sh, 16)
                sp.dma_start(W2A[:, E0:EALL, :], io["w2"][0:P, E0:EALL, :]).then_inc(ld_sh, 16)
                sp.dma_start(W2B[0:KI, E0:EALL, :], io["w2"][P:I0, E0:EALL, :]).then_inc(ld_sh, 16)
                sp.dma_start(XD[:], fx.xs[0:TOKENS, :].rearrange("(t p) d -> p t d", p=P)).then_inc(ld_xd, 16)
                for m in range(KC):
                    sp.dma_start(W13[:, m, 0:E0, :], io["w13"][m, :, 0:E0, :]).then_inc(ld_w, 16)
                sp.dma_start(W2A[:, 0:E0, :], io["w2"][0:P, 0:E0, :]).then_inc(ld_w, 16)
                sp.dma_start(W2B[0:KI, 0:E0, :], io["w2"][P:I0, 0:E0, :]).then_inc(ld_w, 16)

                for j in range(4, 7):
                    load(j, j % 4)

                def step(j, b, ahead):
                    if follows(ahead, 7):
                        load(j + 7, (b + 3) % 4)
                    sp.wait_ge(y_used, j + 1)
                    sp.dma_start(fx.ys[bass.ds(j * P, P), :], Y[:, b % 2, :]).then_inc(stored[b % 2], 16)

                tile_pipeline(sp, step, NT, NSH - 8, lambda: sp.wait_ge(sent, 16 * TILES * TOP0))
                for b in range(2):
                    sp.wait_ge(stored[b], 16 + 8 * NT)

            @block.gpsimd
            def _(pool):
                pool.wait_ge(ld_xd, 16)
                pool.wait_ge(fx.slots_zeroed, 16)
                pool.wait_ge(r.placed, 1)
                for t in range(TILES):
                    for k in range(TOP0):
                        pool.indirect_dma_start(
                            out=fx.xs, out_offset=bass.IndirectOffsetOnAxis(ap=r.pos[:, t, k:k + 1], axis=0),
                            in_=XD[:, t, :], in_offset=None).then_inc(sent, 16)

            @block.scalar
            def _(act):
                r.on_act(nc, act)

                def rows(j, b):
                    act.wait_ge(t_full, j + 5)
                    nc.scalar.activation(XGT[:, b % 2, :], BT[b % 2][:, 0:KC * P], ACT.Copy).then_inc(t_used, 1)

                def silu(j, b):
                    act.wait_ge(u_full, j + 1)
                    nc.scalar.activation(SG[:, b % 2, :], BU[b % 2][:, 0:I0], ACT.Silu).then_inc(gate, 1)

                def turned_product(j, b):
                    act.wait_ge(ht_full, j + 1)
                    nc.scalar.activation(HT[:, b % 2, 0, :], BH[b % 2][:, 0:P], ACT.Copy)
                    nc.scalar.activation(HT[0:KI, b % 2, 1, :], BH[b % 2][0:KI, P:2 * P], ACT.Copy).then_inc(ht_used, 1)

                def step(j, b, ahead):
                    if follows(ahead, 3):
                        rows(j + 3, b + 3)
                    if follows(ahead, 2):
                        silu(j + 2, b + 2)
                    if follows(ahead, 1):
                        turned_product(j + 1, b + 1)

                rows(0, 0)
                rows(1, 1)
                silu(0, 0)
                rows(2, 2)
                silu(1, 1)
                turned_product(0, 0)
                tile_pipeline(act, step, NT)

            @block.vector
            def _(dve):
                for n in range(SHARED):
                    last = nc.vector.memset(r.texp[:, n * TILES:(n + 1) * TILES], E0 + n)
                last.then_inc(shared_set, 1)
                r.on_dve(nc, dve, fx.LG[:], fx.tri[:], fx.last_first[:, 0:E0], fx.thresholds[:], fx.tile_row[:], BH[0], BH[1])

                def product(j, b):
                    dve.wait_ge(gate, j + 1)
                    nc.vector.tensor_tensor(H[:, b % 2, :], BU[b % 2][:, I0:IW], SG[:, b % 2, :],
                                            ALU.mult).then_inc(h_done, 1)

                def step(j, b, ahead):
                    if follows(ahead, 2):
                        product(j + 2, b + 2)
                    dve.wait_ge(y_full, j + 1)
                    dve.wait_ge(stored[b % 2], 8 * (j + (2 - b % 2)))
                    nc.vector.tensor_copy(Y[:, b % 2, :], BY[b % 2][:, 0:DIM]).then_inc(y_used, 1)

                product(0, 0)
                product(1, 1)
                tile_pipeline(dve, step, NT)

            @block.tensor
            def _(pe):
                pe.sem_inc(t_full, 4)
                r.on_pe(nc, pe, fx.before, fx.ones, BH[0], BH[1])

                def expert(j):
                    return pe.value_load(r.texp[0:1, bass.ds(j, 1)], min_val=0, max_val=EALL - 1)

                def rows(j, b):
                    pe.wait_ge(ld_x[b], 4 * (j - b) + 16)
                    for m in range(KC):
                        last = nc.tensor.transpose(BT[b % 2][:, m * P:(m + 1) * P], XG[:, b, m * P:(m + 1) * P],
                                                   fx.ident[:])
                    last.then_inc(t_full, 1)

                def gate_up(j, b):
                    e = expert(j)
                    pe.wait_ge(t_used, j + 1)
                    for m in range(KC):
                        last = nc.tensor.matmul(BU[b % 2][:, 0:IW], XGT[:, b % 2, m * P:(m + 1) * P],
                                                W13[:, m, bass.ds(e, 1), :], start=m == 0, stop=m == KC - 1)
                    last.then_inc(u_full, 1)

                def turn_product(j, b):
                    pe.wait_ge(h_done, j + 1)
                    nc.tensor.transpose(BH[b % 2][:, 0:P], H[:, b % 2, 0:P], fx.ident[:])
                    nc.tensor.transpose(BH[b % 2][0:KI, P:2 * P], H[:, b % 2, P:I0], fx.ident[:]).then_inc(ht_full, 1)

                def step(j, b, ahead):
                    if follows(ahead, 3):
                        rows(j + 3, (b + 3) % 4)
                    if follows(ahead, 2):
                        gate_up(j + 2, b + 2)
                    if follows(ahead, 1):
                        turn_product(j + 1, b + 1)
                    e = expert(j)
                    if not follows(ahead, 2):
                        pe.wait_ge(y_used, j - 1)
                    pe.wait_ge(ht_used, j + 1)
                    nc.tensor.matmul(BY[b % 2][:, 0:DIM], HT[:, b % 2, 0, :], W2A[:, bass.ds(e, 1), :],
                                     start=True, stop=False)
                    nc.tensor.matmul(BY[b % 2][:, 0:DIM], HT[0:KI, b % 2, 1, :], W2B[0:KI, bass.ds(e, 1), :],
                                     start=False, stop=True).then_inc(y_full, 1)

                def routed():
                    pe.wait_ge(r.placed, 1)
                    pe.wait_ge(ld_w, 64)

                pe.wait_ge(shared_set, 1)
                rows(0, 0)
                rows(1, 1)
                pe.wait_ge(ld_sh, 64)
                gate_up(0, 0)
                rows(2, 2)
                gate_up(1, 1)
                turn_product(0, 0)
                tile_pipeline(pe, step, NT, NSH - 4, routed)


def layer1(nc, es, io, fx):
    PJ, SB, OB = fx.PJ, fx.SB, fx.OB
    sa = Core(es, nc, "sa_", H16, D16, False, True, fx.softmax_core)
    xb = Core(es, nc, "xb_", H32, D32, True, True, fx.linear_core)
    xb.s_used = xb.p_ready
    xq_steps = staggered(("xb_xtr", 0), ("xb_q", 1))
    engine_of = {"xb_out": "D", "sa_out": "D", "r1_logit": "D"}
    sa.fillers = {i: [(n, t), (n, t + 1)] for i, (n, t) in enumerate((n, t) for n in ("xb_k", "xb_v") for t in (0, 2))}
    names = [("sa_xtr", t) for t in range(TG)]
    names += [(n, m) for n in ("sa_q", "sa_k") for m in range(KC)]
    names += [("sa_v", t) for t in range(TG)] + sa.names() + xq_steps
    names += [(n, t) for n in ("xb_trq", "xb_trk") for t in range(TG)]
    names += xb.names() + [("r1_xtr", t) for t in range(TG)] + [("r1_h", 0), ("r1_logit", 0)]
    uses = [(n, engine_of.get(n[0], "A")) for n in names]

    def ev(name, per, primed=False, step=1):
        return Event(es, nc, "l1_" + name, per, primed, step)

    full = ev("full", len(uses), True)
    emptied = {k: ev("emptied" + k, sum(e == k for _, e in uses), True) for k in "AD"}
    ring = Ring(PJ, full, emptied, uses)
    zeroed = es.enter_context(nc.semaphore("l1_zeroed"))
    ld_n = es.enter_context(nc.semaphore("l1_ld_n"))
    ld_c = ev("ld_c", 1, step=16)
    ld_r = ev("ld_r", 1, step=48)
    slots_read = ev("slots_read", 1)
    gathered = ev("gathered", TG, step=16 * TOP0)
    combined = ev("combined", 1, True)
    sums, root = ev("sums", 1), ev("root", 1)
    kn, qn = ev("kn", TG), ev("qn", TG)
    kept_x = ev("kept_x", 1, True, 16)
    ln0, (ln1, ln2) = Norm(es, nc, fx, "l1n0_"), (Norm(es, nc, fx, None, n) for n in fx.norms)
    dve_chain = Chain(es, nc, "l1_dve_chain", 6 + 3 * TG + 1 + 2 * 2 * TG + 2 * TG)
    pool_chain = Chain(es, nc, "l1_pool_chain", 3 * TG)
    first_dve, first_pool = (Steps(es.enter_context(nc.semaphore(n))) for n in ("l1_first_dve", "l1_first_pool"))
    NLOADS = 7 * 16

    with ExitStack() as mem:
        def sb(name, shape, dt=F32):
            return mem.enter_context(nc.sbuf_tensor("l1_" + name, shape, dt))

        wq, wk, wv, wo = sb("wq", [P, KC, DIM]), sb("wk", [P, KC, DIM]), sb("wv", [P, KC, SEQ]), sb("wo", [P, KC, DIM])
        xwq, xwkv = sb("xwq", [P, KC, DIM]), sb("xwkv", [P, KC, 2 * DIM])
        rw1, rw2 = sb("rw1", [P, KC, P]), sb("rw2", [P, E1])
        XIN, SH, GA = sb("XIN", [P, TG, DIM]), sb("SH", [P, SHARED, TG, DIM]), sb("GA", [P, TG, TOP0, DIM])
        slots, weight = sb("slots", [P, TG, TOP0], U32), sb("weight", [P, TG, TOP0])
        CT, X, XT = sb("CT", [P, KC, GTOK]), sb("X", [P, TG, DIM]), sb("XT", [P, KC, GTOK])
        QKT, KN, QN = sb("QKT", [P, 2 * KC, GTOK]), sb("KN", [P, TG, DIM]), sb("QN", [P, TG, DIM])
        KT, QT = sb("KT", [P, KC, GTOK]), sb("QT", [P, KC, GTOK])
        SQK = QN
        QM = sb("QM", [P, KC, GSEQ, 16, SEQ])
        KM = QM[:].rearrange("p m s h q -> p (m s h q)")[:, 0:KC * GSEQ * 8 * SEQ].rearrange(
            "p (m s h q) -> p m s h q", m=KC, s=GSEQ, h=8)
        W, WT = sb("W", [P, 2, H32, SEQ]), sb("WT", [P, 2, H16 // 2, P])
        VS, VX = sb("VS", [P, TG, PER, 8, 2 * 17]), sb("VX", [P, TG, H32, 2 * 9])
        O, OT, HR = sb("O", [P, 2, DIM]), sb("OT", [P, KC, GTOK]), sb("HR", [P, GTOK])
        SS, R = sb("SS", [P, 2, TG, H32]), sb("R", [P, 2, TG, H32])
        XN = sb("XN", [P, TG, DIM])
        st, mv, rs = sb("st", [P, TG, 6]), sb("mv", [P, TG, 2]), sb("rs", [P, TG])
        st0, mv0, rs0 = sb("st0", [P, TG, 6]), sb("mv0", [P, TG, 2]), sb("rs0", [P, TG])
        den, mx = sb("den", [P, TG, H32]), sb("mx", [P, TG, H16])
        SQ = WT[:].rearrange("p a j q -> p (a j q)")[:, 0:TG * DIM].rearrange("p (t o) -> p t o", t=TG)
        WS = W[:, :, 0:H16, :]

        with nc.Block() as block:
            @block.sync
            def _(sp):
                for dst, src in ((xwkv, io["xb_wkv"]), (wq, io["sa_wq"]), (wk, io["sa_wk"]), (wv, io["sa_wv"]), (wo, io["sa_wo"]),
                                 (xwq, io["xb_wq"]), (rw1, io["rw1"])):
                    sp.dma_start(dst[:], src.rearrange("(m p) o -> p m o", p=P)).then_inc(ld_n, 16)
                sp.dma_start(rw2[:], io["rw2"]).then_inc(ld_n, 16)
                with sp.Fori(0, GROUPS) as g:
                    ring.wait_filled_before(sp, g, ("xb_v", TG - 1))
                    sp.dma_start(CT[:], io["cT"][:, bass.ds(g * GTOK, GTOK)].rearrange(
                        "(m p) t -> p m t", p=P)).then_inc(ld_c.sem, 16)
                    sp.wait_ge(combined.sem, combined.at(g, -1))
                    for dst, src, first in ((XIN[:], fx.xs, 0), (SH[:, 0], fx.ys, 0), (SH[:, 1], fx.ys, TOKENS)):
                        sp.dma_start(dst, src[bass.ds(g * GTOK + first, GTOK), :].rearrange(
                            "(t p) d -> p t d", p=P)).then_inc(ld_r.sem, 16)

            @block.gpsimd
            def _(pool):
                def gather(g):
                    pool.wait_ge(combined.sem, combined.at(g, -1))
                    nc.gpsimd.tensor_copy(slots[:], fx.pos0[:, bass.ds(g * TG, TG), :]).then_inc(slots_read.sem, 1)
                    pool.wait_ge(slots_read.sem, slots_read.at(g, 0))
                    settle(pool, fx.pool_passed)
                    for t in range(TG):
                        for k in range(TOP0):
                            pool.indirect_dma_start(
                                out=GA[:, t, k, :], out_offset=None, in_=fx.ys,
                                in_offset=bass.IndirectOffsetOnAxis(ap=slots[:, t, k:k + 1], axis=0),
                            ).then_inc(gathered.sem, 16)

                def norms(g, which):
                    for t in range(TG):
                        which.root(nc, pool, g, t, mv, rs, fx.neghalf, pool_chain)

                gather(0)
                nc.gpsimd.memset(VS[:], 0.0)
                nc.gpsimd.memset(VX[:], 0.0).then_inc(zeroed, 1)
                pool.wait_ge(zeroed, 1)
                for a in range(2):
                    half = slice(a * SEQ, (a + 1) * SEQ)
                    nc.gpsimd.memset(VS[half, :, :, :, a * 17 + 16:a * 17 + 17].rearrange(
                        "p t s j o -> p (t s) j o"), 1.0)
                    last = nc.gpsimd.memset(VX[half, :, :, a * 9 + 8:a * 9 + 9], 1.0)
                last.then_inc(zeroed, 1)
                pool.wait_ge(zeroed, 2)
                for t in range(TG):
                    ln0.root(nc, pool, 0, t, mv0, rs0, fx.neghalf, first_pool)
                pool.wait_ge(ln0.rstd.sem, ln0.rstd.at(0, TG - 1))
                with pool.Fori(0, GROUPS - 1) as g:
                    gather(g + 1)
                    norms(g, ln1)
                    for t in range(TG):
                        ln0.root(nc, pool, g, t, mv0, rs0, fx.neghalf, pool_chain, 1)
                    norms(g, ln2)
                    pool.wait_ge(ln2.rstd.sem, ln2.rstd.at(g, TG - 1))
                pool_chain.close()
                pool_chain.k = 0
                for which in (ln1, ln2):
                    norms(GROUPS - 1, which)

            @block.scalar
            def _(act):
                emptied["A"].prime(act)
                kept_x.prime(act)
                act.wait_ge(zeroed, 2)
                with act.Fori(0, GROUPS) as g:
                    def copy_and_square(name, t, dst, squares):
                        ring.wait_full(act, g, (name, t))
                        src = ring.bank((name, t))[:, 0:DIM]
                        nc.scalar.activation(dst[:, t, :], src, ACT.Copy)
                        nc.scalar.activation(squares[:, t, :], src, ACT.Square).then_inc(emptied["A"].sem, 1)

                    def empty(name, t):
                        if name == "xb_k":
                            return copy_and_square(name, t, KN, SQK)
                        ring.wait_full(act, g, (name, t))
                        for s in range(PER):
                            half = slice(s * SEQ, (s + 1) * SEQ)
                            last = nc.scalar.activation(VX[half, t, :, s * 9:s * 9 + 8],
                                                        heads(ring.bank((name, t))[half, 0:DIM], H32), ACT.Copy)
                        last.then_inc(emptied["A"].sem, 1)

                    for t in range(TG):
                        turned(nc, act, g, ring, ("sa_xtr", t), XT[:, :, t * P:(t + 1) * P], KC)
                    for i, name in enumerate(("sa_q", "sa_k")):
                        for m in range(KC):
                            ring.wait_full(act, g, (name, m))
                            nc.scalar.activation(QKT[:, i * KC + m, :], ring.bank((name, m))[:],
                                                 ACT.Copy).then_inc(emptied["A"].sem, 1)
                    masks_act(nc, act, g, ring, ("sa_k", KC - 1), KM, QKT[:, KC:2 * KC], fx.hm16, sa)
                    for t in range(TG):
                        name = ("sa_v", t)
                        ring.wait_full(act, g, name)
                        for a in range(2):
                            half = slice(a * SEQ, (a + 1) * SEQ)
                            last = nc.scalar.activation(
                                VS[half, t, :, :, a * 17:a * 17 + 16].rearrange("p s (v i) d -> p (s v) i d", i=2),
                                ring.bank(name)[half, 0:PER * SEQ].rearrange("p (v d) -> p v d", d=16).unsqueeze(
                                    2).broadcast_to([SEQ, PER * 4, 2, 16]), ACT.Copy)
                        last.then_inc(emptied["A"].sem, 1)
                    softmax_act(nc, act, g, sa, ring, SB, WS, WT, OT, 0.25, empty)
                    for n, t in xq_steps:
                        if n == "xb_xtr":
                            turned(nc, act, g, ring, (n, t), XT[:, :, t * P:(t + 1) * P], KC)
                        else:
                            copy_and_square(n, t, QN, SQ)
                    act.wait_ge(sums.sem, sums.at(g, 0))
                    nc.scalar.activation(R[:], SS[:], ACT.Sqrt, bias=fx.epsrms[:, 0:1],
                                         scale=1.0 / D32).then_inc(root.sem, 1)
                    for t in range(TG):
                        turned(nc, act, g, ring, ("xb_trq", t), QT[:, :, t * P:(t + 1) * P], KC)
                    for t in range(TG):
                        turned(nc, act, g, ring, ("xb_trk", t), KT[:, :, t * P:(t + 1) * P], KC)
                    masks_act(nc, act, g, ring, ("xb_trq", TG - 1), QM, QT, fx.hm8, xb)
                    for step in range(TG + xb.lag + 1):
                        if step < TG:
                            for b in range(xb.nb):
                                u = step * xb.nb + b
                                act.wait_ge(xb.s_full.sem, xb.s_full.at(g, u))
                                nc.scalar.activation(W[:, step % 2, 8 * b:8 * b + 8, :], heads(SB[u % 4][:], 8),
                                                     ACT.Exp, scale=D32 ** -0.5).then_inc(xb.p_ready.sem, 1)
                        if 0 <= step - xb.lag - 1 < TG:
                            core_turned_output(nc, act, g, xb, step - xb.lag - 1, ring, OT)
                    for t in range(TG):
                        turned(nc, act, g, ring, ("r1_xtr", t), XT[:, :, t * P:(t + 1) * P], KC)
                    act.wait_ge(ln2.done.sem, ln2.done.at(g, TG - 1))
                    act.dma_start(fx.xs1[bass.ds(g * GTOK, GTOK), :].rearrange(
                        "(t p) d -> p t d", p=P), X[:]).then_inc(kept_x.sem, 16)
                    ring.wait_full(act, g, ("r1_h", 0))
                    nc.scalar.activation(HR[:], ring.bank(("r1_h", 0))[:], ACT.Gelu).then_inc(emptied["A"].sem, 1)
                act.wait_ge(kept_x.sem, 16 * (GROUPS + 1))

            @block.vector
            def _(dve):
                emptied["D"].prime(dve)
                combined.prime(dve)

                def combine(g, chain, at):
                    chain.link(dve, at, nc.vector.tensor_scalar(weight[:], fx.wt0[:, bass.ds(g * TG, TG), :],
                                                                1.0, None, ALU.mult))
                    dve.wait_ge(ld_r.sem, ld_r.at(g, 0))
                    chain.link(dve, at, nc.vector.tensor_tensor(XN[:], XIN[:], SH[:, 0], ALU.add))
                    chain.link(dve, at, nc.vector.tensor_tensor(XN[:], XN[:], SH[:, 1], ALU.add))
                    dve.wait_ge(gathered.sem, gathered.at(g, TG - 1))
                    for k in range(TOP0):
                        for t in range(TG):
                            last = nc.vector.scalar_tensor_tensor(out=XN[:, t, :], in0=GA[:, t, k, :],
                                                                  scalar=weight[:, t, k:k + 1], in1=XN[:, t, :],
                                                                  op0=ALU.mult, op1=ALU.add)
                        if k < TOP0 - 1:
                            chain.link(dve, at, last)
                    last.then_inc(combined.sem, 1)
                    dve.wait_ge(combined.sem, combined.at(g, 0))
                    for t in range(TG):
                        ln0.moments(nc, dve, at, t, XN[:, t, :], st0, mv0, chain)

                def group(g, more):
                    def residual(name, t, norm, order):
                        ring.wait_full(dve, g, (name, t))
                        x = X[:, t, :].rearrange(order, a=2, d=D32) if order else X[:, t, :]
                        y = ring.bank((name, t))[:, 0:DIM]
                        y = y.rearrange("p (a j d) -> p a j d", a=2, d=D32) if order else y
                        nc.vector.tensor_tensor(x, y, x, ALU.add).then_inc(emptied["D"].sem, 1)
                        ring.wait_emptied(dve, g, (name, t))
                        norm.moments(nc, dve, g, t, X[:, t, :], st, mv, dve_chain)

                    def head_sums(n, name, squares):
                        for t in range(TG):
                            ring.wait_emptied(dve, g, (name, t))
                            last = nc.vector.tensor_reduce(SS[:, n, t, :], heads(squares[:, t, :], H32), AX, ALU.add)
                        return last

                    dve.wait_ge(kept_x.sem, kept_x.at(g, -1))
                    for t in range(TG):
                        dve.wait_ge(ln0.rstd.sem, ln0.rstd.at(g, t))
                        nc.vector.tensor_scalar(X[:, t, :], XN[:, t, :], mv0[:, t, 0:1], rs0[:, t:t + 1],
                                                ALU.subtract, ALU.mult).then_inc(ln0.done.sem, 1)
                    ring.wait_emptied(dve, g, ("sa_k", KC - 1))
                    masks_dve(nc, g, KM, QKT[:, KC:2 * KC], fx.hm16, sa)
                    for step in range(TG + sa.lag + 3):
                        if step < TG:
                            softmax_scores(nc, dve, g, sa, step, SB, WS, mx, dve_chain, fx.cneg)
                        if 0 <= step - sa.lag < TG:
                            core_outputs(nc, dve, g, sa, step - sa.lag, OB, O, den, dve_chain, None)
                        if 0 <= step - sa.lag - 2 < TG:
                            residual("sa_out", step - sa.lag - 2, ln1, None)
                        if 0 <= step - sa.lag - 3 < TG:
                            ln1.apply(nc, dve, g, step - sa.lag - 3, X[:, step - sa.lag - 3, :], mv, rs)
                        if step == TG:
                            head_sums(1, "xb_k", SQK)
                    head_sums(0, "xb_q", SQ).then_inc(sums.sem, 1)
                    dve.wait_ge(root.sem, root.at(g, 0))
                    dve_chain.link(dve, g, nc.vector.reciprocal(R[:], R[:]))
                    for n, values, done in ((0, QN, qn), (1, KN, kn)):
                        for t in range(TG):
                            nc.vector.tensor_tensor(heads(values[:, t, :], H32), heads(values[:, t, :], H32),
                                                    R[:, n, t, :].unsqueeze(2).broadcast_to([P, H32, D32]),
                                                    ALU.mult).then_inc(done.sem, 1)
                    ring.wait_emptied(dve, g, ("xb_trq", TG - 1))
                    masks_dve(nc, g, QM, QT, fx.hm8, xb)
                    if more:
                        combine(g + 1, dve_chain, g)
                    for step in range(TG + xb.lag + 3):
                        if 0 <= step - xb.lag < TG:
                            core_outputs(nc, dve, g, xb, step - xb.lag, OB, O, den, dve_chain, None)
                        if 0 <= step - xb.lag - 2 < TG:
                            residual("xb_out", step - xb.lag - 2, ln2, "p (j a d) -> p a j d")
                        if 0 <= step - xb.lag - 3 < TG:
                            ln2.apply(nc, dve, g, step - xb.lag - 3, X[:, step - xb.lag - 3, :], mv, rs)
                    name = ("r1_logit", 0)
                    ring.wait_full(dve, g, name)
                    nc.vector.tensor_scalar(fx.LG1[:, bass.ds(g * TG, TG), :],
                                            ring.bank(name)[:, 0:TG * E1].rearrange("p (t e) -> p t e", e=E1),
                                            1.0, None, ALU.mult).then_inc(emptied["D"].sem, 1)
                combine(0, first_dve, 0)
                with dve.Fori(0, GROUPS - 1) as g:
                    group(g, True)
                dve_chain.close()
                dve_chain.k = 0
                group(GROUPS - 1, False)

            @block.tensor
            def _(pe):
                full.prime(pe)
                pe.wait_ge(ld_n, NLOADS + 16)
                with pe.Fori(0, GROUPS) as g:
                    def fill(name, t, stills, movings, width):
                        ring.before_fill(pe, g, (name, t))
                        product(nc, ring.bank((name, t))[:, 0:width], stills, movings).then_inc(full.sem, 1)

                    def turn_rows(name, t, done, src):
                        ring.before_fill(pe, g, (name, t))
                        pe.wait_ge(done.sem, done.at(g, t))
                        turn(nc, pe, g, ring, (name, t), [src[:, t, m * P:(m + 1) * P] for m in range(KC)], fx.ident)

                    for t in range(TG):
                        turn_rows("sa_xtr", t, ln0.done, X)
                    ring.wait_emptied(pe, g, ("sa_xtr", TG - 1))
                    for name, w in (("sa_q", wq), ("sa_k", wk)):
                        for o in range(KC):
                            fill(name, o, [w[:, m, o * P:(o + 1) * P] for m in range(KC)],
                                 [XT[:, m, :] for m in range(KC)], GTOK)
                    for t in range(TG):
                        ring.before_fill(pe, g, ("sa_v", t))
                        bank = ring.bank(("sa_v", t))
                        for s in range(PER):
                            tok = slice(t * P + s * SEQ, t * P + (s + 1) * SEQ)
                            for a in range(2):
                                last = product(nc, bank[a * SEQ:(a + 1) * SEQ, s * SEQ:(s + 1) * SEQ],
                                               [XT[:, m, tok] for m in range(KC)], [wv[:, m, :] for m in range(KC)])
                        last.then_inc(full.sem, 1)

                    def context(name, t):
                        if (name, t) == ("xb_k", 0):
                            pe.wait_ge(ld_c.sem, ld_c.at(g, 0))
                        lo = DIM if name == "xb_v" else 0
                        fill(name, t, chunks(CT, t), [xwkv[:, m, lo:lo + DIM] for m in range(KC)], DIM)

                    def out_sa(bank, t):
                        return product(nc, bank[:, 0:DIM], chunks(OT, t), [wo[:, m, :] for m in range(KC)])

                    core_pe(nc, pe, g, sa, ring, QKT[:, 0:KC], KM, SB, OB, WS, WT, VS, O, OT, fx.ident, out_sa,
                            context)
                    for n, t in xq_steps:
                        if n == "xb_xtr":
                            turn_rows(n, t, ln1.done, X)
                        else:
                            ring.wait_emptied(pe, g, ("xb_xtr", t))
                            fill(n, t, chunks(XT, t), [xwq[:, m, :] for m in range(KC)], DIM)
                    for t in range(TG):
                        turn_rows("xb_trq", t, qn, QN)
                    for t in range(TG):
                        turn_rows("xb_trk", t, kn, KN)

                    def out_xb(bank, t):
                        for a in range(2):
                            last = nc.tensor.transpose(bank[:, a * P:(a + 1) * P], OT[:, a, t * P:(t + 1) * P],
                                                       fx.ident[:])
                        return last

                    core_pe(nc, pe, g, xb, ring, KT, QM, SB, OB, W, None, VX, O, OT, fx.ident, out_xb)
                    for t in range(TG):
                        turn_rows("r1_xtr", t, ln2.done, X)
                    ring.wait_emptied(pe, g, ("r1_xtr", TG - 1))
                    fill("r1_h", 0, [rw1[:, m, :] for m in range(KC)], [XT[:, m, :] for m in range(KC)], GTOK)
                    name = ("r1_logit", 0)
                    ring.before_fill(pe, g, name)
                    ring.wait_emptied(pe, g, ("r1_h", 0))
                    for t in range(TG):
                        last = nc.tensor.matmul(ring.bank(name)[:, t * E1:(t + 1) * E1], HR[:, t * P:(t + 1) * P],
                                                rw2[:], start=True, stop=True)
                    last.then_inc(full.sem, 1)


def moe1(nc, es, io, fx):
    NS, CH = fx.NS1, I1 // P
    E2 = 2 * E1
    HALF, HC = I1 // 2, CH // 2
    with ExitStack() as kept:
        def keep(name, shape):
            return kept.enter_context(nc.sbuf_tensor("m1_" + name, shape, F32))

        def sem(name):
            return es.enter_context(nc.semaphore("m1_" + name))

        AC, ZB = keep("AC", [P, TILES, E2]), keep("ZB", [P, DIM])
        z_done = sem("z_done")
        with ExitStack() as mem:
            def sb(name, shape):
                return mem.enter_context(nc.sbuf_tensor("m1_" + name, shape, F32))

            r = Route(es, nc, mem, (fx.pos1, fx.wt1), "r1_", E1, TOP1, 0, NS, 0, TOKENS)
            w1, w2 = sb("w1", [P, KC, E1, I1]), sb("w2", [P, E1, CH, DIM])
            b1 = sb("b1", [P, E1, I1])
            b1T, b2 = sb("b1T", [P, E1, CH]), sb("b2", [P, DIM])
            eye = sb("eye", [P, E1, E2])
            GB = sb("GB", [P, E1, CH, E2])
            work = sb("work", [P, 4 * DIM + 2 * KC * P + I1 + 2 * I1 + 2 * DIM])
            XD = work[:, 0:TILES * DIM].rearrange("p (t d) -> p t d", t=TILES)
            at = [0]

            def part(n):
                at[0] += n
                return work[:, at[0] - n:at[0]]

            XG = part(4 * DIM).rearrange("p (b d) -> p b d", b=4)
            XGT = part(2 * KC * P).rearrange("p (b d) -> p b d", b=2)
            H = part(I1)
            HT = part(2 * I1).rearrange("p (b c q) -> p b c q", b=2, c=CH)
            Y = part(2 * DIM).rearrange("p (b d) -> p b d", b=2)
            used, term = sb("used", [P, TOP1, E1]), sb("term", [P, TILES, E1])
            BT, BU, BH, BY = fx.PJ, fx.SB[0:2], fx.SB[2:4], fx.OB
            ld_s, ld_xd = sem("ld_s"), sem("ld_xd")
            ld_w1 = [sem(f"ld_w1_{i}") for i in range(E1 // 2)]
            ld_w2 = [sem(f"ld_w2_{e}") for e in range(E1)]
            w1_in = sem("w1_in")
            sent = sem("sent")
            ld_x = [sem(f"ld_x{b}") for b in range(4)]
            z_gelu, z_parts, z_full = sem("z_gelu"), sem("z_parts"), sem("z_full")
            used_full = sem("used_full")
            t_full, t_used = sem("t_full"), sem("t_used")
            u_full, h_done = sem("u_full"), sem("h_done")
            ht_full, ht_used = sem("ht_full"), sem("ht_used")
            y_full, y_used = sem("y_full"), sem("y_used")
            stored = [sem(f"stored{b}") for b in range(2)]

            with nc.Block() as block:
                @block.sync
                def _(sp):
                    for b in range(2):
                        sp.sem_inc(stored[b], 16)
                    for dst, src in ((b1T, io["b1T"]), (eye, io["eye"])):
                        sp.dma_start(dst[:], src).then_inc(ld_s, 16)
                    sp.dma_start(b2[0:E2, :], io["b2"]).then_inc(ld_s, 16)
                    sp.dma_start(XD, fx.xs1[0:TOKENS, :].rearrange("(t p) d -> p t d", p=P)).then_inc(ld_xd, 16)

                    def load_w1(e):
                        sp.dma_start(w1[:, :, e, :], io["m1_w1"][:, :, e, :]).then_inc(ld_w1[e // 2], 16)
                        sp.dma_start(b1[:, e, :], io["b1"][:, e, :]).then_inc(ld_w1[e // 2], 16)

                    load_w1(0)
                    load_w1(1)
                    for e in range(E1):
                        sp.dma_start(w2[:, e], io["m1_w2"][:, e]).then_inc(ld_w2[e], 16)
                    sp.wait_ge(sent, 16 * TILES * TOP1)

                    def load(j, b):
                        sp.wait_ge(t_full, j + 1)
                        sp.dma_start(XG[:, b, :], fx.xs1[bass.ds(TOKENS + j * P, P), :]).then_inc(ld_x[b], 16)

                    for j in range(4):
                        load(j, j)
                    for e in range(2, E1):
                        load_w1(e)
                    for j in range(4, 6):
                        load(j, j % 4)

                    def step(j, b, ahead):
                        if follows(ahead, 6):
                            load(j + 6, (b + 2) % 4)
                        sp.wait_ge(y_used, j + 1)
                        sp.dma_start(fx.ys1[bass.ds(j * P, P), :], Y[:, b % 2, :]).then_inc(stored[b % 2], 16)

                    tile_pipeline(sp, step, NS)
                    for b in range(2):
                        sp.wait_ge(stored[b], 16 + 8 * NS)

                @block.gpsimd
                def _(pool):
                    pool.wait_ge(ld_xd, 16)
                    pool.wait_ge(fx.slots_zeroed1, 16)
                    pool.wait_ge(r.placed, 1)
                    for t in range(TILES):
                        for k in range(TOP1):
                            pool.indirect_dma_start(
                                out=fx.xs1, out_offset=bass.IndirectOffsetOnAxis(ap=r.row[:, t, k:k + 1], axis=0),
                                in_=XD[:, t, :], in_offset=None).then_inc(sent, 16)
                    for i in range(E1 // 2):
                        pool.wait_ge(ld_w1[i], 64)
                        pool.sem_inc(w1_in, 2)

                @block.scalar
                def _(act):
                    r.on_act(nc, act)
                    act.wait_ge(ld_s, 48)
                    nc.scalar.activation(b1T[:], b1T[:], ACT.Gelu).then_inc(z_gelu, 1)

                    def rows(j, b):
                        act.wait_ge(t_full, j + 5)
                        nc.scalar.activation(XGT[:, b % 2, :], BT[b % 2][:, 0:KC * P], ACT.Copy).then_inc(t_used, 1)

                    def step(j, b, ahead):
                        if follows(ahead, 2):
                            rows(j + 2, b)
                        for i in range(2):
                            act.wait_ge(ht_full, 2 * j + i + 1)
                            nc.scalar.activation(HT[:, b % 2, i * HC:(i + 1) * HC, :].rearrange("p c q -> p (c q)"),
                                                 BH[i][:], ACT.Gelu).then_inc(ht_used, 1)

                    rows(0, 0)
                    rows(1, 1)
                    tile_pipeline(act, step, NS)

                @block.vector
                def _(dve):
                    dve.wait_ge(ld_s, 48)
                    r.on_dve(nc, dve, fx.LG1[:], fx.tri[:], fx.last_first[:, 0:E1], fx.thresholds[:], fx.tile_row[:], BH[0], BH[1])
                    do = r.steps
                    dve.wait_ge(z_gelu, 1)
                    nc.vector.tensor_tensor(GB[:], b1T[:].unsqueeze(3).broadcast_to([P, E1, CH, E2]),
                                            eye[:].unsqueeze(2).broadcast_to([P, E1, CH, E2]),
                                            ALU.mult).then_inc(z_parts, 1)
                    dve.wait_ge(used_full, 1)
                    do(dve, nc.vector.tensor_reduce(
                        used[:], BU[1][:, 0:TOP1 * TILES * E1].rearrange("p (k t e) -> p k e t", k=TOP1, t=TILES), AX,
                        ALU.max))
                    do(dve, nc.vector.tensor_scalar(used[:], used[:], 0.0, None, ALU.is_gt))
                    for k in range(TOP1):
                        weight = r.wt[:, :, k].unsqueeze(2).broadcast_to([P, TILES, E1])
                        for lo, x, op in ((0, used[:, k].unsqueeze(1).broadcast_to([P, TILES, E1]), ALU.add),
                                          (E1, r.hot[:, k], ALU.subtract)):
                            out = AC[:, :, lo:lo + E1]
                            if k == 0 and op == ALU.add:
                                do(dve, nc.vector.tensor_tensor(out, x, weight, ALU.mult))
                                continue
                            do(dve, nc.vector.tensor_tensor(term[:], x, weight, ALU.mult))
                            if k == 0:
                                do(dve, nc.vector.tensor_scalar(out, term[:], -1.0, None, ALU.mult))
                            else:
                                do(dve, nc.vector.tensor_tensor(out, out, term[:], op))

                    def expert(j):
                        return dve.value_load(r.texp[0:1, bass.ds(j, 1)], min_val=0, max_val=E1 - 1)

                    def bias(j, b):
                        e = expert(j)
                        for i in range(2):
                            dve.wait_ge(u_full, 2 * j + i + 1)
                            nc.vector.tensor_tensor(H[:, i * HALF:(i + 1) * HALF].unsqueeze(1), BU[i][:].unsqueeze(1),
                                                    b1[:, bass.ds(e, 1), i * HALF:(i + 1) * HALF],
                                                    ALU.add).then_inc(h_done, 1)

                    def step(j, b, ahead):
                        if follows(ahead, 1):
                            bias(j + 1, b + 1)
                        dve.wait_ge(y_full, j + 1)
                        dve.wait_ge(stored[b % 2], 8 * (j + (2 - b % 2)))
                        nc.vector.tensor_copy(Y[:, b % 2, :], BY[b % 2][:, 0:DIM]).then_inc(y_used, 1)

                    dve.wait_ge(z_full, 1)
                    nc.vector.tensor_tensor(ZB[0:E2, :], BY[1][0:E2, 0:DIM], b2[0:E2, :], ALU.add).then_inc(z_done, 1)
                    bias(0, 0)
                    tile_pipeline(dve, step, NS)

                @block.tensor
                def _(pe):
                    pe.sem_inc(t_full, 4)
                    r.on_pe(nc, pe, fx.before, fx.ones, BH[0], BH[1])
                    nc.tensor.matmul(BU[1][:, 0:TOP1 * TILES * E1], fx.ones[:], r.hot[:].rearrange("p k t e -> p (k t e)"),
                                     start=True, stop=True).then_inc(used_full, 1)
                    pe.wait_ge(z_parts, 1)
                    for e in range(E1):
                        pe.wait_ge(ld_w2[e], 16)
                        for c in range(CH):
                            last = nc.tensor.matmul(BY[1][0:E2, 0:DIM], GB[:, e, c, :], w2[:, e, c, :],
                                                    start=e == 0 and c == 0, stop=e == E1 - 1 and c == CH - 1)
                    last.then_inc(z_full, 1)
                    pe.wait_ge(z_done, 1)
                    pe.wait_ge(r.placed, 1)

                    def expert(j):
                        return pe.value_load(r.texp[0:1, bass.ds(j, 1)], min_val=0, max_val=E1 - 1)

                    def rows(j, b):
                        pe.wait_ge(ld_x[b], 4 * (j - b) + 16)
                        for m in range(KC):
                            last = nc.tensor.transpose(BT[b % 2][:, m * P:(m + 1) * P],
                                                       XG[:, b, m * P:(m + 1) * P], fx.ident[:])
                        last.then_inc(t_full, 1)

                    def up(j, b):
                        e = expert(j)
                        pe.wait_ge(t_used, j + 1)
                        pe.wait_ge(w1_in, e + 1)
                        for i in range(2):
                            for m in range(KC):
                                last = nc.tensor.matmul(BU[i][:], XGT[:, b % 2, m * P:(m + 1) * P],
                                                        w1[:, m, bass.ds(e, 1), i * HALF:(i + 1) * HALF],
                                                        start=m == 0, stop=m == KC - 1)
                            last.then_inc(u_full, 1)

                    def step(j, b, ahead):
                        if follows(ahead, 2):
                            rows(j + 2, (b + 2) % 4)
                        for i in range(2):
                            pe.wait_ge(h_done, 2 * j + i + 1)
                            for c in range(HC):
                                lo = (i * HC + c) * P
                                last = nc.tensor.transpose(BH[i][:, c * P:(c + 1) * P], H[:, lo:lo + P], fx.ident[:])
                            last.then_inc(ht_full, 1)
                        if follows(ahead, 1):
                            up(j + 1, b + 1)
                        e = expert(j)
                        for i in range(2):
                            pe.wait_ge(ht_used, 2 * j + i + 1)
                            for c in range(i * HC, (i + 1) * HC):
                                last = nc.tensor.matmul(BY[b % 2][:, 0:DIM], HT[:, b % 2, c, :],
                                                        w2[:, bass.ds(e, 1), c, :], start=c == 0, stop=c == CH - 1)
                        last.then_inc(y_full, 1)

                    rows(0, 0)
                    rows(1, 1)
                    up(0, 0)
                    tile_pipeline(pe, step, NS)

        PAIRS, AHEAD = TILES // 2, 4
        gathered = [sem(f"gathered{i}") for i in range(AHEAD)]
        ld_xd = sem("ld_x_again")
        ac_full, ac_used = sem("ac_full"), sem("ac_used")
        rest_full = sem("rest_full")
        moments, root = sem("moments"), sem("root")
        normed, written = sem("normed"), sem("written")
        do = Steps(sem("fin_steps"))
        turned_banks = [fx.PJ[0], fx.PJ[1], fx.OB[0], fx.OB[1]]
        banks = fx.SB + fx.PJ + fx.OB
        with ExitStack() as mem:
            def sb(name, shape):
                return mem.enter_context(nc.sbuf_tensor("fin_" + name, shape, F32))

            X, GA = sb("X", [P, TILES, DIM]), sb("GA", [P, TILES, TOP1, DIM])
            ACT_T = sb("ACT_T", [P, GROUPS, GTOK])
            st, mv, rs = sb("st", [P, TILES, 6]), sb("mv", [P, TILES, 2]), sb("rs", [P, TILES])

            def pair(p):
                return slice(2 * p, 2 * p + 2)

            with nc.Block() as block:
                @block.gpsimd
                def _(pool):
                    for p in range(PAIRS):
                        if p >= AHEAD:
                            pool.wait_ge(gathered[p % AHEAD], 32 * TOP1 * (p // AHEAD))
                        for t in range(2 * p, 2 * p + 2):
                            for k in range(TOP1):
                                pool.indirect_dma_start(
                                    out=GA[:, t, k, :], out_offset=None, in_=fx.ys1,
                                    in_offset=bass.IndirectOffsetOnAxis(ap=fx.pos1[:, t, k:k + 1], axis=0),
                                ).then_inc(gathered[p % AHEAD], 16)

                @block.sync
                def _(sp):
                    sp.dma_start(X[:], fx.xs1[0:TOKENS, :].rearrange("(t p) d -> p t d", p=P)).then_inc(ld_xd, 16)
                    for p in range(PAIRS):
                        sp.wait_ge(normed, p + 1)
                        sp.dma_start(io["out"][2 * p * P:2 * (p + 1) * P, :].rearrange("(t p) d -> p t d", p=P),
                                     X[:, pair(p)]).then_inc(written, 16)
                    sp.wait_ge(written, 16 * PAIRS)

                @block.scalar
                def _(act):
                    for g in range(GROUPS):
                        act.wait_ge(ac_full, g + 1)
                        nc.scalar.activation(ACT_T[0:E2, g, :], turned_banks[g][0:E2, :], ACT.Copy).then_inc(ac_used, 1)
                    for p in range(PAIRS):
                        act.wait_ge(moments, p + 1)
                        nc.scalar.activation(rs[:, pair(p)], mv[:, pair(p), 1], ACT.Sqrt,
                                             bias=fx.epsln[:, 0:1]).then_inc(root, 1)

                @block.vector
                def _(dve):
                    def finish(p):
                        dve.wait_ge(root, p + 1)
                        do(dve, nc.vector.reciprocal(rs[:, pair(p)], rs[:, pair(p)]))
                        for t in range(2 * p, 2 * p + 2):
                            last = nc.vector.tensor_scalar(X[:, t, :], X[:, t, :], mv[:, t, 0:1], rs[:, t:t + 1],
                                                           ALU.subtract, ALU.mult)
                        last.then_inc(normed, 1)

                    dve.wait_ge(ld_xd, 16)
                    for p in range(PAIRS):
                        dve.wait_ge(rest_full, p // 2 + 1)
                        do(dve, nc.vector.tensor_tensor(X[:, pair(p)], banks[p][:].rearrange("p (t d) -> p t d", t=2),
                                                        X[:, pair(p)], ALU.add))
                        dve.wait_ge(gathered[p % AHEAD], 32 * TOP1 * (p // AHEAD + 1))
                        for k in range(TOP1):
                            for t in range(2 * p, 2 * p + 2):
                                last = nc.vector.scalar_tensor_tensor(
                                    out=X[:, t, :], in0=GA[:, t, k, :], scalar=fx.wt1[:, t, k:k + 1], in1=X[:, t, :],
                                    op0=ALU.mult, op1=ALU.add)
                            do(dve, last)
                        for t in range(2 * p, 2 * p + 2):
                            last = nc.vector.bn_stats(st[:, t, :], X[:, t, :])
                        do(dve, last)
                        for t in range(2 * p, 2 * p + 2):
                            last = nc.vector.bn_aggr(mv[:, t, :], st[:, t, :])
                        last.then_inc(moments, 1)
                        if p:
                            finish(p - 1)
                    finish(PAIRS - 1)

                @block.tensor
                def _(pe):
                    for g in range(GROUPS):
                        for t in range(TG):
                            last = nc.tensor.transpose(turned_banks[g][0:E2, t * P:(t + 1) * P],
                                                       AC[:, g * TG + t, :], fx.ident[:])
                        last.then_inc(ac_full, 1)
                    for g in range(GROUPS):
                        pe.wait_ge(ac_used, max(g + 1, min(2 * g - 1, GROUPS)))
                        for t in range(TG):
                            last = nc.tensor.matmul(banks[2 * g + t // 2][:, t % 2 * DIM:(t % 2 + 1) * DIM],
                                                    ACT_T[0:E2, g, t * P:(t + 1) * P], ZB[0:E2, :], start=True, stop=True)
                        last.then_inc(rest_full, 1)


class Fixed:
    pass


def decoder(nc, io):
    es = ExitStack()
    with es:
        fx = Fixed()

        def sb(name, shape):
            return es.enter_context(nc.sbuf_tensor(name, shape, F32))

        banks = [es.enter_context(nc.psum_tensor(f"bank{i}", [P, 512], F32)) for i in range(8)]
        fx.PJ, fx.SB, fx.OB = banks[0:2], banks[2:6], banks[6:8]
        fx.ident, fx.ones = sb("ident", [P, P]), sb("ones", [P, P])
        fx.cmask = sb("cmask", [P, SEQ])
        fx.cneg = sb("cneg", [P, SEQ])
        fx.hm16 = sb("hm16", [P, 8])
        fx.hm8 = sb("hm8", [P, 16])
        fx.neghalf, fx.epsln, fx.epsrms = sb("neghalf", [P, 1]), sb("epsln", [P, 1]), sb("epsrms", [P, 1])
        fx.NS0 = -(-((TOKENS * TOP0 + E0 * (P - 1)) // P) // 4) * 4
        fx.NS1 = -(-((TOKENS * TOP1 + E1 * (P - 1)) // P) // 4) * 4
        rows = SHARED * TOKENS + fx.NS0 * P
        fx.xs, fx.ys = (nc.dram_tensor(n, (rows, DIM), F32).ap() for n in ("xs", "ys"))
        fx.xs1, fx.ys1 = (nc.dram_tensor(n, (rows, DIM), F32).ap() for n, rows in
                          (("xs1", TOKENS + fx.NS1 * P), ("ys1", fx.NS1 * P)))
        fx.tri = sb("tri", [P, NGRP, NGRP])
        fx.last_first = sb("last_first", [P, E0])
        fx.before = sb("before", [P, P])
        fx.thresholds = sb("thresholds", [P, TILES])
        fx.tile_row = sb("tile_row", [P, fx.NS0])
        fx.zeros = sb("zeros", [P, DIM])
        fx.slots_zeroed = es.enter_context(nc.semaphore("slots_zeroed"))
        fx.slots_zeroed1 = es.enter_context(nc.semaphore("slots_zeroed1"))
        fx.LG, fx.LG1 = sb("LG", [P, TILES, E0]), sb("LG1", [P, TILES, E1])
        (fx.pos0, fx.wt0), (fx.pos1, fx.wt1) = (
            (es.enter_context(nc.sbuf_tensor(n + "pos", [P, TILES, k], U32)), sb(n + "wt", [P, TILES, k]))
            for n, k in (("r0_", TOP0), ("r1_", TOP1)))
        fx.ready = es.enter_context(nc.semaphore("constants"))
        fx.READY = 15 * 16
        fx.dve_passed, fx.pool_passed = (es.enter_context(nc.semaphore(n)) for n in ("dve_passed", "pool_passed"))
        with nc.Block() as block:
            @block.scalar
            def _(act):
                for dst, src in ((fx.ident, io["ident"]), (fx.ones, io["ones"]), (fx.cmask, io["cmask"]), (fx.cneg, io["cneg"]),
                                 (fx.hm16, io["hm16"]), (fx.hm8, io["hm8"]), (fx.neghalf, io["neghalf"]),
                                 (fx.epsln, io["epsln"]), (fx.epsrms, io["epsrms"]), (fx.tri, io["tri"]),
                                 (fx.last_first, io["last_first"]), (fx.before, io["before"]),
                                 (fx.thresholds, io["thresholds"]), (fx.tile_row, io["tile_row"]), (fx.zeros, io["zeros"])):
                    act.dma_start(dst[:], src).then_inc(fx.ready, 16)
        layer0(nc, es, io, fx)
        moe0(nc, es, io, fx)
        layer1(nc, es, io, fx)
        moe1(nc, es, io, fx)


def layouts(a):
    f = np.float32
    ar = {}
    x, c = a["x"].reshape(TOKENS, DIM), a["ctx_2048"].reshape(TOKENS, DIM)
    ar["x"], ar["xT"], ar["cT"] = x, x.T, c.T
    ar["la_wq"], ar["la_wk"], ar["la_wv"] = a["L0_attn_Wq"], a["L0_attn_Wk"], a["L0_attn_Wv"].T
    ar["la_wo"] = a["L0_attn_Wo"].T.reshape(8, 2, 16, DIM).transpose(1, 0, 2, 3).reshape(DIM, DIM)
    ar["gb"] = np.stack([np.tile(a["L0_attn_gamma"], 8), np.tile(a["L0_attn_beta"], 8)], 1)
    ar["xa_wq"], ar["xa_wk"], ar["xa_wo"] = a["L0_xattn_q_w"].T, a["L0_xattn_k_img_w"].T, a["L0_xattn_o_w"].T
    ar["xa_wv"] = a["L0_xattn_v_img_w"].T.reshape(DIM, 8, 2, 16).transpose(0, 2, 1, 3).reshape(DIM, DIM)
    vb = a["L0_xattn_v_img_b"].reshape(8, 2, 16).transpose(1, 0, 2).reshape(2, 1, P)
    ar["vb"] = np.tile(vb, (1, SEQ, 1)).reshape(P, P)
    for n, k in (("qb", "q_b"), ("kb", "k_img_b"), ("ob", "o_b"), ("nq", "norm_q_w"), ("nk", "norm_k_img_w")):
        ar[n] = np.tile(a["L0_xattn_" + k][None, :], (P, 1))
    ar["wg"] = a["L0_ffn_Wg"].T
    p, q = np.arange(P)[:, None], np.arange(SEQ)[None, :]
    ar["ident"], ar["ones"] = np.eye(P, dtype=f), np.ones((P, P), f)
    ar["cmask"] = (p % SEQ <= q).astype(f)
    ar["cneg"] = np.where(q <= p % SEQ, f(0), f(NEG)).astype(f)
    ar["hm16"] = (p // 16 == np.arange(8)).astype(f)
    ar["hm8"] = (p // 8 == np.arange(16)).astype(f)
    ar["neghalf"], ar["epsln"], ar["epsrms"] = (np.full((P, 1), v, f) for v in (-0.5, EPS_LN, EPS_RMS))
    e = np.arange(NGRP)
    ar["last_first"] = np.tile(np.arange(E0, 0, -1, dtype=f), (P, 1))
    ar["tri"] = np.tile((e[None, :] < e[:, None]).astype(f), (P, 1, 1))
    t = np.arange(P)
    ar["before"] = (t[:, None] < t[None, :]).astype(f)
    ar["thresholds"] = np.tile(np.arange(TILES, dtype=f) * P, (P, 1))
    ar["tile_row"] = np.tile(np.arange(-(-((TOKENS * TOP0 + E0 * (P - 1)) // P) // 4) * 4, dtype=f), (P, 1))
    ar["zeros"] = np.zeros((P, DIM), f)
    ar["sa_wq"], ar["sa_wv"], ar["sa_wo"] = a["L1_attn_Wq"], a["L1_attn_Wv"], a["L1_attn_Wo"]
    ar["sa_wk"] = np.repeat(a["L1_attn_Wk"].reshape(DIM, 4, 1, 16), 4, 2).reshape(DIM, DIM)
    kv = np.concatenate([a["L1_xattn_Wk"], a["L1_xattn_Wv"]])
    ar["xb_wq"], ar["xb_wkv"] = a["L1_xattn_Wq"].T, np.concatenate([kv[0::2], kv[1::2]]).T
    ar["rw1"], ar["rw2"] = a["L1_ffn_rw1"], a["L1_ffn_rw2"]
    both = [np.concatenate([a["L0_ffn_" + n], a["L0_ffn_" + m].reshape(SHARED, I0, DIM)]) for n, m in
            (("W1", "Ws1"), ("W3", "Ws3"))]
    w13 = np.concatenate(both, 1)
    ar["w13"] = w13.transpose(2, 0, 1).reshape(KC, P, EALL, 2 * I0)
    w2 = np.concatenate([a["L0_ffn_W2"], a["L0_ffn_Ws2"].reshape(DIM, SHARED, I0).transpose(1, 0, 2)])
    ar["w2"] = w2.transpose(2, 0, 1)
    ar["m1_w1"] = a["L1_ffn_w1"].reshape(E1, KC, P, I1).transpose(2, 1, 0, 3)
    ar["m1_w2"] = a["L1_ffn_w2"].reshape(E1, I1 // P, P, DIM).transpose(2, 0, 1, 3)
    ar["b1"] = np.tile(a["L1_ffn_b1"][None], (P, 1, 1))
    ar["b1T"] = a["L1_ffn_b1"].reshape(E1, I1 // P, P).transpose(2, 0, 1)
    ar["b2"] = np.concatenate([a["L1_ffn_b2"], np.zeros((E1, DIM), f)])
    ar["eye"] = np.tile(np.concatenate([np.eye(E1, dtype=f)] * 2, 1), (P, 1, 1))
    ar["centre"] = (np.eye(P) - (p // 16 == np.arange(P) // 16) / 16).astype(f)
    return {k: np.ascontiguousarray(v) for k, v in ar.items()}


def kernel(**inputs):
    import concourse.bacc as _bacc
    from concourse.bass_utils import run_bass_kernel_spmd as _run

    arrays = layouts({k: np.asarray(v) for k, v in inputs.items()})
    nc = _bacc.Bacc("TRN2", target_bir_lowering=False, num_devices=1)
    io = {}
    for name, v in arrays.items():
        io[name] = nc.dram_tensor("in_" + name, v.shape, mybir.dt.from_np(v.dtype), kind="ExternalInput").ap()
    io["out"] = nc.dram_tensor("out", (TOKENS, DIM), F32, kind="ExternalOutput").ap()
    decoder(nc, io)
    r = _run(nc, [{"in_" + k: v for k, v in arrays.items()}], core_ids=[0])
    return r.results[0]["out"].reshape(BATCH, SEQ, DIM)
```
